# Optimizing a Trainium2 kernel written in Bass

```python
import numpy as np
import jax
import jax.numpy as jnp

def _softmax(x, axis=-1):
    return jax.nn.softmax(x, axis=axis)

def _gelu(x):
    return jax.nn.gelu(x, approximate=True)

def _silu(x):
    return jax.nn.silu(x)

def _sigmoid(x):
    return jax.nn.sigmoid(x)

def _layernorm(x, axis=-1, eps=1e-05):
    m = jnp.mean(x, axis=axis, keepdims=True)
    v = jnp.var(x, axis=axis, keepdims=True)
    return (x - m) / jnp.sqrt(v + eps)

def _scatter_add(tgt, idx, src, axis=0):
    return tgt.at[idx].add(src)

def _segment_sum(src, seg, n):
    return jax.ops.segment_sum(src, seg, n)
kernel_name = 'mk_macaron_d1_jaxref_r8_41ccc1'

def setup_inputs(seed: int=0):
    np.random.seed(seed)
    _w = jnp.asarray

    def _L0_attn_setup():
        import jax, jax.numpy as jnp
        import numpy as np
        N_EMBD = 128
        N_HEAD = 16
        HEAD_DIM = N_EMBD // N_HEAD
        KV_RANK = 32
        Q_RANK = 64
        ROPE_DIM = 32
        B, T = (2, 256)
        EPS = 1e-06

        def _rope_tables(T, dim):
            inv_freq = 1.0 / 10000.0 ** (np.arange(0, dim, 2, dtype=np.float32) / dim)
            t = np.arange(T, dtype=np.float32)
            freqs = np.outer(t, inv_freq)
            emb = np.concatenate([freqs, freqs], -1)
            return (jnp.asarray(np.cos(emb)), jnp.asarray(np.sin(emb)))

        def _apply_rope(x, cos, sin):
            d2 = x.shape[-1] // 2
            x1, x2 = (x[..., :d2], x[..., d2:])
            rot = jnp.concatenate([-x2, x1], axis=-1)
            return x * cos[None, None, :, :] + rot * sin[None, None, :, :]
        key = jax.random.key(seed)
        ks = jax.random.split(key, 10)

        def w(k, fan_in, fan_out):
            return jax.random.normal(k, (fan_in, fan_out), dtype=jnp.float32) * fan_in ** (-0.5)
        return {'x': jax.random.normal(ks[0], (B, T, N_EMBD), dtype=jnp.float32), 'W_kv': w(ks[1], N_EMBD, KV_RANK), 'g_kv': jnp.ones((KV_RANK,), dtype=jnp.float32), 'W_kdec': w(ks[2], KV_RANK, N_HEAD * HEAD_DIM), 'W_vdec': w(ks[3], KV_RANK, N_HEAD * HEAD_DIM), 'W_q': w(ks[4], N_EMBD, Q_RANK), 'W_qdec': w(ks[5], Q_RANK, N_HEAD * HEAD_DIM), 'W_krope': w(ks[6], N_EMBD, N_HEAD * ROPE_DIM), 'W_qrope': w(ks[7], Q_RANK, N_HEAD * ROPE_DIM), 'W_o': w(ks[8], N_HEAD * HEAD_DIM, N_EMBD)}
    _L0_attn_in = _L0_attn_setup()

    def _L0_ffn_setup():
        import jax, jax.numpy as jnp
        import numpy as np
        DIM = 128
        DEPTH = 6
        HEADS = 16
        DIM_HEAD = 64
        WINDOW = 32
        INNER = HEADS * DIM_HEAD
        DIM_INNER = int(DIM * 4 * 2 / 3)
        QK_SCALE = 8.0

        def shift_tokens(t):
            a, s = jnp.split(t, 2, -1)
            s = jnp.pad(s, ((0, 0), (1, 0), (0, 0)))[:, :-1]
            return jnp.concatenate([a, s], -1)

        def l2norm(t):
            return t / jnp.maximum(jnp.linalg.norm(t, axis=-1, keepdims=True), 1e-12)

        def rotate_half(x):
            x1, x2 = jnp.split(x, 2, -1)
            return jnp.concatenate([-x2, x1], -1)

        def rotary_tables(n):
            half = jnp.arange(0, DIM_HEAD, 2, dtype=jnp.float32)
            inv_freq = 1.0 / 10000.0 ** (half / DIM_HEAD)
            t = jnp.arange(n, dtype=jnp.float32)
            freqs = t[:, None] * inv_freq[None, :]
            freqs = jnp.concatenate([freqs, freqs], -1)
            base_scale = (half + 0.4 * DIM_HEAD) / (1.4 * DIM_HEAD)
            power = (t - n // 2) / (WINDOW // 2)
            scale = base_scale[None, :] ** power[:, None]
            scale = jnp.concatenate([scale, scale], -1)
            return (freqs, scale)

        def local_attention(q, k, v):
            b, h, n, d = q.shape
            w = WINDOW
            nw = n // w
            bq = q.reshape(b, h, nw, w, d)
            bk = k.reshape(b, h, nw, w, d)
            bv = v.reshape(b, h, nw, w, d)

            def look(t):
                p = jnp.pad(t, ((0, 0), (0, 0), (1, 0), (0, 0), (0, 0)))
                return jnp.concatenate([p[:, :, :nw], p[:, :, 1:]], axis=3)
            bk2, bv2 = (look(bk), look(bv))
            seq = jnp.arange(n).reshape(nw, w)
            seq_p = jnp.pad(seq, ((1, 0), (0, 0)), constant_values=-1)
            jt = jnp.concatenate([seq_p[:nw], seq_p[1:]], axis=1)
            it = seq[:, :, None]
            jb = jt[:, None, :]
            mask = (it < jb) | (it > jb + w) | (jb == -1)
            sim = jnp.einsum('bhwie,bhwje->bhwij', bq, bk2) * QK_SCALE
            sim = jnp.where(mask, -jnp.finfo(sim.dtype).max, sim)
            attn = jax.nn.softmax(sim, -1)
            out = jnp.einsum('bhwij,bhwje->bhwie', attn, bv2)
            return out.reshape(b, h, n, d)

        def attn_layer(x, Wqkv, qs, ksc, Wo):
            b, n, _ = x.shape
            qkv = x @ Wqkv
            q, k, v = jnp.split(qkv, 3, -1)
            sh = lambda t: t.reshape(b, n, HEADS, DIM_HEAD).transpose(0, 2, 1, 3)
            q, k, v = (sh(q), sh(k), sh(v))
            q = l2norm(q) * qs
            k = l2norm(k) * ksc
            freqs, scale = rotary_tables(n)
            cos, sin = (jnp.cos(freqs), jnp.sin(freqs))
            q = q * cos * scale + rotate_half(q) * sin * scale
            inv = 1.0 / scale
            k = k * cos * inv + rotate_half(k) * sin * inv
            out = local_attention(q, k, v)
            out = out.transpose(0, 2, 1, 3).reshape(b, n, INNER)
            return out @ Wo

        def ffn_layer(x, g, bln, W1, b1, W2, b2):
            mu = x.mean(-1, keepdims=True)
            var = ((x - mu) ** 2).mean(-1, keepdims=True)
            xn = (x - mu) / jnp.sqrt(var + 1e-05) * g + bln
            hg = xn @ W1 + b1
            a, gate = jnp.split(hg, 2, -1)
            return a * jax.nn.gelu(gate, approximate=False) @ W2 + b2
        key = jax.random.key(seed)
        ks = jax.random.split(key, 8)
        B, N = (2, 256)
        init = lambda k, shape: jax.random.normal(k, shape, jnp.float32) * 0.02
        return {'x': jax.random.normal(ks[0], (B, N, DIM), jnp.float32), 'Wqkv': init(ks[1], (DEPTH, DIM, 3 * INNER)), 'q_scale': jnp.ones((DEPTH, DIM_HEAD), jnp.float32), 'k_scale': jnp.ones((DEPTH, DIM_HEAD), jnp.float32), 'Wo': init(ks[2], (DEPTH, INNER, DIM)), 'ln_g': jnp.ones((DEPTH, DIM), jnp.float32), 'ln_b': jnp.zeros((DEPTH, DIM), jnp.float32), 'W1': init(ks[3], (DEPTH, DIM, 2 * DIM_INNER)), 'b1': jnp.zeros((DEPTH, 2 * DIM_INNER), jnp.float32), 'W2': init(ks[4], (DEPTH, DIM_INNER, DIM)), 'b2': jnp.zeros((DEPTH, DIM), jnp.float32)}
    _L0_ffn_in = _L0_ffn_setup()
    _d = {'L0_attn_x': _L0_attn_in['x'], 'L0_attn_W_kv': _L0_attn_in['W_kv'], 'L0_attn_g_kv': _L0_attn_in['g_kv'], 'L0_attn_W_kdec': _L0_attn_in['W_kdec'], 'L0_attn_W_vdec': _L0_attn_in['W_vdec'], 'L0_attn_W_q': _L0_attn_in['W_q'], 'L0_attn_W_qdec': _L0_attn_in['W_qdec'], 'L0_attn_W_krope': _L0_attn_in['W_krope'], 'L0_attn_W_qrope': _L0_attn_in['W_qrope'], 'L0_attn_W_o': _L0_attn_in['W_o'], 'L0_ffn_Wqkv': _L0_ffn_in['Wqkv'], 'L0_ffn_q_scale': _L0_ffn_in['q_scale'], 'L0_ffn_k_scale': _L0_ffn_in['k_scale'], 'L0_ffn_Wo': _L0_ffn_in['Wo'], 'L0_ffn_ln_g': _L0_ffn_in['ln_g'], 'L0_ffn_ln_b': _L0_ffn_in['ln_b'], 'L0_ffn_W1': _L0_ffn_in['W1'], 'L0_ffn_b1': _L0_ffn_in['b1'], 'L0_ffn_W2': _L0_ffn_in['W2'], 'L0_ffn_b2': _L0_ffn_in['b2']}
    _x0 = _d['L0_attn_x']
    _d['L0_attn_x'] = jax.random.normal(jax.random.fold_in(jax.random.key(seed), 1), (1, 2048, 128), dtype=_x0.dtype)
    del _x0
    return _d

def reference(L0_attn_x, L0_attn_W_kv, L0_attn_g_kv, L0_attn_W_kdec, L0_attn_W_vdec, L0_attn_W_q, L0_attn_W_qdec, L0_attn_W_krope, L0_attn_W_qrope, L0_attn_W_o, L0_ffn_Wqkv, L0_ffn_q_scale, L0_ffn_k_scale, L0_ffn_Wo, L0_ffn_ln_g, L0_ffn_ln_b, L0_ffn_W1, L0_ffn_b1, L0_ffn_W2, L0_ffn_b2):

    def _L0_attn_ref(x, W_kv, g_kv, W_kdec, W_vdec, W_q, W_qdec, W_krope, W_qrope, W_o):
        import jax, jax.numpy as jnp
        import numpy as np
        N_EMBD = 128
        N_HEAD = 16
        HEAD_DIM = N_EMBD // N_HEAD
        KV_RANK = 32
        Q_RANK = 64
        ROPE_DIM = 32
        B, T = (2, 256)
        EPS = 1e-06

        def _rope_tables(T, dim):
            inv_freq = 1.0 / 10000.0 ** (np.arange(0, dim, 2, dtype=np.float32) / dim)
            t = np.arange(T, dtype=np.float32)
            freqs = np.outer(t, inv_freq)
            emb = np.concatenate([freqs, freqs], -1)
            return (jnp.asarray(np.cos(emb)), jnp.asarray(np.sin(emb)))

        def _apply_rope(x, cos, sin):
            d2 = x.shape[-1] // 2
            x1, x2 = (x[..., :d2], x[..., d2:])
            rot = jnp.concatenate([-x2, x1], axis=-1)
            return x * cos[None, None, :, :] + rot * sin[None, None, :, :]
        Bx, Tx, C = x.shape
        kv_c = x @ W_kv
        kv_c = kv_c * jax.lax.rsqrt(jnp.mean(kv_c * kv_c, axis=-1, keepdims=True) + EPS) * g_kv
        q_c = x @ W_q

        def heads(y, d):
            return y.reshape(Bx, Tx, N_HEAD, d).transpose(0, 2, 1, 3)
        k_content = heads(kv_c @ W_kdec, HEAD_DIM)
        v = heads(kv_c @ W_vdec, HEAD_DIM)
        q_content = heads(q_c @ W_qdec, HEAD_DIM)
        k_rope = heads(x @ W_krope, ROPE_DIM)
        q_rope = heads(q_c @ W_qrope, ROPE_DIM)
        cos, sin = _rope_tables(Tx, ROPE_DIM)
        q_rope = _apply_rope(q_rope, cos, sin)
        k_rope = _apply_rope(k_rope, cos, sin)
        q = jnp.concatenate([q_content, q_rope], axis=-1)
        k = jnp.concatenate([k_content, k_rope], axis=-1)
        scale = 1.0 / jnp.sqrt(jnp.float32(q.shape[-1]))
        scores = jnp.einsum('bhqd,bhkd->bhqk', q, k) * scale
        causal = jnp.tril(jnp.ones((Tx, Tx), dtype=bool))
        scores = jnp.where(causal[None, None], scores, jnp.float32(-jnp.inf))
        attn = jax.nn.softmax(scores, axis=-1)
        out = jnp.einsum('bhqk,bhkd->bhqd', attn, v)
        out = out.transpose(0, 2, 1, 3).reshape(Bx, Tx, N_HEAD * HEAD_DIM)
        return out @ W_o

    def _L0_ffn_ref(x, Wqkv, q_scale, k_scale, Wo, ln_g, ln_b, W1, b1, W2, b2):
        import jax, jax.numpy as jnp
        import numpy as np
        DIM = 128
        DEPTH = 6
        HEADS = 16
        DIM_HEAD = 64
        WINDOW = 32
        INNER = HEADS * DIM_HEAD
        DIM_INNER = int(DIM * 4 * 2 / 3)
        QK_SCALE = 8.0

        def shift_tokens(t):
            a, s = jnp.split(t, 2, -1)
            s = jnp.pad(s, ((0, 0), (1, 0), (0, 0)))[:, :-1]
            return jnp.concatenate([a, s], -1)

        def l2norm(t):
            return t / jnp.maximum(jnp.linalg.norm(t, axis=-1, keepdims=True), 1e-12)

        def rotate_half(x):
            x1, x2 = jnp.split(x, 2, -1)
            return jnp.concatenate([-x2, x1], -1)

        def rotary_tables(n):
            half = jnp.arange(0, DIM_HEAD, 2, dtype=jnp.float32)
            inv_freq = 1.0 / 10000.0 ** (half / DIM_HEAD)
            t = jnp.arange(n, dtype=jnp.float32)
            freqs = t[:, None] * inv_freq[None, :]
            freqs = jnp.concatenate([freqs, freqs], -1)
            base_scale = (half + 0.4 * DIM_HEAD) / (1.4 * DIM_HEAD)
            power = (t - n // 2) / (WINDOW // 2)
            scale = base_scale[None, :] ** power[:, None]
            scale = jnp.concatenate([scale, scale], -1)
            return (freqs, scale)

        def local_attention(q, k, v):
            b, h, n, d = q.shape
            w = WINDOW
            nw = n // w
            bq = q.reshape(b, h, nw, w, d)
            bk = k.reshape(b, h, nw, w, d)
            bv = v.reshape(b, h, nw, w, d)

            def look(t):
                p = jnp.pad(t, ((0, 0), (0, 0), (1, 0), (0, 0), (0, 0)))
                return jnp.concatenate([p[:, :, :nw], p[:, :, 1:]], axis=3)
            bk2, bv2 = (look(bk), look(bv))
            seq = jnp.arange(n).reshape(nw, w)
            seq_p = jnp.pad(seq, ((1, 0), (0, 0)), constant_values=-1)
            jt = jnp.concatenate([seq_p[:nw], seq_p[1:]], axis=1)
            it = seq[:, :, None]
            jb = jt[:, None, :]
            mask = (it < jb) | (it > jb + w) | (jb == -1)
            sim = jnp.einsum('bhwie,bhwje->bhwij', bq, bk2) * QK_SCALE
            sim = jnp.where(mask, -jnp.finfo(sim.dtype).max, sim)
            attn = jax.nn.softmax(sim, -1)
            out = jnp.einsum('bhwij,bhwje->bhwie', attn, bv2)
            return out.reshape(b, h, n, d)

        def attn_layer(x, Wqkv, qs, ksc, Wo):
            b, n, _ = x.shape
            qkv = x @ Wqkv
            q, k, v = jnp.split(qkv, 3, -1)
            sh = lambda t: t.reshape(b, n, HEADS, DIM_HEAD).transpose(0, 2, 1, 3)
            q, k, v = (sh(q), sh(k), sh(v))
            q = l2norm(q) * qs
            k = l2norm(k) * ksc
            freqs, scale = rotary_tables(n)
            cos, sin = (jnp.cos(freqs), jnp.sin(freqs))
            q = q * cos * scale + rotate_half(q) * sin * scale
            inv = 1.0 / scale
            k = k * cos * inv + rotate_half(k) * sin * inv
            out = local_attention(q, k, v)
            out = out.transpose(0, 2, 1, 3).reshape(b, n, INNER)
            return out @ Wo

        def ffn_layer(x, g, bln, W1, b1, W2, b2):
            mu = x.mean(-1, keepdims=True)
            var = ((x - mu) ** 2).mean(-1, keepdims=True)
            xn = (x - mu) / jnp.sqrt(var + 1e-05) * g + bln
            hg = xn @ W1 + b1
            a, gate = jnp.split(hg, 2, -1)
            return a * jax.nn.gelu(gate, approximate=False) @ W2 + b2
        for i in range(DEPTH):
            x = attn_layer(shift_tokens(x), Wqkv[i], q_scale[i], k_scale[i], Wo[i]) + x
            x = ffn_layer(shift_tokens(x), ln_g[i], ln_b[i], W1[i], b1[i], W2[i], b2[i]) + x
        return x
    x = L0_attn_x
    x = x + 0.5 * _L0_ffn_ref(_layernorm(x, axis=-1), L0_ffn_Wqkv, L0_ffn_q_scale, L0_ffn_k_scale, L0_ffn_Wo, L0_ffn_ln_g, L0_ffn_ln_b, L0_ffn_W1, L0_ffn_b1, L0_ffn_W2, L0_ffn_b2)
    x = x + _L0_attn_ref(_layernorm(x, axis=-1), L0_attn_W_kv, L0_attn_g_kv, L0_attn_W_kdec, L0_attn_W_vdec, L0_attn_W_q, L0_attn_W_qdec, L0_attn_W_krope, L0_attn_W_qrope, L0_attn_W_o)
    x = x + 0.5 * _L0_ffn_ref(_layernorm(x, axis=-1), L0_ffn_Wqkv, L0_ffn_q_scale, L0_ffn_k_scale, L0_ffn_Wo, L0_ffn_ln_g, L0_ffn_ln_b, L0_ffn_W1, L0_ffn_b1, L0_ffn_W2, L0_ffn_b2)
    return x

_drawn_inputs = setup_inputs


def setup_inputs(seed=0):
    import zlib

    import numpy as np

    out = dict(_drawn_inputs(seed))
    spreads = {'L0_attn_g_kv': (1.0, 0.6),
     'L0_ffn_q_scale': (1.0, 0.6),
     'L0_ffn_k_scale': (1.0, 0.6),
     'L0_ffn_ln_g': (1.0, 0.6),
     'L0_ffn_ln_b': (0.0, 0.8),
     'L0_ffn_b1': (0.0, 0.8),
     'L0_ffn_b2': (0.0, 0.1)}
    factors = {'L0_ffn_W1': 3.142, 'L0_ffn_W2': 3.066}
    for name, (base, spread) in spreads.items():
        noise = np.random.default_rng([zlib.crc32(name.encode()), seed]).standard_normal(out[name].shape)
        drawn = base * np.exp(spread * noise) if base else spread * noise
        out[name] = jnp.asarray(drawn.astype(out[name].dtype))
    for name, factor in factors.items():
        out[name] = (out[name] * factor).astype(out[name].dtype)
    return out
```

```python
from contextlib import ExitStack

import numpy as np

import concourse.bass as bass
from concourse import mybir


class NormBuffers:

    def __init__(self, M, V, src, xc, sq, ve, rs, dg):
        self.M, self.V, self.src, self.xc, self.sq, self.ve, self.rs, self.dg = M, V, src, xc, sq, ve, rs, dg


ALU = mybir.AluOpType
ACT = mybir.ActivationFunctionType
F32 = mybir.dt.float32
BF16 = mybir.dt.bfloat16
X = mybir.AxisListType.X

P = 128
T = 2048
TILES = T // P
DEPTH = 6
HEADS = 16
DH = 64
WIN = 32
HU = 4
UT = HEADS // HU
UNITS = TILES * UT
KEYS = P + WIN
INNER = 341
CH = [(0, 128), (128, 128), (256, 85)]
G = 4
GT = T // G
NEG = -1.0e30
LN_EPS = 1e-5

QR, KR, CD, RD = 64, 32, 8, 32
QD = CD + RD
RMS_EPS = 1e-6
PAIRS = HEADS // 2

LAG_V, LAG_T, LAG_S, LAG_P, LAG_O, LAG_OT, LAG_Y = 1, 2, 3, 4, 5, 6, 7

WA, WF = 16 * 8, 16 * 12

SEMAPHORES = (
    "const_in consts_ready x_in wa_in wf_in"
    " xs_ready tab_ready qk_ready squared summed clamped inv_ready normed t1_ready t2_ready rotated"
    " tr_ready tr_read s_ready k_carried maxed centred exped pt_ready pt_copied pt_read v_ready vs_ready v_read"
    " o_ready v_carried recip_ready o_normed ot_ready ot_read y_ready x_b_ready"
    " sh_lo sh_hi mean_ready ln_centred ln_squared var_ready vare_ready pow_ready ln_diag rstd_ready ln_scaled ln_ready"
    " up_ready gelu_ready prod_ready down_ready x_a_ready"
    " xt_ready x_res_ready mixed out_t_ready out_ready stored"
    " wl_in wl_zero wl_slots lat_ready lat_sq lat_q lat_ms lat_mse lat_pow lat_diag lat_rs lat_spread lat_kv v_mm v_copied"
    " ab_ready ra_ready rb_ready rope_ready"
    " sc_ready row_max row_neg row_exp ptl_ready ptl_read pv_part ol_rec ol_normed"
    " lo_tr lo_copied lo_mm lo_added"
)


def tables():
    f = np.float32
    half = np.arange(0, DH, 2, dtype=f)
    inv = (f(1.0) / (f(10000.0) ** (half / f(DH)))).astype(f)
    t = np.arange(T, dtype=f)
    fr = (t[:, None] * inv[None, :]).astype(f)
    fr = np.concatenate([fr, fr], -1)
    base = ((half + f(0.4 * DH)) / f(1.4 * DH)).astype(f)
    base = np.concatenate([base, base])
    local = (np.arange(T) % P - P // 2) / (WIN // 2)
    grow = base[None, :].astype(np.float64) ** local[:, None]
    cos, sin = np.cos(fr), np.sin(fr)
    sgn = np.concatenate([-np.ones(DH // 2), np.ones(DH // 2)])
    wc = np.stack([cos * grow, cos / grow], 1)
    ws = np.stack([sin * sgn * grow, sin * sgn / grow], 1)
    wc = wc.reshape(TILES, P, 2, DH).transpose(1, 0, 2, 3)
    ws = ws.reshape(TILES, P, 2, DH).transpose(1, 0, 2, 3)
    carry = (base.astype(np.float64) ** (P / (WIN // 2)))
    carry = np.concatenate([carry, carry])[:, None]
    i, j = np.arange(P)[:, None], np.arange(P)[None, :]
    main = np.where((j <= i) & (j >= i - WIN), 0.0, NEG)
    js = np.arange(WIN)[None, :]
    side = np.where((i < WIN) & (js >= i), 0.0, NEG)
    wmask = np.stack([np.concatenate([main, np.full((P, WIN), NEG)], 1),
                      np.concatenate([main, side], 1)], 1)
    causal = np.where(j <= i, 0.0, NEG)
    inv2 = (1.0 / 10000.0 ** (np.arange(0, RD, 2, dtype=f) / RD)).astype(f)
    fr2 = np.outer(t, inv2).astype(f)
    e2 = np.concatenate([fr2, fr2], -1)
    ac, as_ = np.zeros((P, T)), np.zeros((P, T))
    sg2 = np.concatenate([-np.ones(RD // 2), np.ones(RD // 2)])
    for h in range(2):
        ac[64 * h:64 * h + RD] = np.cos(e2).T
        ac[64 * h + RD:64 * h + QD] = 1.0
        as_[64 * h:64 * h + RD] = (np.sin(e2) * sg2).T
    out = dict(ident=np.eye(P), wc=wc, ws=ws, carry=carry, wmask=wmask, causal=causal, ac=ac, as_=as_)
    return {k: np.ascontiguousarray(v, dtype=f) for k, v in out.items()}



def macaron_kernel(nc, i, c, out):
    with ExitStack() as ctx:
        def sb(name, shape, dt=F32):
            return ctx.enter_context(nc.sbuf_tensor(name, shape, dt))

        z = {n: ctx.enter_context(nc.semaphore(n)) for n in SEMAPHORES.split()}
        x_res = sb("x_res", [P, T])
        x_a = sb("x_a", [P, 1 + T + P])
        x_b = sb("x_b", [P, 1 + T])
        ident = sb("ident", [P, P])
        ident_h = sb("ident_h", [P, P], BF16)
        wmask = sb("wmask", [P, 2, KEYS], BF16)
        causal = sb("causal", [P, P], BF16)
        carry_f = sb("carry_f", [P, 1])
        mean_w = sb("mean_w", [P, P])
        ones_w = sb("ones_w", [P, P])
        neg_half = sb("neg_half", [P, 2 * HU])
        zeros = sb("zeros", [P, P])
        x_dram = i["L0_attn_x"].rearrange("a (n p) d -> p (a n) d", p=P)
        out_dram = out.rearrange("a (n p) d -> p (a n) d", p=P)

        load_input(nc, z, c, x_dram, x_res, x_a, x_b, ident, ident_h, wmask, causal, carry_f, mean_w, ones_w, neg_half, zeros)
        outer_norm(nc, z, "na", 0, x_res, x_a, ident, mean_w, ones_w, neg_half)
        window_stack(nc, z, i, c, 0, G, x_a, x_b, ident, ident_h, wmask, carry_f, mean_w, ones_w, neg_half, zeros)
        mix(nc, z, 0, x_res, x_a)
        n1 = G + DEPTH * G
        outer_norm(nc, z, "nb", n1, x_res, x_a, ident, mean_w, ones_w, neg_half)
        latent_attention(nc, z, i, c, x_res, x_a, ident, ident_h, causal, ones_w, neg_half, zeros)
        outer_norm(nc, z, "nc", n1 + G, x_res, x_a, ident, mean_w, ones_w, neg_half)
        window_stack(nc, z, i, c, 1, n1 + 2 * G, x_a, x_b, ident, ident_h, wmask, carry_f, mean_w, ones_w, neg_half, zeros)
        mix(nc, z, 1, x_res, x_a)
        store_output(nc, z, out_dram, x_res, ident)


def load_input(nc, z, c, x_dram, x_res, x_a, x_b, ident, ident_h, wmask, causal, carry_f, mean_w, ones_w, neg_half, zeros):
    with ExitStack() as st:
        x_tok = st.enter_context(nc.sbuf_tensor("x_tok", [P, TILES, P], F32))
        wmask_f = st.enter_context(nc.sbuf_tensor("wmask_f", [P, 2, KEYS], F32))
        causal_f = st.enter_context(nc.sbuf_tensor("causal_f", [P, P], F32))
        tp = st.enter_context(nc.psum_tensor("turned_in", [P, 2, GT], F32))
        block = st.enter_context(nc.Block())

        @block.sync
        def _(sp):
            sp.dma_start(ident[:, :], c["ident"]).then_inc(z["const_in"], 16)
            for n in range(G):
                sp.dma_start(x_tok[:, 4 * n:4 * n + 4, :], x_dram[:, 4 * n:4 * n + 4, :]).then_inc(z["x_in"], 16)
            sp.dma_start(wmask_f[:, :, :], c["wmask"]).then_inc(z["const_in"], 16)
            sp.dma_start(causal_f[:, :], c["causal"]).then_inc(z["const_in"], 16)
            sp.dma_start(carry_f[:, :], c["carry"]).then_inc(z["const_in"], 16)

        @block.gpsimd
        def _(pool):
            nc.gpsimd.memset(mean_w[:, :], 1.0 / P).then_inc(z["consts_ready"], 1)
            nc.gpsimd.memset(neg_half[:, :], -0.5).then_inc(z["x_a_ready"], 1)
            nc.gpsimd.memset(ones_w[:, :], 1.0).then_inc(z["consts_ready"], 1)
            nc.gpsimd.memset(zeros[:, :], 0.0).then_inc(z["consts_ready"], 1)
            nc.gpsimd.memset(x_a[:, :], 0.0).then_inc(z["consts_ready"], 1)
            nc.gpsimd.memset(x_b[:, 0:1], 0.0).then_inc(z["consts_ready"], 1)

        @block.tensor
        def _(pe):
            pe.wait_ge(z["const_in"], 64)
            for n in range(G):
                pe.wait_ge(z["x_in"], 16 * G)
                if n >= 2:
                    pe.wait_ge(z["x_res_ready"], n - 1)
                for m in range(4):
                    mm = pe.transpose(tp[:, n % 2, m * P:(m + 1) * P], x_tok[:, 4 * n + m, :], ident[:, :])
                mm.then_inc(z["xt_ready"], 1)

        @block.vector
        def _(dve):
            dve.wait_ge(z["const_in"], 64)
            nc.vector.tensor_copy(ident_h[:, :], ident[:, :]).then_inc(z["consts_ready"], 1)
            nc.vector.tensor_copy(wmask[:, :, :], wmask_f[:, :, :]).then_inc(z["consts_ready"], 1)
            nc.vector.tensor_copy(causal[:, :], causal_f[:, :]).then_inc(z["consts_ready"], 1)
            for n in range(G):
                dve.wait_ge(z["xt_ready"], n + 1)
                nc.vector.tensor_copy(x_res[:, n * GT:(n + 1) * GT], tp[:, n % 2, :]).then_inc(z["x_res_ready"], 1)


def norm_mean(nc, z, pe, b, mean_w, q, n):
    if n >= 1:
        pe.wait_ge(z["ln_centred"], q)
    pe.matmul(b.M, mean_w[:, :], b.src(n), start=True, stop=True).then_inc(z["mean_ready"], 1)


def norm_var(nc, z, pe, b, mean_w, q, n):
    pe.wait_ge(z["ln_squared"], q + 1)
    if n >= 1:
        pe.wait_ge(z["ln_scaled"], q)
    for m in range(GT // P):
        mm = pe.matmul(b.V[:, m:m + 1], b.sq(n)[:, m * P:(m + 1) * P], mean_w[:, 0:1], start=True, stop=True)
    mm.then_inc(z["var_ready"], 1)


def norm_spread(nc, z, pe, b, ones_w, q, n):
    pe.wait_ge(z["ln_diag"], q + 1)
    pe.matmul(b.V, ones_w[:, :], b.dg[:, :, :], start=True, stop=True).then_inc(z["rstd_ready"], 1)


def norm_centre(nc, z, dve, b, q, n):
    dve.wait_ge(z["mean_ready"], q + 1)
    if n >= 2:
        dve.wait_ge(z["ln_squared"], q - 1)
        dve.wait_ge(z["ln_scaled"], q - 1)
    nc.vector.tensor_tensor(b.xc(n), b.src(n), b.M, ALU.subtract).then_inc(z["ln_centred"], 1)


def norm_square(nc, z, act, b, q, n):
    act.wait_ge(z["ln_centred"], q + 1)
    if n >= 2:
        act.wait_ge(z["var_ready"], q - 1)
    nc.scalar.activation(b.sq(n), b.xc(n), ACT.Square).then_inc(z["ln_squared"], 1)


def norm_eps(nc, z, dve, b, q, n):
    dve.wait_ge(z["var_ready"], q + 1)
    if n >= 1:
        dve.wait_ge(z["pow_ready"], q)
    nc.vector.tensor_scalar(b.ve, b.V[:, 0:GT // P], LN_EPS, None, ALU.add).then_inc(z["vare_ready"], 1)


def norm_rstd(nc, z, pool, b, neg_half, q, n):
    if n >= 1:
        pool.wait_ge(z["ln_diag"], q)
    pool.wait_ge(z["vare_ready"], q + 1)
    nc.gpsimd.tensor_tensor(b.rs, b.ve, neg_half[:, 0:GT // P], ALU.pow).then_inc(z["pow_ready"], 1)


def norm_diagonal(nc, z, dve, b, ident, q, n):
    dve.wait_ge(z["pow_ready"], q + 1)
    if n >= 1:
        dve.wait_ge(z["rstd_ready"], q)
    nc.vector.tensor_tensor(b.dg[:, :, :], ident[:, :].unsqueeze(1).to_broadcast([P, GT // P, P]),
                            b.rs.unsqueeze(2).to_broadcast([P, GT // P, P]), ALU.mult).then_inc(z["ln_diag"], 1)


def outer_norm(nc, z, tag, q0, x_res, x_a, ident, mean_w, ones_w, neg_half):
    with ExitStack() as st:
        b4 = {n: st.enter_context(nc.sbuf_tensor(f"{tag}_{n}", [P, 2, GT], F32)) for n in ("xc", "sq")}
        small = st.enter_context(nc.sbuf_tensor(f"{tag}_small", [P, 2, GT // P], F32))
        dg = st.enter_context(nc.sbuf_tensor(f"{tag}_dg", [P, GT // P, P], F32))
        ps = st.enter_context(nc.psum_tensor(f"{tag}_ps", [P, 2, GT], F32))
        b = NormBuffers(
            M=ps[:, 0, :], V=ps[:, 1, :], src=lambda n: x_res[:, n * GT:(n + 1) * GT],
            xc=lambda n: b4["xc"][:, n % 2, :], sq=lambda n: b4["sq"][:, n % 2, :],
            ve=small[:, 0, :], rs=small[:, 1, :], dg=dg)
        block = st.enter_context(nc.Block())

        @block.tensor
        def _(pe):
            pe.wait_ge(z["consts_ready"], 8)
            for n in range(G + 1):
                if n < G:
                    norm_mean(nc, z, pe, b, mean_w, q0 + n, n)
                if n >= 1:
                    norm_var(nc, z, pe, b, mean_w, q0 + n - 1, n - 1)
                    norm_spread(nc, z, pe, b, ones_w, q0 + n - 1, n - 1)

        @block.scalar
        def _(act):
            for n in range(G):
                norm_square(nc, z, act, b, q0 + n, n)

        @block.gpsimd
        def _(pool):
            for n in range(G):
                norm_rstd(nc, z, pool, b, neg_half, q0 + n, n)

        @block.vector
        def _(dve):
            for n in range(G + 1):
                if n < G:
                    norm_centre(nc, z, dve, b, q0 + n, n)
                if n >= 1:
                    m = n - 1
                    norm_eps(nc, z, dve, b, q0 + m, m)
                    norm_diagonal(nc, z, dve, b, ident, q0 + m, m)
                    dve.wait_ge(z["rstd_ready"], q0 + m + 1)
                    nc.vector.tensor_tensor(x_a[:, 1 + m * GT:1 + (m + 1) * GT], b.xc(m), b.V, ALU.mult).then_inc(z["ln_scaled"], 1)


def window_stack(nc, z, i, c, k, q0, x_a, x_b, ident, ident_h, wmask, carry_f, mean_w, ones_w, neg_half, zeros):
    with ExitStack() as st:
        def sb(name, shape, dt=F32):
            return st.enter_context(nc.sbuf_tensor(f"{name}_{k}", shape, dt))

        w_qkv = sb("w_qkv", [P, 3, HEADS * DH])
        w_o = sb("w_o", [P, HEADS * DH // P, P])
        w_1 = sb("w_1", [P, 2 * INNER])
        w_2 = sb("w_2", [P, len(CH), P])
        vec = sb("vec", [P, 9])
        qk_sc = sb("qk_sc", [P, 2, DH])
        qk_sw = sb("qk_sw", [P, 2, DH])
        wcos = sb("wcos", [P, TILES + 1, 2, DH])
        wsin = sb("wsin", [P, TILES + 1, 2, DH])
        tab_c = sb("tab_c", [P, 2, 2, DH])
        tab_s = sb("tab_s", [P, 2, 2, DH])
        xs = sb("xs", [P, 2, P])
        QK = 2 * HU * DH
        sq = sb("sq", [P, 2, QK])
        ss = sb("ss", [P, 2, 2 * HU])
        ssm = sb("ssm", [P, 2, 2 * HU])
        inv = sb("inv", [P, 2, 2 * HU])
        qn = sb("qn", [P, 2, QK])
        t1 = sb("t1", [P, 2, QK])
        t2 = sb("t2", [P, 2, QK])
        rot = sb("rot", [P, 4, QK])
        qkt = sb("qkt", [P, 2, 4, P])
        k_car = sb("k_car", [P, UT, 2, WIN])
        mx = sb("mx", [P, 2, HU])
        cen = sb("cen", [P, 2, HU, KEYS])
        prob = sb("prob", [P, 2, HU, KEYS])
        pt = sb("pt", [P, 2, HU, P])
        pts = sb("pts", [P, 2, HU, WIN])
        AW = DH + 1
        vt = sb("vt", [P, 8, HU, AW])
        v_car = sb("v_car", [P, UT, HU, AW])
        rec = sb("rec", [P, 2, HU])
        on = sb("on", [P, 2, HU * DH])
        ots = sb("ots", [P, 8, 2, P])
        f2 = {n: sb("f" + n, [P, 2, GT]) for n in ("src", "xc", "sq", "xn", "gl")}
        fsmall = sb("fsmall", [P, 2, GT // P])
        fdg = sb("fdg", [P, GT // P, P])
        fsc = sb("fsc", [P, GT])
        hm = sb("hm", [P, 4, GT])
        ps = st.enter_context(nc.psum_tensor(f"ps_{k}", [P, 8, 512], F32))
        fb = NormBuffers(
            M=ps[:, 0, :], V=ps[:, 1, :], src=lambda n: f2["src"][:, n % 2, :],
            xc=lambda n: f2["xc"][:, n % 2, :], sq=lambda n: f2["sq"][:, n % 2, :],
            ve=fsmall[:, 0, :], rs=fsmall[:, 1, :], dg=fdg)
        L0 = k * DEPTH
        side = ps[:, 6, 256:256 + HU * WIN]
        heads_qk = lambda t: t.rearrange("p (q h d) -> p q h d", q=2, h=HU)
        scores = ps[:, 2:4, 0:2 * KEYS].rearrange("p b (r j) -> p b r j", r=2)
        by_bank = lambda t: t.rearrange("p (r b) j -> p b r j", b=2)

        def slots(eng, slot):
            for s in range(8):
                slot(s, 0, "first")
            with eng.Fori(1, TILES // 2) as pair:
                for s in range(8):
                    slot(s, pair, "steady")
            for s in range(8):
                slot(s, TILES // 2, "last")

        def clock(L, s, pair, part):
            def live(lag):
                return {"first": s >= lag, "steady": True, "last": s < lag}[part]

            def had(lag, back):
                return part != "first" or s - lag - back >= 0

            def done(lag, back=0):
                return (L + L0) * UNITS + pair * 8 + (s - lag - back + 1)
            return live, had, done

        def tile_no(L, s, pair):
            return (L + L0) * (TILES + 1) + pair * 2 + (s // UT + 1)

        def tiles_out(L, s, pair):
            return (L + L0) * TILES + pair * 2 + (s - LAG_Y - (UT - 1)) // UT + 1

        block = st.enter_context(nc.Block())

        @block.sync
        def _(sp):
            sp.dma_start(wcos[:, 0:TILES], c["wc"]).then_inc(z["const_in"], 16)
            sp.dma_start(wsin[:, 0:TILES], c["ws"]).then_inc(z["const_in"], 16)
            hf = DH // 2
            def attention_weights(L):
                sp.dma_start(w_qkv[:, :, :], i["L0_ffn_Wqkv"][bass.ds(L, 1)].rearrange("a p (t n) -> p (a t) n", t=3)).then_inc(z["wa_in"], 16)
                sp.dma_start(w_o[:, :, :], i["L0_ffn_Wo"][bass.ds(L, 1)].rearrange("a (c p) n -> p (a c) n", p=P)).then_inc(z["wa_in"], 16)

            def attention_scales(L):
                for q, name in enumerate(("L0_ffn_q_scale", "L0_ffn_k_scale")):
                    row = i[name][bass.ds(L, 1)]
                    sp.dma_start(qk_sc[:, q, :], row.to_broadcast([P, DH])).then_inc(z["wa_in"], 16)
                    sp.dma_start(qk_sw[:, q, 0:hf], row[:, hf:DH].to_broadcast([P, hf])).then_inc(z["wa_in"], 16)
                    sp.dma_start(qk_sw[:, q, hf:DH], row[:, 0:hf].to_broadcast([P, hf])).then_inc(z["wa_in"], 16)

            def feed_forward_weights(L):
                sp.dma_start(w_1[:, :], i["L0_ffn_W1"][bass.ds(L, 1)].rearrange("a p n -> p (a n)")).then_inc(z["wf_in"], 16)
                whole = 2 * P
                sp.dma_start(w_2[:, 0:2, :], i["L0_ffn_W2"][bass.ds(L, 1), 0:whole].rearrange("a (c p) n -> p (a c) n", p=P)).then_inc(z["wf_in"], 16)
                sp.dma_start(w_2[0:INNER - whole, 2, :], i["L0_ffn_W2"][bass.ds(L, 1), whole:INNER].rearrange("a p n -> p (a n)")).then_inc(z["wf_in"], 16)
                with nc.allow_non_contiguous_dma(reason="vectors onto partitions"):
                    for q, name in enumerate(("L0_ffn_ln_g", "L0_ffn_ln_b", "L0_ffn_b2")):
                        sp.dma_start(vec[:, q:q + 1], i[name][bass.ds(L, 1)].rearrange("a p -> p a")).then_inc(z["wf_in"], 16)
                    for q in range(2):
                        for m, (lo, w) in enumerate(CH):
                            b1 = i["L0_ffn_b1"][bass.ds(L, 1), q * INNER + lo:q * INNER + lo + w]
                            sp.dma_start(vec[0:w, 3 + 3 * q + m:4 + 3 * q + m], b1.rearrange("a p -> p a")).then_inc(z["wf_in"], 16)

            attention_weights(0)
            attention_scales(0)
            feed_forward_weights(0)
            with sp.Fori(1, DEPTH) as L:
                sp.wait_ge(z["y_ready"], (L + L0) * TILES)
                attention_weights(L)
                sp.wait_ge(z["tab_ready"], (L + L0) * (2 * TILES + 2))
                attention_scales(L)
                sp.wait_ge(z["x_a_ready"], (L + L0) * G + 1)
                feed_forward_weights(L)

        @block.gpsimd
        def _(pool):
            nc.gpsimd.memset(vt[:, :, :, :], 1.0).then_inc(z["consts_ready"], 1)
            nc.gpsimd.memset(k_car[:, :, :, :], 0.0).then_inc(z["consts_ready"], 1)
            nc.gpsimd.memset(v_car[:, :, :, :], 0.0).then_inc(z["consts_ready"], 1)
            nc.gpsimd.memset(wcos[:, TILES], 0.0).then_inc(z["consts_ready"], 1)
            nc.gpsimd.memset(wsin[:, TILES], 0.0).then_inc(z["consts_ready"], 1)
            pool.wait_ge(z["consts_ready"], 8 + 5 * (k + 1))
            pool.wait_ge(z["const_in"], 64 + 32 * (k + 1))
            with pool.Fori(0, DEPTH) as L:
                def scaled_tables(tile, par):
                    flat = lambda t: t[:, bass.ds(tile, 1)].rearrange("p a q d -> p (a q) d")
                    nc.gpsimd.tensor_tensor(tab_c[:, par], flat(wcos), qk_sc[:, :, :], ALU.mult).then_inc(z["tab_ready"], 1)
                    nc.gpsimd.tensor_tensor(tab_s[:, par], flat(wsin), qk_sw[:, :, :], ALU.mult).then_inc(z["tab_ready"], 1)

                pool.wait_ge(z["wa_in"], (L + L0 + 1) * WA)
                scaled_tables(0, 0)

                def slot(s, pair, part):
                    live, had, done = clock(L, s, pair, part)
                    r2, r4, par = s % 2, s % 4, s // UT
                    if live(0):
                        if s % UT == 1:
                            if had(0, 2):
                                pool.wait_ge(z["t2_ready"], 2 * done(0, 2))
                            scaled_tables(pair * 2 + (par + 1), (par + 1) % 2)
                        pool.wait_ge(z["clamped"], done(0))
                        if had(0, 2):
                            pool.wait_ge(z["normed"], done(0, 2))
                        nc.gpsimd.tensor_tensor(inv[:, r2], ssm[:, r2], neg_half[:, 0:2 * HU], ALU.pow).then_inc(z["inv_ready"], 1)
                        pool.wait_ge(z["normed"], done(0))
                        pool.wait_ge(z["tab_ready"], 2 * tile_no(L, s, pair))
                        if had(0, 2):
                            pool.wait_ge(z["rotated"], done(0, 2))
                        cb = tab_c[:, par].unsqueeze(2).to_broadcast([P, 2, HU, DH])
                        nc.gpsimd.tensor_tensor(heads_qk(t1[:, r2]), heads_qk(qn[:, r2]), cb, ALU.mult).then_inc(z["t1_ready"], 1)
                        pool.wait_ge(z["t1_ready"], done(0))
                        pool.wait_ge(z["t2_ready"], 2 * done(0))
                        if had(0, 4):
                            pool.wait_ge(z["tr_ready"], done(0, 4))
                        nc.gpsimd.tensor_tensor(rot[:, r4], t1[:, r2], t2[:, r2], ALU.add).then_inc(z["rotated"], 1)
                    if live(LAG_S):
                        m = (s - LAG_S) % 8
                        pool.wait_ge(z["s_ready"], done(LAG_S))
                        nc.gpsimd.tensor_tensor(k_car[:, m % UT], qkt[:, m % 2, 2:4, P - WIN:P], carry_f[:, 0:1].unsqueeze(2).to_broadcast([P, 2, WIN]), ALU.mult).then_inc(z["k_carried"], 1)
                slots(pool, slot)

                for n in range(G):
                    norm_rstd(nc, z, pool, fb, neg_half, q0 + L * G + n, n)

        @block.tensor
        def _(pe):
            pe.wait_ge(z["consts_ready"], 8 + 5 * (k + 1))
            with pe.Fori(0, DEPTH) as L:
                pe.wait_ge(z["wa_in"], (L + L0 + 1) * WA)
                pe.wait_ge(z["x_a_ready"], (L + L0) * G + 1)

                def slot(s, pair, part):
                    live, had, done = clock(L, s, pair, part)
                    if live(0):
                        u = s % UT
                        pe.wait_ge(z["xs_ready"], 2 * tile_no(L, s, pair))
                        if had(0, 2):
                            pe.wait_ge(z["squared"], done(0, 2))
                            pe.wait_ge(z["normed"], done(0, 2))
                        pe.matmul(ps[:, s % 2, :], xs[:, s // UT, :], w_qkv[:, 0:2, u * 256:(u + 1) * 256],
                                  start=True, stop=True).then_inc(z["qk_ready"], 1)
                    if live(LAG_T):
                        bank = 4 + (3 * s) % 2
                        pe.wait_ge(z["rotated"], done(LAG_T))
                        if had(LAG_P, 1):
                            pe.wait_ge(z["pt_read"], done(LAG_P, 1))
                        elif had(LAG_T, 2):
                            pe.wait_ge(z["tr_read"], done(LAG_T, 2))
                        for m in range(4):
                            mm = pe.transpose(ps[:, bank, m * P:(m + 1) * P],
                                              rot[:, (s - LAG_T) % 4, m * P:(m + 1) * P], ident[:, :])
                        mm.then_inc(z["tr_ready"], 1)
                    if live(LAG_S):
                        n = (s - LAG_S) % 8
                        pe.wait_ge(z["tr_read"], done(LAG_S))
                        if had(LAG_S, 1):
                            pe.wait_ge(z["centred"], done(LAG_S, 1))
                        if had(LAG_S, UT):
                            pe.wait_ge(z["k_carried"], done(LAG_S, UT))
                        first = part == "first" and n < UT
                        for b in range(2):
                            m = wmask[:, 0 if first else 1].unsqueeze(1).to_broadcast([P, 2, KEYS])
                            pe.matmul(scores[:, b], ident_h[:, :], m, start=True, stop=False, skip_group_check=True)
                            h0 = 64 * b
                            for r in range(2):
                                q = qkt[h0:h0 + 64, n % 2, r, :]
                                pe.matmul(scores[:, b, r, 0:P], q, qkt[h0:h0 + 64, n % 2, 2 + r, :],
                                          start=False, stop=False, skip_group_check=True)
                                mm = pe.matmul(scores[0:WIN, b, r, P:KEYS], q[:, 0:WIN], k_car[h0:h0 + 64, n % UT, r, :],
                                               start=False, stop=True, skip_group_check=True)
                        mm.then_inc(z["s_ready"], 1)
                    if live(LAG_P):
                        n = (s - LAG_P) % 8
                        bank = 4 + (3 * s + 1) % 2
                        pe.wait_ge(z["exped"], done(LAG_P))
                        if had(LAG_OT, 1):
                            pe.wait_ge(z["ot_read"], done(LAG_OT, 1))
                        else:
                            pe.wait_ge(z["tr_read"], done(LAG_T, 1))
                        if part != "last" or s <= LAG_V:
                            pe.wait_ge(z["v_read"], done(LAG_V, 1))
                        if had(LAG_P, 1):
                            pe.wait_ge(z["pt_read"], done(LAG_P, 1))
                        for h in range(HU):
                            mm = pe.transpose(ps[:, bank, h * P:(h + 1) * P], prob[:, n % 2, h, 0:P], ident[:, :])
                        mm.then_inc(z["pt_ready"], 1)
                        for h in range(HU):
                            mm = pe.transpose(side[0:WIN, h * WIN:(h + 1) * WIN], prob[0:WIN, n % 2, h, P:KEYS], ident[0:WIN, 0:WIN])
                        if not live(LAG_V):
                            mm.then_inc(z["vs_ready"], 1)
                    if live(LAG_V):
                        n = (s - LAG_V) % 8
                        if had(LAG_V, 1) and not live(LAG_P):
                            pe.wait_ge(z["v_read"], done(LAG_V, 1))
                        mm = pe.matmul(ps[:, 6, 0:256], xs[:, n // UT, :], w_qkv[:, 2, (n % UT) * 256:(n % UT + 1) * 256],
                                       start=True, stop=True)
                        mm.then_inc(z["v_ready"], 1)
                    yt = live(LAG_Y) and (s - LAG_Y) % UT == UT - 1
                    if yt:
                        pe.wait_ge(z["ot_read"], done(LAG_Y))
                        if part != "last" or s <= LAG_O:
                            pe.wait_ge(z["o_normed"], done(LAG_O, 1))
                        else:
                            pe.wait_ge(z["o_normed"], (L + L0 + 1) * UNITS)
                        base = (s - LAG_Y - (UT - 1)) % 8
                        for m in range(2 * UT):
                            mm = pe.matmul(ps[:, 7, 384:512], w_o[:, m, :], ots[:, base + m // 2, m % 2, :],
                                           start=(m == 0), stop=(m == 2 * UT - 1))
                        mm.then_inc(z["y_ready"], 1)
                    if live(LAG_O):
                        n = (s - LAG_O) % 8
                        pe.wait_ge(z["pt_read"], done(LAG_O))
                        pe.wait_ge(z["v_read"], done(LAG_O))
                        if had(LAG_O, UT - 1):
                            pe.wait_ge(z["v_carried"], done(LAG_O, UT - 1))
                        if had(LAG_O, 1):
                            pe.wait_ge(z["o_normed"], done(LAG_O, 1))
                        if had(LAG_Y, 1) and (s - LAG_Y - 1) % UT == UT - 1:
                            pe.wait_ge(z["x_b_ready"], tiles_out(L, s - 1, pair))
                        for h in range(HU):
                            o = ps[:, 7, h * AW:(h + 1) * AW]
                            pe.matmul(o, pt[:, n % 2, h, :], vt[:, n, h, :], start=True, stop=False, skip_group_check=True)
                            mm = pe.matmul(o[0:WIN], pts[P - WIN:P, n % 2, h, :], v_car[P - WIN:P, n % UT, h, :],
                                           start=False, stop=True, skip_group_check=True, tile_position=(P - WIN, 0))
                        mm.then_inc(z["o_ready"], 1)
                    if live(LAG_OT):
                        n = (s - LAG_OT) % 8
                        bank = 4 + (3 * s + 2) % 2
                        pe.wait_ge(z["o_normed"], done(LAG_OT))
                        if live(LAG_T):
                            pe.wait_ge(z["tr_read"], done(LAG_T))
                        elif s <= LAG_P:
                            pe.wait_ge(z["pt_read"], done(LAG_P, 1))
                        else:
                            pe.wait_ge(z["ot_read"], done(LAG_OT, 2))
                        for m in range(2):
                            mm = pe.transpose(ps[:, bank, m * P:(m + 1) * P], on[:, n % 2, m * P:(m + 1) * P], ident[:, :])
                        mm.then_inc(z["ot_ready"], 1)
                slots(pe, slot)

                g = L + L0
                pe.wait_ge(z["wf_in"], (g + 1) * WF)
                pe.wait_ge(z["x_b_ready"], (g + 1) * TILES)
                q1 = q0 + L * G

                def mean(n):
                    pe.wait_ge(z["sh_lo"], g * G + (n + 1))
                    pe.wait_ge(z["sh_hi"], g * G + (n + 1))
                    norm_mean(nc, z, pe, fb, mean_w, q1 + n, n)

                def up(n, m):
                    j = 3 * n + m
                    lo, w = CH[m]
                    pe.wait_ge(z["ln_ready"], g * G + (n + 1))
                    if j >= 2:
                        pe.wait_ge(z["prod_ready"], g * 3 * G + (j - 1))
                    pe.matmul(ps[0:w, 2 + j % 2, :], w_1[:, lo:lo + w], f2["xn"][:, n % 2, :], start=True, stop=True)
                    pe.matmul(ps[0:w, 4 + j % 2, :], w_1[:, INNER + lo:INNER + lo + w], f2["xn"][:, n % 2, :],
                              start=True, stop=True).then_inc(z["up_ready"], 1)

                def down(n, m):
                    j = 3 * n + m
                    w = CH[m][1]
                    pe.wait_ge(z["prod_ready"], g * 3 * G + (j + 1))
                    if m == 0 and n >= 2:
                        pe.wait_ge(z["x_a_ready"], g * G + n)
                    pe.matmul(ps[:, 6 + n % 2, :], w_2[0:w, m, :], hm[0:w, j % 4, :],
                              start=(m == 0), stop=(m == len(CH) - 1)).then_inc(z["down_ready"], 1)

                mean(0)
                norm_var(nc, z, pe, fb, mean_w, q1, 0)
                norm_spread(nc, z, pe, fb, ones_w, q1, 0)
                for n in range(G):
                    up(n, 0)
                    up(n, 1)
                    if n + 1 < G:
                        mean(n + 1)
                    down(n, 0)
                    up(n, 2)
                    if n + 1 < G:
                        norm_var(nc, z, pe, fb, mean_w, q1 + n + 1, n + 1)
                    down(n, 1)
                    if n + 1 < G:
                        norm_spread(nc, z, pe, fb, ones_w, q1 + n + 1, n + 1)
                    down(n, 2)

        @block.scalar
        def _(act):
            with act.Fori(0, DEPTH) as L:
                def slot(s, pair, part):
                    live, had, done = clock(L, s, pair, part)
                    if live(0):
                        act.wait_ge(z["qk_ready"], done(0))
                        if had(0, 2):
                            act.wait_ge(z["summed"], done(0, 2))
                        nc.scalar.activation(sq[:, s % 2], ps[:, s % 2, :], ACT.Square).then_inc(z["squared"], 1)
                    if live(LAG_T):
                        n = (s - LAG_T) % 8
                        act.wait_ge(z["tr_ready"], done(LAG_T))
                        if had(LAG_T, 2):
                            act.wait_ge(z["s_ready"], done(LAG_T, 2))
                            act.wait_ge(z["k_carried"], done(LAG_T, 2))
                        nc.scalar.copy(qkt[:, n % 2].rearrange("p a t -> p (a t)"), ps[:, 4 + (3 * s) % 2, :]).then_inc(z["tr_read"], 1)
                    if live(LAG_P):
                        n = (s - LAG_P) % 8
                        act.wait_ge(z["pt_ready"], done(LAG_P))
                        if had(LAG_P, 2):
                            act.wait_ge(z["o_ready"], done(LAG_P, 2))
                        nc.scalar.copy(pt[:, n % 2].rearrange("p a t -> p (a t)"), ps[:, 4 + (3 * s + 1) % 2, :]).then_inc(z["pt_copied"], 1)
                        if live(LAG_V):
                            act.wait_ge(z["v_ready"], done(LAG_V))
                        else:
                            act.wait_ge(z["vs_ready"], (L + L0) * (LAG_P - LAG_V) + (s - LAG_V + 1))
                        nc.scalar.copy(pts[P - WIN:P, n % 2].rearrange("p a t -> p (a t)"), side[0:WIN]).then_inc(z["pt_read"], 1)
                    if live(LAG_V):
                        n = (s - LAG_V) % 8
                        act.wait_ge(z["v_ready"], done(LAG_V))
                        if had(LAG_V, 7):
                            act.wait_ge(z["v_carried"], done(LAG_V, 7))
                        nc.scalar.copy(vt[:, n, :, 0:DH], ps[:, 6, 0:256].rearrange("p (h d) -> p h d", h=HU)).then_inc(z["v_read"], 1)
                    if live(LAG_OT):
                        n = (s - LAG_OT) % 8
                        act.wait_ge(z["ot_ready"], done(LAG_OT))
                        nc.scalar.copy(ots[:, n].rearrange("p a t -> p (a t)"), ps[:, 4 + (3 * s + 2) % 2, 0:256]).then_inc(z["ot_read"], 1)
                    if live(LAG_S):
                        n = (s - LAG_S) % 8
                        act.wait_ge(z["centred"], done(LAG_S))
                        if had(LAG_S, 2):
                            act.wait_ge(z["pt_ready"], done(LAG_S, 2))
                            act.wait_ge(z["pt_read"], done(LAG_S, 2))
                        nc.scalar.activation(prob[:, n % 2], cen[:, n % 2], ACT.Exp, scale=float(DH) ** 0.5).then_inc(z["exped"], 1)
                    if live(LAG_O):
                        n = (s - LAG_O) % 8
                        act.wait_ge(z["o_ready"], done(LAG_O))
                        act.wait_ge(z["v_read"], done(LAG_O))
                        nc.scalar.copy(v_car[P - WIN:P, n % UT], vt[P - WIN:P, n]).then_inc(z["v_carried"], 1)
                slots(act, slot)

                g = L + L0
                q1 = q0 + L * G

                def shift(n):
                    act.wait_ge(z["x_b_ready"], g * TILES + 4 * (n + 1))
                    if n >= 2:
                        act.wait_ge(z["ln_centred"], q1 + (n - 1))
                    nc.scalar.copy(f2["src"][0:64, n % 2, :], x_b[0:64, 1 + n * GT:1 + (n + 1) * GT]).then_inc(z["sh_lo"], 1)

                def gelu(n, m):
                    j = 3 * n + m
                    w = CH[m][1]
                    act.wait_ge(z["up_ready"], g * 3 * G + (j + 1))
                    if j >= 2:
                        act.wait_ge(z["prod_ready"], g * 3 * G + (j - 1))
                    nc.scalar.activation(f2["gl"][0:w, j % 2, :], ps[0:w, 4 + j % 2, :], ACT.Gelu,
                                         bias=vec[0:w, 6 + m:7 + m]).then_inc(z["gelu_ready"], 1)

                act.wait_ge(z["wf_in"], (g + 1) * WF)
                shift(0)
                shift(1)
                norm_square(nc, z, act, fb, q1, 0)
                for n in range(G):
                    gelu(n, 0)
                    if n + 1 < G:
                        norm_square(nc, z, act, fb, q1 + n + 1, n + 1)
                    gelu(n, 1)
                    gelu(n, 2)
                    if n + 2 < G:
                        shift(n + 2)

        @block.vector
        def _(dve):
            with dve.Fori(0, DEPTH) as L:
                def slot(s, pair, part):
                    live, had, done = clock(L, s, pair, part)
                    if live(0):
                        dve.wait_ge(z["squared"], done(0))
                        if had(0, 2):
                            dve.wait_ge(z["clamped"], done(0, 2))
                        nc.vector.tensor_reduce(ss[:, s % 2], sq[:, s % 2].rearrange("p (h d) -> p h d", d=DH), X, ALU.add).then_inc(z["summed"], 1)
                    if live(LAG_S):
                        n = (s - LAG_S) % 8
                        dve.wait_ge(z["s_ready"], done(LAG_S))
                        if had(LAG_S, 2):
                            dve.wait_ge(z["centred"], done(LAG_S, 2))
                        m = mx[:, n % 2].rearrange("p (r b) -> p b r", b=2)
                        nc.vector.tensor_reduce(m, scores, X, ALU.max).then_inc(z["maxed"], 1)
                    if live(0):
                        dve.wait_ge(z["summed"], done(0))
                        if had(0, 2):
                            dve.wait_ge(z["inv_ready"], done(0, 2))
                        nc.vector.tensor_scalar(ssm[:, s % 2], ss[:, s % 2], 1e-24, None, ALU.max).then_inc(z["clamped"], 1)
                    if live(LAG_S):
                        dve.wait_ge(z["maxed"], done(LAG_S))
                        if had(LAG_S, 2):
                            dve.wait_ge(z["exped"], done(LAG_S, 2))
                        nc.vector.tensor_tensor(by_bank(cen[:, n % 2]), scores, m.unsqueeze(3).to_broadcast([P, 2, 2, KEYS]),
                                                ALU.subtract).then_inc(z["centred"], 1)
                    if live(0):
                        dve.wait_ge(z["inv_ready"], done(0))
                        if had(0, 2):
                            dve.wait_ge(z["t1_ready"], done(0, 2))
                            dve.wait_ge(z["t2_ready"], 2 * done(0, 2))
                        ib = inv[:, s % 2].unsqueeze(2).to_broadcast([P, 2 * HU, DH])
                        nc.vector.tensor_tensor(qn[:, s % 2].rearrange("p (h d) -> p h d", d=DH),
                                                ps[:, s % 2].rearrange("p (h d) -> p h d", d=DH), ib, ALU.mult).then_inc(z["normed"], 1)
                    if live(0) and s % UT == 1:
                        if had(0, 2):
                            dve.wait_ge(z["v_ready"], done(0, 2))
                        shifted(pair * 2 + (s // UT + 1), (s // UT + 1) % 2)
                    yt = live(LAG_Y) and (s - LAG_Y) % UT == UT - 1
                    if live(LAG_O):
                        n = (s - LAG_O) % 8
                        dve.wait_ge(z["o_ready"], done(LAG_O))
                        if had(LAG_O, 2):
                            dve.wait_ge(z["o_normed"], done(LAG_O, 2))
                        o = ps[:, 7, 0:HU * AW].rearrange("p (h d) -> p h d", d=AW)
                        nc.vector.reciprocal(rec[:, n % 2], o[:, :, DH]).then_inc(z["recip_ready"], 1)
                        dve.wait_ge(z["recip_ready"], done(LAG_O))
                        if had(LAG_O, 2):
                            dve.wait_ge(z["ot_ready"], done(LAG_O, 2))
                        nc.vector.tensor_tensor(on[:, n % 2].rearrange("p (h d) -> p h d", d=DH), o[:, :, 0:DH],
                                                rec[:, n % 2].unsqueeze(2).to_broadcast([P, HU, DH]), ALU.mult).then_inc(z["o_normed"], 1)
                    if yt:
                        dve.wait_ge(z["y_ready"], tiles_out(L, s, pair))
                        tile = pair * 2 + (s - LAG_Y - (UT - 1)) // UT
                        cols = bass.ds(tile * P + 1, P)
                        nc.vector.tensor_tensor(x_b[:, cols], ps[:, 7, 384:512], x_a[:, cols], ALU.add).then_inc(z["x_b_ready"], 1)
                    if live(0):
                        par, hf = s // UT, DH // 2
                        dve.wait_ge(z["normed"], done(0))
                        dve.wait_ge(z["tab_ready"], 2 * tile_no(L, s, pair))
                        if had(0, 2):
                            dve.wait_ge(z["rotated"], done(0, 2))
                        a, b = heads_qk(t2[:, s % 2]), heads_qk(qn[:, s % 2])
                        for lo, hi in ((0, hf), (hf, 0)):
                            sn = tab_s[:, par, :, lo:lo + hf].unsqueeze(2).to_broadcast([P, 2, HU, hf])
                            nc.vector.tensor_tensor(a[:, :, :, lo:lo + hf], b[:, :, :, hi:hi + hf], sn, ALU.mult).then_inc(z["t2_ready"], 1)
                def shifted(tile, par):
                    nc.vector.tensor_copy(xs[0:64, par, :], x_a[0:64, bass.ds(tile * P + 1, P)]).then_inc(z["xs_ready"], 1)
                    nc.vector.tensor_copy(xs[64:P, par, :], x_a[64:P, bass.ds(tile * P, P)]).then_inc(z["xs_ready"], 1)
                dve.wait_ge(z["x_a_ready"], (L + L0) * G + 1)
                dve.wait_ge(z["ln_scaled"], q0 + L * G)
                shifted(0, 0)
                slots(dve, slot)

                g = L + L0
                q1 = q0 + L * G

                def affine(n):
                    dve.wait_ge(z["rstd_ready"], q1 + (n + 1))
                    if n >= 1:
                        dve.wait_ge(z["ln_ready"], g * G + n)
                    nc.vector.scalar_tensor_tensor(fsc[:, :], fb.xc(n), vec[:, 0:1], fb.V, ALU.mult, ALU.mult).then_inc(z["ln_scaled"], 1)
                    dve.wait_ge(z["ln_scaled"], q1 + (n + 1))
                    if n >= 2:
                        dve.wait_ge(z["up_ready"], g * 3 * G + 3 * (n - 1))
                    nc.vector.tensor_scalar(f2["xn"][:, n % 2, :], fsc[:, :], vec[:, 1:2], None, ALU.add).then_inc(z["ln_ready"], 1)

                def prod(n, m):
                    j = 3 * n + m
                    w = CH[m][1]
                    dve.wait_ge(z["gelu_ready"], g * 3 * G + (j + 1))
                    if j >= 4:
                        dve.wait_ge(z["down_ready"], g * 3 * G + (j - 3))
                    nc.vector.scalar_tensor_tensor(hm[0:w, j % 4, :], ps[0:w, 2 + j % 2, :], vec[0:w, 3 + m:4 + m],
                                                   f2["gl"][0:w, j % 2, :], ALU.add, ALU.mult).then_inc(z["prod_ready"], 1)

                def shift(n):
                    dve.wait_ge(z["x_b_ready"], g * TILES + 4 * (n + 1))
                    if n >= 2:
                        dve.wait_ge(z["ln_centred"], q1 + (n - 1))
                    nc.vector.tensor_copy(f2["src"][64:P, n % 2, :], x_b[64:P, n * GT:(n + 1) * GT]).then_inc(z["sh_hi"], 1)

                dve.wait_ge(z["wf_in"], (g + 1) * WF)
                shift(0)
                shift(1)
                norm_centre(nc, z, dve, fb, q1, 0)
                norm_eps(nc, z, dve, fb, q1, 0)
                norm_diagonal(nc, z, dve, fb, ident, q1, 0)
                affine(0)
                for n in range(G):
                    prod(n, 0)
                    if n + 1 < G:
                        norm_centre(nc, z, dve, fb, q1 + n + 1, n + 1)
                    prod(n, 1)
                    if n + 1 < G:
                        norm_eps(nc, z, dve, fb, q1 + n + 1, n + 1)
                    prod(n, 2)
                    if n + 1 < G:
                        norm_diagonal(nc, z, dve, fb, ident, q1 + n + 1, n + 1)
                        affine(n + 1)
                    if n + 2 < G:
                        shift(n + 2)
                    dve.wait_ge(z["down_ready"], g * 3 * G + 3 * (n + 1))
                    cols = slice(1 + n * GT, 1 + (n + 1) * GT)
                    nc.vector.scalar_tensor_tensor(x_a[:, cols], ps[:, 6 + n % 2, :], vec[:, 2:3], x_b[:, cols],
                                                   ALU.add, ALU.add).then_inc(z["x_a_ready"], 1)


def copy_on_pool(nc, dst, src, zeros):
    return nc.gpsimd.tensor_tensor(dst, src, zeros, ALU.add)


def mix(nc, z, k, x_res, x_a):
    with nc.Block() as block:
        @block.vector
        def _(dve):
            nc.vector.scalar_tensor_tensor(x_res[:, :], x_a[:, 1:1 + T], 0.5, x_res[:, :], ALU.mult, ALU.add).then_inc(z["mixed"], 1)


def store_output(nc, z, out_dram, x_res, ident):
    with ExitStack() as st:
        o_tok = st.enter_context(nc.sbuf_tensor("o_tok", [P, TILES, P], F32))
        tp = st.enter_context(nc.psum_tensor("turned_out", [P, 2, GT], F32))
        block = st.enter_context(nc.Block())

        @block.tensor
        def _(pe):
            for n in range(G):
                if n >= 2:
                    pe.wait_ge(z["out_ready"], n - 1)
                for m in range(4):
                    t = 4 * n + m
                    mm = pe.transpose(tp[:, n % 2, m * P:(m + 1) * P], x_res[:, t * P:(t + 1) * P], ident[:, :])
                mm.then_inc(z["out_t_ready"], 1)

        @block.vector
        def _(dve):
            for n in range(G):
                dve.wait_ge(z["out_t_ready"], n + 1)
                nc.vector.tensor_copy(o_tok[:, 4 * n:4 * n + 4, :].rearrange("p a d -> p (a d)"), tp[:, n % 2, :]).then_inc(z["out_ready"], 1)

        @block.sync
        def _(sp):
            for n in range(G):
                sp.wait_ge(z["out_ready"], n + 1)
                sp.dma_start(out_dram[:, 4 * n:4 * n + 4, :], o_tok[:, 4 * n:4 * n + 4, :]).then_inc(z["stored"], 16)
            sp.wait_ge(z["stored"], 16 * G)


def latent_attention(nc, z, i, c, x_res, x_a, ident, ident_h, causal, ones_w, neg_half, zeros):
    VW = CD + 1
    with ExitStack() as st:
        def sb(name, shape, dt=F32):
            return st.enter_context(nc.sbuf_tensor(name, shape, dt))

        wl_kv = sb("wl_kv", [P, KR])
        wl_q = sb("wl_q", [P, QR])
        g_kv = sb("g_kv", [KR, 1])
        wl_v = sb("wl_v", [KR, P])
        wl_o = sb("wl_o", [P, P])
        wa = {"q": sb("wa_q", [QR, HEADS, 64]), "qr": sb("wa_qr", [QR, HEADS, 64]),
              "k": sb("wa_k", [P, HEADS, 64]), "kr": sb("wa_kr", [P, HEADS, 64]), "kc": sb("wa_kc", [KR, HEADS, 64])}
        ws = {n: sb("ws_" + n, [t.shape[0], 2, 64]) for n, t in wa.items()}
        mean_kv = sb("mean_kv", [KR, KR])
        kvc = sb("kvc", [KR, T])
        qc = sb("qc", [QR, T])
        lsq = sb("lsq", [KR, GT])
        lms = sb("lms", [P, GT // P])
        lrs = sb("lrs", [P, GT // P])
        lrb = sb("lrb", [KR, GT])
        ldg = sb("ldg", [P, GT // P, P])
        ac = sb("ac", [P, T])
        as_ = sb("as_", [P, T])
        qT = sb("qT", [P, T])
        kT = sb("kT", [P, T])
        ra = sb("ra", [P, 2, GT])
        rb = sb("rb", [P, 2, GT])
        vall = sb("vall", [P, TILES, HEADS, VW])
        prow = sb("prow", [P, 2, T])
        ptl = sb("ptl", [P, 2, GT])
        rmx = sb("rmx", [P, 2])
        rng = sb("rng", [P, 2])
        lrec = sb("lrec", [P, 2])
        oall = sb("oall", [P, TILES, P])
        lot = sb("lot", [P, 2, GT])
        ps = st.enter_context(nc.psum_tensor("ps_l", [P, 8, 512], F32))
        scale = 1.0 / float(np.sqrt(np.float32(QD)))

        block = st.enter_context(nc.Block())
        rows = [(h, r) for h in range(2) for r in range(TILES)]
        items = [(w, n) for w in ("q", "k") for n in range(G)]
        quads = [(x, m) for x, (h, r) in enumerate(rows) for m in range(r // 4 + 1)]
        NQ = len(quads)
        row_end = [sum(r // 4 + 1 for h, r in rows[:x + 1]) for x in range(len(rows))]

        @block.sync
        def _(sp):
            sp.dma_start(wl_kv[:, :], i["L0_attn_W_kv"]).then_inc(z["wl_in"], 16)
            sp.dma_start(wl_q[:, :], i["L0_attn_W_q"]).then_inc(z["wl_in"], 16)
            with nc.allow_non_contiguous_dma(reason="a vector onto partitions"):
                sp.dma_start(g_kv[:, :], i["L0_attn_g_kv"].rearrange("(p a) -> p a", a=1)).then_inc(z["wl_in"], 16)
            sp.dma_start(wl_v[:, :], i["L0_attn_W_vdec"]).then_inc(z["wl_in"], 16)
            sp.dma_start(wl_o[:, :], i["L0_attn_W_o"]).then_inc(z["wl_in"], 16)
            sp.dma_start(ac[:, :], c["ac"]).then_inc(z["wl_in"], 16)
            sp.dma_start(as_[:, :], c["as_"]).then_inc(z["wl_in"], 16)
            sp.wait_ge(z["wl_zero"], 7)
            hf = RD // 2
            for n, name in (("q", "L0_attn_W_qrope"), ("k", "L0_attn_W_krope")):
                src = i[name].rearrange("p (h d) -> p h d", h=HEADS)
                sp.dma_start(wa[n][:, :, 0:RD], src).then_inc(z["wl_in"], 16)
                sp.dma_start(wa[n + "r"][:, :, 0:hf], src[:, :, hf:RD]).then_inc(z["wl_in"], 16)
                sp.dma_start(wa[n + "r"][:, :, hf:RD], src[:, :, 0:hf]).then_inc(z["wl_in"], 16)
            for n, name in (("q", "L0_attn_W_qdec"), ("kc", "L0_attn_W_kdec")):
                src = i[name].rearrange("p (h d) -> p h d", h=HEADS)
                sp.dma_start(wa[n][:, :, RD:QD], src).then_inc(z["wl_in"], 16)

        WL = 16 * (7 + 8)

        @block.gpsimd
        def _(pool):
            for n, t in enumerate(wa.values()):
                nc.gpsimd.memset(t[:, :, :], 0.0).then_inc(z["wl_zero"], 1)
                pool.wait_ge(z["wl_zero"], n + 1)
            nc.gpsimd.memset(mean_kv[:, :], 1.0 / KR).then_inc(z["wl_zero"], 1)
            pool.wait_ge(z["wl_zero"], 6)
            nc.gpsimd.memset(vall[:, :, :, :], 1.0).then_inc(z["wl_zero"], 1)
            for n in range(G):
                pool.wait_ge(z["wl_zero"], 7)
                pool.wait_ge(z["lat_mse"], n + 1)
                if n >= 1:
                    pool.wait_ge(z["lat_diag"], n)
                nc.gpsimd.tensor_tensor(lrs[:, :], lms[:, :], neg_half[:, 0:GT // P], ALU.pow).then_inc(z["lat_pow"], 1)
            pool.wait_ge(z["wl_in"], WL)
            pool.wait_ge(z["lat_pow"], G)
            with pool.Fori(0, PAIRS) as pair:
                pool.wait_ge(z["ol_normed"], pair * len(rows) + 1)
                for m, n in enumerate(wa):
                    copy_on_pool(nc, ws[n][:, :, :], wa[n][:, bass.ds(pair * 2, 2), :],
                                 zeros[0:wa[n].shape[0], 0:P].rearrange("p (h d) -> p h d", h=2)).then_inc(z["wl_slots"], 1)
                    pool.wait_ge(z["wl_slots"], pair * len(wa) + (m + 1))
                for j, (w, n) in enumerate(items):
                    pool.wait_ge(z["ra_ready"], pair * len(items) + (j + 1))
                    pool.wait_ge(z["rb_ready"], pair * len(items) + (j + 1))
                    dst = qT if w == "q" else kT
                    nc.gpsimd.tensor_tensor(dst[:, n * GT:(n + 1) * GT], ra[:, j % 2, :], rb[:, j % 2, :], ALU.add).then_inc(z["rope_ready"], 1)

        @block.tensor
        def _(pe):
            pe.wait_ge(z["wl_in"], WL)
            pe.wait_ge(z["wl_zero"], 7)
            for n in range(G):
                cols = slice(1 + n * GT, 1 + (n + 1) * GT)
                if n >= 1:
                    pe.wait_ge(z["lat_kv"], n)
                    pe.wait_ge(z["lat_q"], n)
                pe.matmul(ps[0:KR, 0, :], wl_kv[:, :], x_a[:, cols], start=True, stop=True)
                pe.matmul(ps[0:QR, 1, :], wl_q[:, :], x_a[:, cols], start=True, stop=True).then_inc(z["lat_ready"], 1)
                pe.wait_ge(z["lat_sq"], n + 1)
                if n >= 1:
                    pe.wait_ge(z["lat_mse"], n)
                    pe.wait_ge(z["lat_kv"], n)
                for m in range(GT // P):
                    mm = pe.matmul(ps[:, 2, m:m + 1], lsq[:, m * P:(m + 1) * P], mean_kv[:, 0:1], start=True, stop=True)
                mm.then_inc(z["lat_ms"], 1)
                pe.wait_ge(z["lat_diag"], n + 1)
                pe.matmul(ps[0:KR, 2, :], ones_w[:, 0:KR], ldg[:, :, :], start=True, stop=True).then_inc(z["lat_rs"], 1)
            for n in range(G):
                pe.wait_ge(z["lat_kv"], n + 1)
                if n >= 2:
                    pe.wait_ge(z["v_copied"], n - 1)
                for m in range(4):
                    t = 4 * n + m
                    mm = pe.matmul(ps[:, 4 + n % 2, m * P:(m + 1) * P], kvc[:, t * P:(t + 1) * P], wl_v[:, :], start=True, stop=True)
                mm.then_inc(z["v_mm"], 1)
            pe.wait_ge(z["v_copied"], G)
            with pe.Fori(0, PAIRS) as pair:
                pe.wait_ge(z["wl_slots"], (pair + 1) * len(wa))
                pe.wait_ge(z["ol_normed"], pair * len(rows) + 1)
                for j, (w, n) in enumerate(items):
                    if j >= 2:
                        pe.wait_ge(z["ra_ready"], pair * len(items) + (j - 1))
                        pe.wait_ge(z["rb_ready"], pair * len(items) + (j - 1))
                    cols = slice(1 + n * GT, 1 + (n + 1) * GT)
                    a, b = ps[:, j % 2, :], ps[:, 2 + j % 2, :]
                    flat = lambda t: t[:, :, :].rearrange("p h d -> p (h d)")
                    if w == "q":
                        pe.matmul(a, flat(ws["q"]), qc[:, n * GT:(n + 1) * GT], start=True, stop=True)
                        mm = pe.matmul(b, flat(ws["qr"]), qc[:, n * GT:(n + 1) * GT], start=True, stop=True)
                    else:
                        pe.matmul(a, flat(ws["k"]), x_a[:, cols], start=True, stop=False)
                        pe.matmul(a, flat(ws["kc"]), kvc[:, n * GT:(n + 1) * GT], start=False, stop=True)
                        mm = pe.matmul(b, flat(ws["kr"]), x_a[:, cols], start=True, stop=True)
                    mm.then_inc(z["ab_ready"], 1)

                def row_scores(x):
                    h, r = rows[x]
                    pe.wait_ge(z["rope_ready"], (pair + 1) * len(items))
                    if x >= 1:
                        pe.wait_ge(z["row_exp"], pair * len(rows) + x)
                    else:
                        pe.wait_ge(z["rb_ready"], (pair + 1) * len(items))
                    keys = (r + 1) * P
                    for m in range(r // 4 + 1):
                        last = m == r // 4
                        w = min(GT, keys - m * GT)
                        mm = pe.matmul(ps[:, m, 0:w], qT[64 * h:64 * h + QD, r * P:(r + 1) * P],
                                       kT[64 * h:64 * h + QD, m * GT:m * GT + w], start=True, stop=not last, skip_group_check=True)
                        if last:
                            mm = pe.matmul(ps[:, m, w - P:w], ident_h[:, :], causal[:, :], start=False, stop=True, skip_group_check=True)
                    mm.then_inc(z["sc_ready"], 1)

                def row_turn(y):
                    x, m = quads[y]
                    r = rows[x][1]
                    pe.wait_ge(z["row_exp"], pair * len(rows) + (x + 1))
                    if y >= 2:
                        pe.wait_ge(z["ptl_read"], pair * NQ + (y - 1))
                    for t in range(4 * m, min(4 * m + 4, r + 1)):
                        mm = pe.transpose(ps[:, 4 + y % 2, (t % 4) * P:(t % 4 + 1) * P], prow[:, x % 2, t * P:(t + 1) * P], ident[:, :])
                    mm.then_inc(z["ptl_ready"], 1)

                def row_out(y):
                    x, m = quads[y]
                    h, r = rows[x]
                    pe.wait_ge(z["ptl_read"], pair * NQ + (y + 1))
                    if m == 0 and x >= 1:
                        pe.wait_ge(z["ol_normed"], pair * len(rows) + (x + 1))
                    for t in range(4 * m, min(4 * m + 4, r + 1)):
                        v = vall[:, t, bass.ds(pair * 2 + h, 1), :].rearrange("p a d -> p (a d)")
                        mm = pe.matmul(ps[:, 6, 0:VW], ptl[:, y % 2, (t % 4) * P:(t % 4 + 1) * P], v,
                                       start=(t == 0), stop=(t == r))
                    mm.then_inc(z["pv_part"], 1)

                row_scores(0)
                y = 0
                for x in range(len(rows)):
                    if x + 1 < len(rows):
                        row_scores(x + 1)
                    while y < NQ and quads[y][0] == x:
                        row_turn(y)
                        if y >= 1:
                            row_out(y - 1)
                        y += 1
                row_out(NQ - 1)

            for n in range(G):
                pe.wait_ge(z["ol_normed"], PAIRS * len(rows) + 1)
                if n >= 2:
                    pe.wait_ge(z["lo_copied"], n - 1)
                for m in range(4):
                    mm = pe.transpose(ps[:, n % 2, m * P:(m + 1) * P], oall[:, 4 * n + m, :], ident[:, :])
                mm.then_inc(z["lo_tr"], 1)
                pe.wait_ge(z["lo_copied"], n + 1)
                if n >= 2:
                    pe.wait_ge(z["lo_added"], n - 1)
                pe.matmul(ps[:, 2 + n % 2, :], wl_o[:, :], lot[:, n % 2, :], start=True, stop=True).then_inc(z["lo_mm"], 1)

        @block.scalar
        def _(act):
            for n in range(G):
                act.wait_ge(z["lat_ready"], n + 1)
                if n >= 1:
                    act.wait_ge(z["lat_ms"], n)
                nc.scalar.activation(lsq[:, :], ps[0:KR, 0, :], ACT.Square).then_inc(z["lat_sq"], 1)
                nc.scalar.copy(qc[:, n * GT:(n + 1) * GT], ps[0:QR, 1, :]).then_inc(z["lat_q"], 1)
            with act.Fori(0, PAIRS) as pair:
                def row_exp(x):
                    h, r = rows[x]
                    act.wait_ge(z["row_neg"], pair * len(rows) + (x + 1))
                    act.wait_ge(z["sc_ready"], pair * len(rows) + (x + 1))
                    if x >= 2:
                        act.wait_ge(z["pv_part"], pair * NQ + row_end[x - 2])
                    keys = (r + 1) * P
                    nc.scalar.activation(prow[:, x % 2, 0:keys], ps[:, 0:4, :].rearrange("p b w -> p (b w)")[:, 0:keys],
                                         ACT.Exp, bias=rng[:, x % 2:x % 2 + 1], scale=scale).then_inc(z["row_exp"], 1)

                def turned(y):
                    x, m = quads[y]
                    w = min(GT, (rows[x][1] + 1) * P - m * GT)
                    act.wait_ge(z["ptl_ready"], pair * NQ + (y + 1))
                    if y >= 2:
                        act.wait_ge(z["pv_part"], pair * NQ + (y - 1))
                    nc.scalar.copy(ptl[:, y % 2, 0:w], ps[:, 4 + y % 2, 0:w]).then_inc(z["ptl_read"], 1)

                row_exp(0)
                y = 0
                for x in range(len(rows)):
                    while y < NQ and quads[y][0] == x:
                        turned(y)
                        y += 1
                    if x + 1 < len(rows):
                        row_exp(x + 1)

        @block.vector
        def _(dve):
            for n in range(G):
                cols = slice(n * GT, (n + 1) * GT)
                dve.wait_ge(z["lat_ms"], n + 1)
                if n >= 1:
                    dve.wait_ge(z["lat_pow"], n)
                nc.vector.tensor_scalar(lms[:, :], ps[:, 2, 0:GT // P], RMS_EPS, None, ALU.add).then_inc(z["lat_mse"], 1)
                dve.wait_ge(z["lat_pow"], n + 1)
                if n >= 1:
                    dve.wait_ge(z["lat_rs"], n)
                nc.vector.tensor_tensor(ldg[:, :, :], ident[:, :].unsqueeze(1).to_broadcast([P, GT // P, P]),
                                        lrs[:, :].unsqueeze(2).to_broadcast([P, GT // P, P]), ALU.mult).then_inc(z["lat_diag"], 1)
                dve.wait_ge(z["lat_rs"], n + 1)
                dve.wait_ge(z["lat_q"], n + 1)
                nc.vector.tensor_copy(lrb[:, :], ps[0:KR, 2, :]).then_inc(z["lat_spread"], 1)
                dve.wait_ge(z["lat_spread"], n + 1)
                nc.vector.scalar_tensor_tensor(kvc[:, cols], ps[0:KR, 0, :], g_kv[:, 0:1], lrb[:, :], ALU.mult, ALU.mult).then_inc(z["lat_kv"], 1)
            for n in range(G):
                dve.wait_ge(z["v_mm"], n + 1)
                nc.vector.tensor_copy(vall[:, 4 * n:4 * n + 4, :, 0:CD],
                                      ps[:, 4 + n % 2, :].rearrange("p (t h d) -> p t h d", t=4, h=HEADS)).then_inc(z["v_copied"], 1)
            nc.vector.memset(lrec[:, :], 0.0).then_inc(z["ol_normed"], 1)
            with dve.Fori(0, PAIRS) as pair:
                for j, (w, n) in enumerate(items):
                    cols = slice(n * GT, (n + 1) * GT)
                    dve.wait_ge(z["ab_ready"], pair * len(items) + (j + 1))
                    if j >= 2:
                        dve.wait_ge(z["rope_ready"], pair * len(items) + (j - 1))
                    nc.vector.tensor_tensor(ra[:, j % 2, :], ps[:, j % 2, :], ac[:, cols], ALU.mult).then_inc(z["ra_ready"], 1)
                    nc.vector.tensor_tensor(rb[:, j % 2, :], ps[:, 2 + j % 2, :], as_[:, cols], ALU.mult).then_inc(z["rb_ready"], 1)

                def row_max(x):
                    h, r = rows[x]
                    keys = (r + 1) * P
                    dve.wait_ge(z["sc_ready"], pair * len(rows) + (x + 1))
                    if x >= 2:
                        dve.wait_ge(z["row_neg"], pair * len(rows) + (x - 1))
                    nc.vector.tensor_reduce(rmx[:, x % 2:x % 2 + 1], ps[:, 0:4, :].rearrange("p b w -> p (b w)")[:, 0:keys], X, ALU.max).then_inc(z["row_max"], 1)
                    dve.wait_ge(z["row_max"], pair * len(rows) + (x + 1))
                    if x >= 2:
                        dve.wait_ge(z["row_exp"], pair * len(rows) + (x - 1))
                    nc.vector.tensor_scalar(rng[:, x % 2:x % 2 + 1], rmx[:, x % 2:x % 2 + 1], -scale, None, ALU.mult).then_inc(z["row_neg"], 1)

                def row_norm(x):
                    h, r = rows[x]
                    dve.wait_ge(z["pv_part"], pair * NQ + row_end[x])
                    dve.wait_ge(z["ol_normed"], pair * len(rows) + max(x, 1))
                    nc.vector.reciprocal(lrec[:, x % 2:x % 2 + 1], ps[:, 6, CD:VW]).then_inc(z["ol_rec"], 1)
                    dve.wait_ge(z["ol_rec"], pair * len(rows) + (x + 1))
                    nc.vector.tensor_scalar(oall[:, r, bass.ds(pair * 2 * CD + h * CD, CD)], ps[:, 6, 0:CD], lrec[:, x % 2:x % 2 + 1],
                                            None, ALU.mult).then_inc(z["ol_normed"], 1)

                for x in range(len(rows)):
                    row_max(x)
                    if x >= 2:
                        row_norm(x - 2)
                row_norm(len(rows) - 2)
                row_norm(len(rows) - 1)

            for n in range(G):
                cols = slice(n * GT, (n + 1) * GT)
                dve.wait_ge(z["lo_tr"], n + 1)
                nc.vector.tensor_copy(lot[:, n % 2, :], ps[:, n % 2, :]).then_inc(z["lo_copied"], 1)
                dve.wait_ge(z["lo_mm"], n + 1)
                nc.vector.tensor_tensor(x_res[:, cols], ps[:, 2 + n % 2, :], x_res[:, cols], ALU.add).then_inc(z["lo_added"], 1)


_INS = ["L0_attn_x", "L0_attn_W_kv", "L0_attn_g_kv", "L0_attn_W_kdec", "L0_attn_W_vdec", "L0_attn_W_q", "L0_attn_W_qdec",
        "L0_attn_W_krope", "L0_attn_W_qrope", "L0_attn_W_o", "L0_ffn_Wqkv", "L0_ffn_q_scale", "L0_ffn_k_scale", "L0_ffn_Wo",
        "L0_ffn_ln_g", "L0_ffn_ln_b", "L0_ffn_W1", "L0_ffn_b1", "L0_ffn_W2", "L0_ffn_b2"]


def kernel(**inputs):
    import concourse.bacc as _bacc
    from concourse.bass_utils import run_bass_kernel_spmd as _run

    nc = _bacc.Bacc("TRN2", target_bir_lowering=False, num_devices=1)
    arrays, ins, consts = {}, {}, {}
    for name in _INS:
        a = np.ascontiguousarray(inputs[name])
        arrays[f"in_{name}"] = a
        ins[name] = nc.dram_tensor(f"in_{name}", a.shape, mybir.dt.from_np(a.dtype), kind="ExternalInput").ap()
    for name, a in tables().items():
        arrays[f"const_{name}"] = a
        consts[name] = nc.dram_tensor(f"const_{name}", a.shape, F32, kind="ExternalInput").ap()
    out = nc.dram_tensor("out_0", (1, T, P), F32, kind="ExternalOutput").ap()
    macaron_kernel(nc, ins, consts, out)
    r = _run(nc, [arrays], core_ids=[0])
    return r.results[0]["out_0"]
```

```python
from contextlib import ExitStack

import numpy as np

import concourse.bass as bass
from concourse import mybir


class NormBuffers:

    def __init__(self, M, V, src, xc, sq, ve, rs, dg):
        self.M, self.V, self.src, self.xc, self.sq, self.ve, self.rs, self.dg = M, V, src, xc, sq, ve, rs, dg


ALU = mybir.AluOpType
ACT = mybir.ActivationFunctionType
F32 = mybir.dt.float32
BF16 = mybir.dt.bfloat16
X = mybir.AxisListType.X

P = 128
T = 2048
TILES = T // P
DEPTH = 6
HEADS = 16
DH = 64
WIN = 32
HU = 4
UT = HEADS // HU
UNITS = TILES * UT
KEYS = P + WIN
INNER = 341
CH = [(0, 128), (128, 128), (256, 85)]
G = 4
GT = T // G
NEG = -1.0e30
LN_EPS = 1e-5

QR, KR, CD, RD = 64, 32, 8, 32
QD = CD + RD
RMS_EPS = 1e-6
PAIRS = HEADS // 2

LAG_V, LAG_T, LAG_S, LAG_P, LAG_O, LAG_OT, LAG_Y = 1, 2, 3, 4, 5, 6, 7

WA, WF = 16 * 8, 16 * 12

SEMAPHORES = (
    "const_in consts_ready x_in wa_in wf_in"
    " xs_ready tab_ready qk_ready squared summed clamped inv_ready normed t1_ready t2_ready rotated"
    " tr_ready tr_read s_ready k_carried maxed centred exped pt_ready pt_copied pt_read v_ready vs_ready v_read"
    " o_ready v_carried recip_ready o_normed ot_ready ot_read y_ready x_b_ready"
    " sh_lo sh_hi mean_ready ln_centred ln_squared var_ready vare_ready pow_ready ln_diag rstd_ready ln_scaled ln_ready"
    " up_ready gelu_ready prod_ready down_ready x_a_ready"
    " xt_ready x_res_ready mixed out_t_ready out_ready stored"
    " wl_in wl_zero wl_slots lat_ready lat_sq lat_q lat_ms lat_mse lat_pow lat_diag lat_rs lat_spread lat_kv v_mm v_copied"
    " ab_ready ra_ready rb_ready rope_ready"
    " q_roped sel_ready sc_ready row_max row_top row_neg row_exp ptl_ready ptl_even ptl_odd pv_part ol_copied ol_summed"
    " ol_rec ol_normed"
    " lo_tr lo_copied lo_mm lo_added"
)


def tables():
    f = np.float32
    half = np.arange(0, DH, 2, dtype=f)
    inv = (f(1.0) / (f(10000.0) ** (half / f(DH)))).astype(f)
    t = np.arange(T, dtype=f)
    fr = (t[:, None] * inv[None, :]).astype(f)
    fr = np.concatenate([fr, fr], -1)
    base = ((half + f(0.4 * DH)) / f(1.4 * DH)).astype(f)
    base = np.concatenate([base, base])
    local = (np.arange(T) % P - P // 2) / (WIN // 2)
    grow = base[None, :].astype(np.float64) ** local[:, None]
    cos, sin = np.cos(fr), np.sin(fr)
    sgn = np.concatenate([-np.ones(DH // 2), np.ones(DH // 2)])
    wc = np.stack([cos * grow, cos / grow], 1)
    ws = np.stack([sin * sgn * grow, sin * sgn / grow], 1)
    wc = wc.reshape(TILES, P, 2, DH).transpose(1, 0, 2, 3)
    ws = ws.reshape(TILES, P, 2, DH).transpose(1, 0, 2, 3)
    carry = (base.astype(np.float64) ** (P / (WIN // 2)))
    carry = np.concatenate([carry, carry])[:, None]
    i, j = np.arange(P)[:, None], np.arange(P)[None, :]
    main = np.where((j <= i) & (j >= i - WIN), 0.0, NEG)
    js = np.arange(WIN)[None, :]
    side = np.where((i < WIN) & (js >= i), 0.0, NEG)
    wmask = np.stack([np.concatenate([main, np.full((P, WIN), NEG)], 1),
                      np.concatenate([main, side], 1)], 1)
    causal = np.where(j <= i, 0.0, NEG)
    inv2 = (1.0 / 10000.0 ** (np.arange(0, RD, 2, dtype=f) / RD)).astype(f)
    fr2 = np.outer(t, inv2).astype(f)
    e2 = np.concatenate([fr2, fr2], -1)
    ac, as_ = np.zeros((P, T)), np.zeros((P, T))
    sg2 = np.concatenate([-np.ones(RD // 2), np.ones(RD // 2)])
    for h in range(2):
        ac[64 * h:64 * h + RD] = np.cos(e2).T
        ac[64 * h + RD:64 * h + QD] = 1.0
        as_[64 * h:64 * h + RD] = (np.sin(e2) * sg2).T
    out = dict(ident=np.eye(P), wc=wc, ws=ws, carry=carry, wmask=wmask, causal=causal, ac=ac, as_=as_)
    return {k: np.ascontiguousarray(v, dtype=f) for k, v in out.items()}



def macaron_kernel(nc, i, c, out):
    with ExitStack() as ctx:
        def sb(name, shape, dt=F32):
            return ctx.enter_context(nc.sbuf_tensor(name, shape, dt))

        z = {n: ctx.enter_context(nc.semaphore(n)) for n in SEMAPHORES.split()}
        x_res = sb("x_res", [P, T])
        x_a = sb("x_a", [P, 1 + T + P])
        x_b = sb("x_b", [P, 1 + T])
        ident = sb("ident", [P, P])
        ident_h = sb("ident_h", [P, P], BF16)
        wmask = sb("wmask", [P, 2, KEYS], BF16)
        causal = sb("causal", [P, P], BF16)
        carry_f = sb("carry_f", [P, 1])
        mean_w = sb("mean_w", [P, P])
        ones_w = sb("ones_w", [P, P])
        neg_half = sb("neg_half", [P, 2 * HU])
        zeros = sb("zeros", [P, P])
        x_dram = i["L0_attn_x"].rearrange("a (n p) d -> p (a n) d", p=P)
        out_dram = out.rearrange("a (n p) d -> p (a n) d", p=P)

        load_input(nc, z, c, x_dram, x_res, x_a, x_b, ident, ident_h, wmask, causal, carry_f, mean_w, ones_w, neg_half, zeros)
        outer_norm(nc, z, "na", 0, x_res, x_a, ident, mean_w, ones_w, neg_half)
        window_stack(nc, z, i, c, 0, G, x_a, x_b, ident, ident_h, wmask, carry_f, mean_w, ones_w, neg_half, zeros)
        mix(nc, z, 0, x_res, x_a)
        n1 = G + DEPTH * G
        outer_norm(nc, z, "nb", n1, x_res, x_a, ident, mean_w, ones_w, neg_half)
        latent_attention(nc, z, i, c, x_res, x_a, ident, ident_h, causal, ones_w, neg_half, zeros)
        outer_norm(nc, z, "nc", n1 + G, x_res, x_a, ident, mean_w, ones_w, neg_half)
        window_stack(nc, z, i, c, 1, n1 + 2 * G, x_a, x_b, ident, ident_h, wmask, carry_f, mean_w, ones_w, neg_half, zeros)
        mix(nc, z, 1, x_res, x_a)
        store_output(nc, z, out_dram, x_res, ident)


def load_input(nc, z, c, x_dram, x_res, x_a, x_b, ident, ident_h, wmask, causal, carry_f, mean_w, ones_w, neg_half, zeros):
    with ExitStack() as st:
        x_tok = st.enter_context(nc.sbuf_tensor("x_tok", [P, TILES, P], F32))
        wmask_f = st.enter_context(nc.sbuf_tensor("wmask_f", [P, 2, KEYS], F32))
        causal_f = st.enter_context(nc.sbuf_tensor("causal_f", [P, P], F32))
        tp = st.enter_context(nc.psum_tensor("turned_in", [P, 2, GT], F32))
        block = st.enter_context(nc.Block())

        @block.sync
        def _(sp):
            sp.dma_start(ident[:, :], c["ident"]).then_inc(z["const_in"], 16)
            for n in range(G):
                sp.dma_start(x_tok[:, 4 * n:4 * n + 4, :], x_dram[:, 4 * n:4 * n + 4, :]).then_inc(z["x_in"], 16)
            sp.dma_start(wmask_f[:, :, :], c["wmask"]).then_inc(z["const_in"], 16)
            sp.dma_start(causal_f[:, :], c["causal"]).then_inc(z["const_in"], 16)
            sp.dma_start(carry_f[:, :], c["carry"]).then_inc(z["const_in"], 16)

        @block.gpsimd
        def _(pool):
            nc.gpsimd.memset(mean_w[:, :], 1.0 / P).then_inc(z["consts_ready"], 1)
            nc.gpsimd.memset(neg_half[:, :], -0.5).then_inc(z["x_a_ready"], 1)
            nc.gpsimd.memset(ones_w[:, :], 1.0).then_inc(z["consts_ready"], 1)
            nc.gpsimd.memset(zeros[:, :], 0.0).then_inc(z["consts_ready"], 1)
            nc.gpsimd.memset(x_a[:, :], 0.0).then_inc(z["consts_ready"], 1)
            nc.gpsimd.memset(x_b[:, 0:1], 0.0).then_inc(z["consts_ready"], 1)

        @block.tensor
        def _(pe):
            pe.wait_ge(z["const_in"], 64)
            for n in range(G):
                pe.wait_ge(z["x_in"], 16 * G)
                if n >= 2:
                    pe.wait_ge(z["x_res_ready"], n - 1)
                for m in range(4):
                    mm = pe.transpose(tp[:, n % 2, m * P:(m + 1) * P], x_tok[:, 4 * n + m, :], ident[:, :])
                mm.then_inc(z["xt_ready"], 1)

        @block.vector
        def _(dve):
            dve.wait_ge(z["const_in"], 64)
            nc.vector.tensor_copy(ident_h[:, :], ident[:, :]).then_inc(z["consts_ready"], 1)
            nc.vector.tensor_copy(wmask[:, :, :], wmask_f[:, :, :]).then_inc(z["consts_ready"], 1)
            nc.vector.tensor_copy(causal[:, :], causal_f[:, :]).then_inc(z["consts_ready"], 1)
            for n in range(G):
                dve.wait_ge(z["xt_ready"], n + 1)
                nc.vector.tensor_copy(x_res[:, n * GT:(n + 1) * GT], tp[:, n % 2, :]).then_inc(z["x_res_ready"], 1)


def norm_mean(nc, z, pe, b, mean_w, q, n):
    if n >= 1:
        pe.wait_ge(z["ln_centred"], q)
    pe.matmul(b.M, mean_w[:, :], b.src(n), start=True, stop=True).then_inc(z["mean_ready"], 1)


def norm_var(nc, z, pe, b, mean_w, q, n):
    pe.wait_ge(z["ln_squared"], q + 1)
    if n >= 1:
        pe.wait_ge(z["ln_scaled"], q)
    for m in range(GT // P):
        mm = pe.matmul(b.V[:, m:m + 1], b.sq(n)[:, m * P:(m + 1) * P], mean_w[:, 0:1], start=True, stop=True)
    mm.then_inc(z["var_ready"], 1)


def norm_spread(nc, z, pe, b, ones_w, q, n):
    pe.wait_ge(z["ln_diag"], q + 1)
    pe.matmul(b.V, ones_w[:, :], b.dg[:, :, :], start=True, stop=True).then_inc(z["rstd_ready"], 1)


def norm_centre(nc, z, dve, b, q, n):
    dve.wait_ge(z["mean_ready"], q + 1)
    if n >= 2:
        dve.wait_ge(z["ln_squared"], q - 1)
        dve.wait_ge(z["ln_scaled"], q - 1)
    nc.vector.tensor_tensor(b.xc(n), b.src(n), b.M, ALU.subtract).then_inc(z["ln_centred"], 1)


def norm_square(nc, z, act, b, q, n):
    act.wait_ge(z["ln_centred"], q + 1)
    if n >= 2:
        act.wait_ge(z["var_ready"], q - 1)
    nc.scalar.activation(b.sq(n), b.xc(n), ACT.Square).then_inc(z["ln_squared"], 1)


def norm_eps(nc, z, dve, b, q, n):
    dve.wait_ge(z["var_ready"], q + 1)
    if n >= 1:
        dve.wait_ge(z["pow_ready"], q)
    nc.vector.tensor_scalar(b.ve, b.V[:, 0:GT // P], LN_EPS, None, ALU.add).then_inc(z["vare_ready"], 1)


def norm_rstd(nc, z, pool, b, neg_half, q, n):
    if n >= 1:
        pool.wait_ge(z["ln_diag"], q)
    pool.wait_ge(z["vare_ready"], q + 1)
    nc.gpsimd.tensor_tensor(b.rs, b.ve, neg_half[:, 0:GT // P], ALU.pow).then_inc(z["pow_ready"], 1)


def norm_diagonal(nc, z, dve, b, ident, q, n):
    dve.wait_ge(z["pow_ready"], q + 1)
    if n >= 1:
        dve.wait_ge(z["rstd_ready"], q)
    nc.vector.tensor_tensor(b.dg[:, :, :], ident[:, :].unsqueeze(1).to_broadcast([P, GT // P, P]),
                            b.rs.unsqueeze(2).to_broadcast([P, GT // P, P]), ALU.mult).then_inc(z["ln_diag"], 1)


def outer_norm(nc, z, tag, q0, x_res, x_a, ident, mean_w, ones_w, neg_half):
    with ExitStack() as st:
        b4 = {n: st.enter_context(nc.sbuf_tensor(f"{tag}_{n}", [P, 2, GT], F32)) for n in ("xc", "sq")}
        small = st.enter_context(nc.sbuf_tensor(f"{tag}_small", [P, 2, GT // P], F32))
        dg = st.enter_context(nc.sbuf_tensor(f"{tag}_dg", [P, GT // P, P], F32))
        ps = st.enter_context(nc.psum_tensor(f"{tag}_ps", [P, 2, GT], F32))
        b = NormBuffers(
            M=ps[:, 0, :], V=ps[:, 1, :], src=lambda n: x_res[:, n * GT:(n + 1) * GT],
            xc=lambda n: b4["xc"][:, n % 2, :], sq=lambda n: b4["sq"][:, n % 2, :],
            ve=small[:, 0, :], rs=small[:, 1, :], dg=dg)
        block = st.enter_context(nc.Block())

        @block.tensor
        def _(pe):
            pe.wait_ge(z["consts_ready"], 8)
            for n in range(G + 1):
                if n < G:
                    norm_mean(nc, z, pe, b, mean_w, q0 + n, n)
                if n >= 1:
                    norm_var(nc, z, pe, b, mean_w, q0 + n - 1, n - 1)
                    norm_spread(nc, z, pe, b, ones_w, q0 + n - 1, n - 1)

        @block.scalar
        def _(act):
            for n in range(G):
                norm_square(nc, z, act, b, q0 + n, n)

        @block.gpsimd
        def _(pool):
            for n in range(G):
                norm_rstd(nc, z, pool, b, neg_half, q0 + n, n)

        @block.vector
        def _(dve):
            for n in range(G + 1):
                if n < G:
                    norm_centre(nc, z, dve, b, q0 + n, n)
                if n >= 1:
                    m = n - 1
                    norm_eps(nc, z, dve, b, q0 + m, m)
                    norm_diagonal(nc, z, dve, b, ident, q0 + m, m)
                    dve.wait_ge(z["rstd_ready"], q0 + m + 1)
                    nc.vector.tensor_tensor(x_a[:, 1 + m * GT:1 + (m + 1) * GT], b.xc(m), b.V, ALU.mult).then_inc(z["ln_scaled"], 1)


def window_stack(nc, z, i, c, k, q0, x_a, x_b, ident, ident_h, wmask, carry_f, mean_w, ones_w, neg_half, zeros):
    with ExitStack() as st:
        def sb(name, shape, dt=F32):
            return st.enter_context(nc.sbuf_tensor(f"{name}_{k}", shape, dt))

        w_qkv = sb("w_qkv", [P, 3, HEADS * DH])
        w_o = sb("w_o", [P, HEADS * DH // P, P])
        w_1 = sb("w_1", [P, 2 * INNER])
        w_2 = sb("w_2", [P, len(CH), P])
        vec = sb("vec", [P, 9])
        qk_sc = sb("qk_sc", [P, 2, DH])
        qk_sw = sb("qk_sw", [P, 2, DH])
        wcos = sb("wcos", [P, TILES + 1, 2, DH])
        wsin = sb("wsin", [P, TILES + 1, 2, DH])
        tab_c = sb("tab_c", [P, 2, 2, DH])
        tab_s = sb("tab_s", [P, 2, 2, DH])
        xs = sb("xs", [P, 2, P])
        QK = 2 * HU * DH
        sq = sb("sq", [P, 2, QK])
        ss = sb("ss", [P, 2, 2 * HU])
        ssm = sb("ssm", [P, 2, 2 * HU])
        inv = sb("inv", [P, 2, 2 * HU])
        qn = sb("qn", [P, 2, QK])
        t1 = sb("t1", [P, 2, QK])
        t2 = sb("t2", [P, 2, QK])
        rot = sb("rot", [P, 4, QK])
        qkt = sb("qkt", [P, 2, 4, P])
        k_car = sb("k_car", [P, UT, 2, WIN])
        mx = sb("mx", [P, 2, HU])
        cen = sb("cen", [P, 2, HU, KEYS])
        prob = sb("prob", [P, 2, HU, KEYS])
        pt = sb("pt", [P, 2, HU, P])
        pts = sb("pts", [P, 2, HU, WIN])
        AW = DH + 1
        vt = sb("vt", [P, 8, HU, AW])
        v_car = sb("v_car", [P, UT, HU, AW])
        rec = sb("rec", [P, 2, HU])
        on = sb("on", [P, 2, HU * DH])
        ots = sb("ots", [P, 8, 2, P])
        f2 = {n: sb("f" + n, [P, 2, GT]) for n in ("src", "xc", "sq", "xn", "gl")}
        fsmall = sb("fsmall", [P, 2, GT // P])
        fdg = sb("fdg", [P, GT // P, P])
        fsc = sb("fsc", [P, GT])
        hm = sb("hm", [P, 4, GT])
        ps = st.enter_context(nc.psum_tensor(f"ps_{k}", [P, 8, 512], F32))
        fb = NormBuffers(
            M=ps[:, 0, :], V=ps[:, 1, :], src=lambda n: f2["src"][:, n % 2, :],
            xc=lambda n: f2["xc"][:, n % 2, :], sq=lambda n: f2["sq"][:, n % 2, :],
            ve=fsmall[:, 0, :], rs=fsmall[:, 1, :], dg=fdg)
        L0 = k * DEPTH
        side = ps[:, 6, 256:256 + HU * WIN]
        heads_qk = lambda t: t.rearrange("p (q h d) -> p q h d", q=2, h=HU)
        scores = ps[:, 2:4, 0:2 * KEYS].rearrange("p b (r j) -> p b r j", r=2)
        by_bank = lambda t: t.rearrange("p (r b) j -> p b r j", b=2)

        def slots(eng, slot):
            for s in range(8):
                slot(s, 0, "first")
            with eng.Fori(1, TILES // 2) as pair:
                for s in range(8):
                    slot(s, pair, "steady")
            for s in range(8):
                slot(s, TILES // 2, "last")

        def clock(L, s, pair, part):
            def live(lag):
                return {"first": s >= lag, "steady": True, "last": s < lag}[part]

            def had(lag, back):
                return part != "first" or s - lag - back >= 0

            def done(lag, back=0):
                return (L + L0) * UNITS + pair * 8 + (s - lag - back + 1)
            return live, had, done

        def tile_no(L, s, pair):
            return (L + L0) * (TILES + 1) + pair * 2 + (s // UT + 1)

        def tiles_out(L, s, pair):
            return (L + L0) * TILES + pair * 2 + (s - LAG_Y - (UT - 1)) // UT + 1

        block = st.enter_context(nc.Block())

        @block.sync
        def _(sp):
            sp.dma_start(wcos[:, 0:TILES], c["wc"]).then_inc(z["const_in"], 16)
            sp.dma_start(wsin[:, 0:TILES], c["ws"]).then_inc(z["const_in"], 16)
            hf = DH // 2
            def attention_weights(L):
                sp.dma_start(w_qkv[:, :, :], i["L0_ffn_Wqkv"][bass.ds(L, 1)].rearrange("a p (t n) -> p (a t) n", t=3)).then_inc(z["wa_in"], 16)
                sp.dma_start(w_o[:, :, :], i["L0_ffn_Wo"][bass.ds(L, 1)].rearrange("a (c p) n -> p (a c) n", p=P)).then_inc(z["wa_in"], 16)

            def attention_scales(L):
                for q, name in enumerate(("L0_ffn_q_scale", "L0_ffn_k_scale")):
                    row = i[name][bass.ds(L, 1)]
                    sp.dma_start(qk_sc[:, q, :], row.to_broadcast([P, DH])).then_inc(z["wa_in"], 16)
                    sp.dma_start(qk_sw[:, q, 0:hf], row[:, hf:DH].to_broadcast([P, hf])).then_inc(z["wa_in"], 16)
                    sp.dma_start(qk_sw[:, q, hf:DH], row[:, 0:hf].to_broadcast([P, hf])).then_inc(z["wa_in"], 16)

            def feed_forward_weights(L):
                sp.dma_start(w_1[:, :], i["L0_ffn_W1"][bass.ds(L, 1)].rearrange("a p n -> p (a n)")).then_inc(z["wf_in"], 16)
                whole = 2 * P
                sp.dma_start(w_2[:, 0:2, :], i["L0_ffn_W2"][bass.ds(L, 1), 0:whole].rearrange("a (c p) n -> p (a c) n", p=P)).then_inc(z["wf_in"], 16)
                sp.dma_start(w_2[0:INNER - whole, 2, :], i["L0_ffn_W2"][bass.ds(L, 1), whole:INNER].rearrange("a p n -> p (a n)")).then_inc(z["wf_in"], 16)
                with nc.allow_non_contiguous_dma(reason="vectors onto partitions"):
                    for q, name in enumerate(("L0_ffn_ln_g", "L0_ffn_ln_b", "L0_ffn_b2")):
                        sp.dma_start(vec[:, q:q + 1], i[name][bass.ds(L, 1)].rearrange("a p -> p a")).then_inc(z["wf_in"], 16)
                    for q in range(2):
                        for m, (lo, w) in enumerate(CH):
                            b1 = i["L0_ffn_b1"][bass.ds(L, 1), q * INNER + lo:q * INNER + lo + w]
                            sp.dma_start(vec[0:w, 3 + 3 * q + m:4 + 3 * q + m], b1.rearrange("a p -> p a")).then_inc(z["wf_in"], 16)

            attention_weights(0)
            attention_scales(0)
            feed_forward_weights(0)
            with sp.Fori(1, DEPTH) as L:
                sp.wait_ge(z["y_ready"], (L + L0) * TILES)
                attention_weights(L)
                sp.wait_ge(z["tab_ready"], (L + L0) * (2 * TILES + 2))
                attention_scales(L)
                sp.wait_ge(z["x_a_ready"], (L + L0) * G + 1)
                feed_forward_weights(L)

        @block.gpsimd
        def _(pool):
            nc.gpsimd.memset(vt[:, :, :, :], 1.0).then_inc(z["consts_ready"], 1)
            nc.gpsimd.memset(k_car[:, :, :, :], 0.0).then_inc(z["consts_ready"], 1)
            nc.gpsimd.memset(v_car[:, :, :, :], 0.0).then_inc(z["consts_ready"], 1)
            nc.gpsimd.memset(wcos[:, TILES], 0.0).then_inc(z["consts_ready"], 1)
            nc.gpsimd.memset(wsin[:, TILES], 0.0).then_inc(z["consts_ready"], 1)
            pool.wait_ge(z["consts_ready"], 8 + 5 * (k + 1))
            pool.wait_ge(z["const_in"], 64 + 32 * (k + 1))
            with pool.Fori(0, DEPTH) as L:
                def scaled_tables(tile, par):
                    flat = lambda t: t[:, bass.ds(tile, 1)].rearrange("p a q d -> p (a q) d")
                    nc.gpsimd.tensor_tensor(tab_c[:, par], flat(wcos), qk_sc[:, :, :], ALU.mult).then_inc(z["tab_ready"], 1)
                    nc.gpsimd.tensor_tensor(tab_s[:, par], flat(wsin), qk_sw[:, :, :], ALU.mult).then_inc(z["tab_ready"], 1)

                pool.wait_ge(z["wa_in"], (L + L0 + 1) * WA)
                scaled_tables(0, 0)

                def slot(s, pair, part):
                    live, had, done = clock(L, s, pair, part)
                    r2, r4, par = s % 2, s % 4, s // UT
                    if live(0):
                        if s % UT == 1:
                            if had(0, 2):
                                pool.wait_ge(z["t2_ready"], 2 * done(0, 2))
                            scaled_tables(pair * 2 + (par + 1), (par + 1) % 2)
                        pool.wait_ge(z["clamped"], done(0))
                        if had(0, 2):
                            pool.wait_ge(z["normed"], done(0, 2))
                        nc.gpsimd.tensor_tensor(inv[:, r2], ssm[:, r2], neg_half[:, 0:2 * HU], ALU.pow).then_inc(z["inv_ready"], 1)
                        pool.wait_ge(z["normed"], done(0))
                        pool.wait_ge(z["tab_ready"], 2 * tile_no(L, s, pair))
                        if had(0, 2):
                            pool.wait_ge(z["rotated"], done(0, 2))
                        cb = tab_c[:, par].unsqueeze(2).to_broadcast([P, 2, HU, DH])
                        nc.gpsimd.tensor_tensor(heads_qk(t1[:, r2]), heads_qk(qn[:, r2]), cb, ALU.mult).then_inc(z["t1_ready"], 1)
                        pool.wait_ge(z["t1_ready"], done(0))
                        pool.wait_ge(z["t2_ready"], 2 * done(0))
                        if had(0, 4):
                            pool.wait_ge(z["tr_ready"], done(0, 4))
                        nc.gpsimd.tensor_tensor(rot[:, r4], t1[:, r2], t2[:, r2], ALU.add).then_inc(z["rotated"], 1)
                    if live(LAG_S):
                        m = (s - LAG_S) % 8
                        pool.wait_ge(z["s_ready"], done(LAG_S))
                        nc.gpsimd.tensor_tensor(k_car[:, m % UT], qkt[:, m % 2, 2:4, P - WIN:P], carry_f[:, 0:1].unsqueeze(2).to_broadcast([P, 2, WIN]), ALU.mult).then_inc(z["k_carried"], 1)
                slots(pool, slot)

                for n in range(G):
                    norm_rstd(nc, z, pool, fb, neg_half, q0 + L * G + n, n)

        @block.tensor
        def _(pe):
            pe.wait_ge(z["consts_ready"], 8 + 5 * (k + 1))
            with pe.Fori(0, DEPTH) as L:
                pe.wait_ge(z["wa_in"], (L + L0 + 1) * WA)
                pe.wait_ge(z["x_a_ready"], (L + L0) * G + 1)

                def slot(s, pair, part):
                    live, had, done = clock(L, s, pair, part)
                    if live(0):
                        u = s % UT
                        pe.wait_ge(z["xs_ready"], 2 * tile_no(L, s, pair))
                        if had(0, 2):
                            pe.wait_ge(z["squared"], done(0, 2))
                            pe.wait_ge(z["normed"], done(0, 2))
                        pe.matmul(ps[:, s % 2, :], xs[:, s // UT, :], w_qkv[:, 0:2, u * 256:(u + 1) * 256],
                                  start=True, stop=True).then_inc(z["qk_ready"], 1)
                    if live(LAG_T):
                        bank = 4 + (3 * s) % 2
                        pe.wait_ge(z["rotated"], done(LAG_T))
                        if had(LAG_P, 1):
                            pe.wait_ge(z["pt_read"], done(LAG_P, 1))
                        elif had(LAG_T, 2):
                            pe.wait_ge(z["tr_read"], done(LAG_T, 2))
                        for m in range(4):
                            mm = pe.transpose(ps[:, bank, m * P:(m + 1) * P],
                                              rot[:, (s - LAG_T) % 4, m * P:(m + 1) * P], ident[:, :])
                        mm.then_inc(z["tr_ready"], 1)
                    if live(LAG_S):
                        n = (s - LAG_S) % 8
                        pe.wait_ge(z["tr_read"], done(LAG_S))
                        if had(LAG_S, 1):
                            pe.wait_ge(z["centred"], done(LAG_S, 1))
                        if had(LAG_S, UT):
                            pe.wait_ge(z["k_carried"], done(LAG_S, UT))
                        first = part == "first" and n < UT
                        for b in range(2):
                            m = wmask[:, 0 if first else 1].unsqueeze(1).to_broadcast([P, 2, KEYS])
                            pe.matmul(scores[:, b], ident_h[:, :], m, start=True, stop=False, skip_group_check=True)
                            h0 = 64 * b
                            for r in range(2):
                                q = qkt[h0:h0 + 64, n % 2, r, :]
                                pe.matmul(scores[:, b, r, 0:P], q, qkt[h0:h0 + 64, n % 2, 2 + r, :],
                                          start=False, stop=False, skip_group_check=True)
                                mm = pe.matmul(scores[0:WIN, b, r, P:KEYS], q[:, 0:WIN], k_car[h0:h0 + 64, n % UT, r, :],
                                               start=False, stop=True, skip_group_check=True)
                        mm.then_inc(z["s_ready"], 1)
                    if live(LAG_P):
                        n = (s - LAG_P) % 8
                        bank = 4 + (3 * s + 1) % 2
                        pe.wait_ge(z["exped"], done(LAG_P))
                        if had(LAG_OT, 1):
                            pe.wait_ge(z["ot_read"], done(LAG_OT, 1))
                        else:
                            pe.wait_ge(z["tr_read"], done(LAG_T, 1))
                        if part != "last" or s <= LAG_V:
                            pe.wait_ge(z["v_read"], done(LAG_V, 1))
                        if had(LAG_P, 1):
                            pe.wait_ge(z["pt_read"], done(LAG_P, 1))
                        for h in range(HU):
                            mm = pe.transpose(ps[:, bank, h * P:(h + 1) * P], prob[:, n % 2, h, 0:P], ident[:, :])
                        mm.then_inc(z["pt_ready"], 1)
                        for h in range(HU):
                            mm = pe.transpose(side[0:WIN, h * WIN:(h + 1) * WIN], prob[0:WIN, n % 2, h, P:KEYS], ident[0:WIN, 0:WIN])
                        if not live(LAG_V):
                            mm.then_inc(z["vs_ready"], 1)
                    if live(LAG_V):
                        n = (s - LAG_V) % 8
                        if had(LAG_V, 1) and not live(LAG_P):
                            pe.wait_ge(z["v_read"], done(LAG_V, 1))
                        mm = pe.matmul(ps[:, 6, 0:256], xs[:, n // UT, :], w_qkv[:, 2, (n % UT) * 256:(n % UT + 1) * 256],
                                       start=True, stop=True)
                        mm.then_inc(z["v_ready"], 1)
                    yt = live(LAG_Y) and (s - LAG_Y) % UT == UT - 1
                    if yt:
                        pe.wait_ge(z["ot_read"], done(LAG_Y))
                        if part != "last" or s <= LAG_O:
                            pe.wait_ge(z["o_normed"], done(LAG_O, 1))
                        else:
                            pe.wait_ge(z["o_normed"], (L + L0 + 1) * UNITS)
                        base = (s - LAG_Y - (UT - 1)) % 8
                        for m in range(2 * UT):
                            mm = pe.matmul(ps[:, 7, 384:512], w_o[:, m, :], ots[:, base + m // 2, m % 2, :],
                                           start=(m == 0), stop=(m == 2 * UT - 1))
                        mm.then_inc(z["y_ready"], 1)
                    if live(LAG_O):
                        n = (s - LAG_O) % 8
                        pe.wait_ge(z["pt_read"], done(LAG_O))
                        pe.wait_ge(z["v_read"], done(LAG_O))
                        if had(LAG_O, UT - 1):
                            pe.wait_ge(z["v_carried"], done(LAG_O, UT - 1))
                        if had(LAG_O, 1):
                            pe.wait_ge(z["o_normed"], done(LAG_O, 1))
                        if had(LAG_Y, 1) and (s - LAG_Y - 1) % UT == UT - 1:
                            pe.wait_ge(z["x_b_ready"], tiles_out(L, s - 1, pair))
                        for h in range(HU):
                            o = ps[:, 7, h * AW:(h + 1) * AW]
                            pe.matmul(o, pt[:, n % 2, h, :], vt[:, n, h, :], start=True, stop=False, skip_group_check=True)
                            mm = pe.matmul(o[0:WIN], pts[P - WIN:P, n % 2, h, :], v_car[P - WIN:P, n % UT, h, :],
                                           start=False, stop=True, skip_group_check=True, tile_position=(P - WIN, 0))
                        mm.then_inc(z["o_ready"], 1)
                    if live(LAG_OT):
                        n = (s - LAG_OT) % 8
                        bank = 4 + (3 * s + 2) % 2
                        pe.wait_ge(z["o_normed"], done(LAG_OT))
                        if live(LAG_T):
                            pe.wait_ge(z["tr_read"], done(LAG_T))
                        elif s <= LAG_P:
                            pe.wait_ge(z["pt_read"], done(LAG_P, 1))
                        else:
                            pe.wait_ge(z["ot_read"], done(LAG_OT, 2))
                        for m in range(2):
                            mm = pe.transpose(ps[:, bank, m * P:(m + 1) * P], on[:, n % 2, m * P:(m + 1) * P], ident[:, :])
                        mm.then_inc(z["ot_ready"], 1)
                slots(pe, slot)

                g = L + L0
                pe.wait_ge(z["wf_in"], (g + 1) * WF)
                pe.wait_ge(z["x_b_ready"], (g + 1) * TILES)
                q1 = q0 + L * G

                def mean(n):
                    pe.wait_ge(z["sh_lo"], g * G + (n + 1))
                    pe.wait_ge(z["sh_hi"], g * G + (n + 1))
                    norm_mean(nc, z, pe, fb, mean_w, q1 + n, n)

                def up(n, m):
                    j = 3 * n + m
                    lo, w = CH[m]
                    pe.wait_ge(z["ln_ready"], g * G + (n + 1))
                    if j >= 2:
                        pe.wait_ge(z["prod_ready"], g * 3 * G + (j - 1))
                    pe.matmul(ps[0:w, 2 + j % 2, :], w_1[:, lo:lo + w], f2["xn"][:, n % 2, :], start=True, stop=True)
                    pe.matmul(ps[0:w, 4 + j % 2, :], w_1[:, INNER + lo:INNER + lo + w], f2["xn"][:, n % 2, :],
                              start=True, stop=True).then_inc(z["up_ready"], 1)

                def down(n, m):
                    j = 3 * n + m
                    w = CH[m][1]
                    pe.wait_ge(z["prod_ready"], g * 3 * G + (j + 1))
                    if m == 0 and n >= 2:
                        pe.wait_ge(z["x_a_ready"], g * G + n)
                    pe.matmul(ps[:, 6 + n % 2, :], w_2[0:w, m, :], hm[0:w, j % 4, :],
                              start=(m == 0), stop=(m == len(CH) - 1)).then_inc(z["down_ready"], 1)

                mean(0)
                norm_var(nc, z, pe, fb, mean_w, q1, 0)
                norm_spread(nc, z, pe, fb, ones_w, q1, 0)
                for n in range(G):
                    up(n, 0)
                    up(n, 1)
                    if n + 1 < G:
                        mean(n + 1)
                    down(n, 0)
                    up(n, 2)
                    if n + 1 < G:
                        norm_var(nc, z, pe, fb, mean_w, q1 + n + 1, n + 1)
                    down(n, 1)
                    if n + 1 < G:
                        norm_spread(nc, z, pe, fb, ones_w, q1 + n + 1, n + 1)
                    down(n, 2)

        @block.scalar
        def _(act):
            with act.Fori(0, DEPTH) as L:
                def slot(s, pair, part):
                    live, had, done = clock(L, s, pair, part)
                    if live(0):
                        act.wait_ge(z["qk_ready"], done(0))
                        if had(0, 2):
                            act.wait_ge(z["summed"], done(0, 2))
                        nc.scalar.activation(sq[:, s % 2], ps[:, s % 2, :], ACT.Square).then_inc(z["squared"], 1)
                    if live(LAG_T):
                        n = (s - LAG_T) % 8
                        act.wait_ge(z["tr_ready"], done(LAG_T))
                        if had(LAG_T, 2):
                            act.wait_ge(z["s_ready"], done(LAG_T, 2))
                            act.wait_ge(z["k_carried"], done(LAG_T, 2))
                        nc.scalar.copy(qkt[:, n % 2].rearrange("p a t -> p (a t)"), ps[:, 4 + (3 * s) % 2, :]).then_inc(z["tr_read"], 1)
                    if live(LAG_P):
                        n = (s - LAG_P) % 8
                        act.wait_ge(z["pt_ready"], done(LAG_P))
                        if had(LAG_P, 2):
                            act.wait_ge(z["o_ready"], done(LAG_P, 2))
                        nc.scalar.copy(pt[:, n % 2].rearrange("p a t -> p (a t)"), ps[:, 4 + (3 * s + 1) % 2, :]).then_inc(z["pt_copied"], 1)
                        if live(LAG_V):
                            act.wait_ge(z["v_ready"], done(LAG_V))
                        else:
                            act.wait_ge(z["vs_ready"], (L + L0) * (LAG_P - LAG_V) + (s - LAG_V + 1))
                        nc.scalar.copy(pts[P - WIN:P, n % 2].rearrange("p a t -> p (a t)"), side[0:WIN]).then_inc(z["pt_read"], 1)
                    if live(LAG_V):
                        n = (s - LAG_V) % 8
                        act.wait_ge(z["v_ready"], done(LAG_V))
                        if had(LAG_V, 7):
                            act.wait_ge(z["v_carried"], done(LAG_V, 7))
                        nc.scalar.copy(vt[:, n, :, 0:DH], ps[:, 6, 0:256].rearrange("p (h d) -> p h d", h=HU)).then_inc(z["v_read"], 1)
                    if live(LAG_OT):
                        n = (s - LAG_OT) % 8
                        act.wait_ge(z["ot_ready"], done(LAG_OT))
                        nc.scalar.copy(ots[:, n].rearrange("p a t -> p (a t)"), ps[:, 4 + (3 * s + 2) % 2, 0:256]).then_inc(z["ot_read"], 1)
                    if live(LAG_S):
                        n = (s - LAG_S) % 8
                        act.wait_ge(z["centred"], done(LAG_S))
                        if had(LAG_S, 2):
                            act.wait_ge(z["pt_ready"], done(LAG_S, 2))
                            act.wait_ge(z["pt_read"], done(LAG_S, 2))
                        nc.scalar.activation(prob[:, n % 2], cen[:, n % 2], ACT.Exp, scale=float(DH) ** 0.5).then_inc(z["exped"], 1)
                    if live(LAG_O):
                        n = (s - LAG_O) % 8
                        act.wait_ge(z["o_ready"], done(LAG_O))
                        act.wait_ge(z["v_read"], done(LAG_O))
                        nc.scalar.copy(v_car[P - WIN:P, n % UT], vt[P - WIN:P, n]).then_inc(z["v_carried"], 1)
                slots(act, slot)

                g = L + L0
                q1 = q0 + L * G

                def shift(n):
                    act.wait_ge(z["x_b_ready"], g * TILES + 4 * (n + 1))
                    if n >= 2:
                        act.wait_ge(z["ln_centred"], q1 + (n - 1))
                    nc.scalar.copy(f2["src"][0:64, n % 2, :], x_b[0:64, 1 + n * GT:1 + (n + 1) * GT]).then_inc(z["sh_lo"], 1)

                def gelu(n, m):
                    j = 3 * n + m
                    w = CH[m][1]
                    act.wait_ge(z["up_ready"], g * 3 * G + (j + 1))
                    if j >= 2:
                        act.wait_ge(z["prod_ready"], g * 3 * G + (j - 1))
                    nc.scalar.activation(f2["gl"][0:w, j % 2, :], ps[0:w, 4 + j % 2, :], ACT.Gelu,
                                         bias=vec[0:w, 6 + m:7 + m]).then_inc(z["gelu_ready"], 1)

                act.wait_ge(z["wf_in"], (g + 1) * WF)
                shift(0)
                shift(1)
                norm_square(nc, z, act, fb, q1, 0)
                for n in range(G):
                    gelu(n, 0)
                    if n + 1 < G:
                        norm_square(nc, z, act, fb, q1 + n + 1, n + 1)
                    gelu(n, 1)
                    gelu(n, 2)
                    if n + 2 < G:
                        shift(n + 2)

        @block.vector
        def _(dve):
            with dve.Fori(0, DEPTH) as L:
                def slot(s, pair, part):
                    live, had, done = clock(L, s, pair, part)
                    if live(0):
                        dve.wait_ge(z["squared"], done(0))
                        if had(0, 2):
                            dve.wait_ge(z["clamped"], done(0, 2))
                        nc.vector.tensor_reduce(ss[:, s % 2], sq[:, s % 2].rearrange("p (h d) -> p h d", d=DH), X, ALU.add).then_inc(z["summed"], 1)
                    if live(LAG_S):
                        n = (s - LAG_S) % 8
                        dve.wait_ge(z["s_ready"], done(LAG_S))
                        if had(LAG_S, 2):
                            dve.wait_ge(z["centred"], done(LAG_S, 2))
                        m = mx[:, n % 2].rearrange("p (r b) -> p b r", b=2)
                        nc.vector.tensor_reduce(m, scores, X, ALU.max).then_inc(z["maxed"], 1)
                    if live(0):
                        dve.wait_ge(z["summed"], done(0))
                        if had(0, 2):
                            dve.wait_ge(z["inv_ready"], done(0, 2))
                        nc.vector.tensor_scalar(ssm[:, s % 2], ss[:, s % 2], 1e-24, None, ALU.max).then_inc(z["clamped"], 1)
                    if live(LAG_S):
                        dve.wait_ge(z["maxed"], done(LAG_S))
                        if had(LAG_S, 2):
                            dve.wait_ge(z["exped"], done(LAG_S, 2))
                        nc.vector.tensor_tensor(by_bank(cen[:, n % 2]), scores, m.unsqueeze(3).to_broadcast([P, 2, 2, KEYS]),
                                                ALU.subtract).then_inc(z["centred"], 1)
                    if live(0):
                        dve.wait_ge(z["inv_ready"], done(0))
                        if had(0, 2):
                            dve.wait_ge(z["t1_ready"], done(0, 2))
                            dve.wait_ge(z["t2_ready"], 2 * done(0, 2))
                        ib = inv[:, s % 2].unsqueeze(2).to_broadcast([P, 2 * HU, DH])
                        nc.vector.tensor_tensor(qn[:, s % 2].rearrange("p (h d) -> p h d", d=DH),
                                                ps[:, s % 2].rearrange("p (h d) -> p h d", d=DH), ib, ALU.mult).then_inc(z["normed"], 1)
                    if live(0) and s % UT == 1:
                        if had(0, 2):
                            dve.wait_ge(z["v_ready"], done(0, 2))
                        shifted(pair * 2 + (s // UT + 1), (s // UT + 1) % 2)
                    yt = live(LAG_Y) and (s - LAG_Y) % UT == UT - 1
                    if live(LAG_O):
                        n = (s - LAG_O) % 8
                        dve.wait_ge(z["o_ready"], done(LAG_O))
                        if had(LAG_O, 2):
                            dve.wait_ge(z["o_normed"], done(LAG_O, 2))
                        o = ps[:, 7, 0:HU * AW].rearrange("p (h d) -> p h d", d=AW)
                        nc.vector.reciprocal(rec[:, n % 2], o[:, :, DH]).then_inc(z["recip_ready"], 1)
                        dve.wait_ge(z["recip_ready"], done(LAG_O))
                        if had(LAG_O, 2):
                            dve.wait_ge(z["ot_ready"], done(LAG_O, 2))
                        nc.vector.tensor_tensor(on[:, n % 2].rearrange("p (h d) -> p h d", d=DH), o[:, :, 0:DH],
                                                rec[:, n % 2].unsqueeze(2).to_broadcast([P, HU, DH]), ALU.mult).then_inc(z["o_normed"], 1)
                    if yt:
                        dve.wait_ge(z["y_ready"], tiles_out(L, s, pair))
                        tile = pair * 2 + (s - LAG_Y - (UT - 1)) // UT
                        cols = bass.ds(tile * P + 1, P)
                        nc.vector.tensor_tensor(x_b[:, cols], ps[:, 7, 384:512], x_a[:, cols], ALU.add).then_inc(z["x_b_ready"], 1)
                    if live(0):
                        par, hf = s // UT, DH // 2
                        dve.wait_ge(z["normed"], done(0))
                        dve.wait_ge(z["tab_ready"], 2 * tile_no(L, s, pair))
                        if had(0, 2):
                            dve.wait_ge(z["rotated"], done(0, 2))
                        a, b = heads_qk(t2[:, s % 2]), heads_qk(qn[:, s % 2])
                        for lo, hi in ((0, hf), (hf, 0)):
                            sn = tab_s[:, par, :, lo:lo + hf].unsqueeze(2).to_broadcast([P, 2, HU, hf])
                            nc.vector.tensor_tensor(a[:, :, :, lo:lo + hf], b[:, :, :, hi:hi + hf], sn, ALU.mult).then_inc(z["t2_ready"], 1)
                def shifted(tile, par):
                    nc.vector.tensor_copy(xs[0:64, par, :], x_a[0:64, bass.ds(tile * P + 1, P)]).then_inc(z["xs_ready"], 1)
                    nc.vector.tensor_copy(xs[64:P, par, :], x_a[64:P, bass.ds(tile * P, P)]).then_inc(z["xs_ready"], 1)
                dve.wait_ge(z["x_a_ready"], (L + L0) * G + 1)
                dve.wait_ge(z["ln_scaled"], q0 + L * G)
                shifted(0, 0)
                slots(dve, slot)

                g = L + L0
                q1 = q0 + L * G

                def affine(n):
                    dve.wait_ge(z["rstd_ready"], q1 + (n + 1))
                    if n >= 1:
                        dve.wait_ge(z["ln_ready"], g * G + n)
                    nc.vector.scalar_tensor_tensor(fsc[:, :], fb.xc(n), vec[:, 0:1], fb.V, ALU.mult, ALU.mult).then_inc(z["ln_scaled"], 1)
                    dve.wait_ge(z["ln_scaled"], q1 + (n + 1))
                    if n >= 2:
                        dve.wait_ge(z["up_ready"], g * 3 * G + 3 * (n - 1))
                    nc.vector.tensor_scalar(f2["xn"][:, n % 2, :], fsc[:, :], vec[:, 1:2], None, ALU.add).then_inc(z["ln_ready"], 1)

                def prod(n, m):
                    j = 3 * n + m
                    w = CH[m][1]
                    dve.wait_ge(z["gelu_ready"], g * 3 * G + (j + 1))
                    if j >= 4:
                        dve.wait_ge(z["down_ready"], g * 3 * G + (j - 3))
                    nc.vector.scalar_tensor_tensor(hm[0:w, j % 4, :], ps[0:w, 2 + j % 2, :], vec[0:w, 3 + m:4 + m],
                                                   f2["gl"][0:w, j % 2, :], ALU.add, ALU.mult).then_inc(z["prod_ready"], 1)

                def shift(n):
                    dve.wait_ge(z["x_b_ready"], g * TILES + 4 * (n + 1))
                    if n >= 2:
                        dve.wait_ge(z["ln_centred"], q1 + (n - 1))
                    nc.vector.tensor_copy(f2["src"][64:P, n % 2, :], x_b[64:P, n * GT:(n + 1) * GT]).then_inc(z["sh_hi"], 1)

                dve.wait_ge(z["wf_in"], (g + 1) * WF)
                shift(0)
                shift(1)
                norm_centre(nc, z, dve, fb, q1, 0)
                norm_eps(nc, z, dve, fb, q1, 0)
                norm_diagonal(nc, z, dve, fb, ident, q1, 0)
                affine(0)
                for n in range(G):
                    prod(n, 0)
                    if n + 1 < G:
                        norm_centre(nc, z, dve, fb, q1 + n + 1, n + 1)
                    prod(n, 1)
                    if n + 1 < G:
                        norm_eps(nc, z, dve, fb, q1 + n + 1, n + 1)
                    prod(n, 2)
                    if n + 1 < G:
                        norm_diagonal(nc, z, dve, fb, ident, q1 + n + 1, n + 1)
                        affine(n + 1)
                    if n + 2 < G:
                        shift(n + 2)
                    dve.wait_ge(z["down_ready"], g * 3 * G + 3 * (n + 1))
                    cols = slice(1 + n * GT, 1 + (n + 1) * GT)
                    nc.vector.scalar_tensor_tensor(x_a[:, cols], ps[:, 6 + n % 2, :], vec[:, 2:3], x_b[:, cols],
                                                   ALU.add, ALU.add).then_inc(z["x_a_ready"], 1)


def copy_on_pool(nc, dst, src, zeros):
    return nc.gpsimd.tensor_tensor(dst, src, zeros, ALU.add)


def mix(nc, z, k, x_res, x_a):
    with nc.Block() as block:
        @block.vector
        def _(dve):
            nc.vector.scalar_tensor_tensor(x_res[:, :], x_a[:, 1:1 + T], 0.5, x_res[:, :], ALU.mult, ALU.add).then_inc(z["mixed"], 1)


def store_output(nc, z, out_dram, x_res, ident):
    with ExitStack() as st:
        o_tok = st.enter_context(nc.sbuf_tensor("o_tok", [P, TILES, P], F32))
        tp = st.enter_context(nc.psum_tensor("turned_out", [P, 2, GT], F32))
        block = st.enter_context(nc.Block())

        @block.tensor
        def _(pe):
            for n in range(G):
                if n >= 2:
                    pe.wait_ge(z["out_ready"], n - 1)
                for m in range(4):
                    t = 4 * n + m
                    mm = pe.transpose(tp[:, n % 2, m * P:(m + 1) * P], x_res[:, t * P:(t + 1) * P], ident[:, :])
                mm.then_inc(z["out_t_ready"], 1)

        @block.vector
        def _(dve):
            for n in range(G):
                dve.wait_ge(z["out_t_ready"], n + 1)
                nc.vector.tensor_copy(o_tok[:, 4 * n:4 * n + 4, :].rearrange("p a d -> p (a d)"), tp[:, n % 2, :]).then_inc(z["out_ready"], 1)

        @block.sync
        def _(sp):
            for n in range(G):
                sp.wait_ge(z["out_ready"], n + 1)
                sp.dma_start(out_dram[:, 4 * n:4 * n + 4, :], o_tok[:, 4 * n:4 * n + 4, :]).then_inc(z["stored"], 16)
            sp.wait_ge(z["stored"], 16 * G)


def latent_attention(nc, z, i, c, x_res, x_a, ident, ident_h, causal, ones_w, neg_half, zeros):
    VW = CD + 1
    with ExitStack() as st:
        def sb(name, shape, dt=F32):
            return st.enter_context(nc.sbuf_tensor(name, shape, dt))

        wl_kv = sb("wl_kv", [P, KR])
        wl_q = sb("wl_q", [P, QR])
        g_kv = sb("g_kv", [KR, 1])
        wl_v = sb("wl_v", [KR, P])
        wl_o = sb("wl_o", [P, P])
        wa = {"q": sb("wa_q", [QR, HEADS, 64]), "qr": sb("wa_qr", [QR, HEADS, 64]),
              "k": sb("wa_k", [P, HEADS, 64]), "kr": sb("wa_kr", [P, HEADS, 64]), "kc": sb("wa_kc", [KR, HEADS, 64])}
        ws = {n: sb("ws_" + n, [t.shape[0], 2, 64]) for n, t in wa.items()}
        mean_kv = sb("mean_kv", [KR, KR])
        kvc = sb("kvc", [KR, T])
        qc = sb("qc", [QR, T])
        lsq = sb("lsq", [KR, GT])
        lms = sb("lms", [P, GT // P])
        lrs = sb("lrs", [P, GT // P])
        lrb = sb("lrb", [KR, GT])
        ldg = sb("ldg", [P, GT // P, P])
        ac = sb("ac", [P, T])
        as_ = sb("as_", [P, T])
        qm = [sb("qm0", [P, T]), sb("qm1", [P, T])]
        kT = sb("kT", [P, T])
        ra = sb("ra", [P, 2, GT])
        rb = sb("rb", [P, 2, GT])
        vall = sb("vall", [P, TILES, HEADS, VW])
        vp = sb("vp", [P, 2, TILES, 32])
        sel = sb("sel", [P, VW])
        prow = sb("prow", [P, 2, T])
        ptl = sb("ptl", [P, 4, GT])
        rpm = sb("rpm", [P, 2, 4])
        osb = sb("osb", [P, 2, P])
        rmx = sb("rmx", [P, 2])
        rng = sb("rng", [P, 2])
        lrec = sb("lrec", [P, 2])
        oall = sb("oall", [P, TILES, P])
        lot = sb("lot", [P, 2, GT])
        ps = st.enter_context(nc.psum_tensor("ps_l", [P, 8, 512], F32))
        scale = 1.0 / float(np.sqrt(np.float32(QD)))

        WL = 16 * (7 + 8)
        WZ = 10
        WS = len(wa) + 2

        block = st.enter_context(nc.Block())
        rows = [(h, r) for h in range(2) for r in range(TILES)]
        items = [(w, n) for w in ("q", "k") for n in range(G)]
        quads = [(x, m) for x, (h, r) in enumerate(rows) for m in range(r // 4 + 1)]
        NQ = len(quads)
        quad_no = {q: y for y, q in enumerate(quads)}

        def row_ended(y):
            return quads[y][0] if 0 <= y < NQ and quads[y][1] == rows[quads[y][0]][1] // 4 else None

        def scores_at(y):
            x, m = quads[y]
            before = [(x + 1, m)] if (x + 1, m) in quad_no else []
            after = [(x + 1, m + 1)] if row_ended(y) is not None and (x + 1, m + 1) in quad_no else []
            return before, after

        @block.sync
        def _(sp):
            sp.dma_start(wl_kv[:, :], i["L0_attn_W_kv"]).then_inc(z["wl_in"], 16)
            sp.dma_start(wl_q[:, :], i["L0_attn_W_q"]).then_inc(z["wl_in"], 16)
            with nc.allow_non_contiguous_dma(reason="a vector onto partitions"):
                sp.dma_start(g_kv[:, :], i["L0_attn_g_kv"].rearrange("(p a) -> p a", a=1)).then_inc(z["wl_in"], 16)
            sp.dma_start(wl_v[:, :], i["L0_attn_W_vdec"]).then_inc(z["wl_in"], 16)
            sp.dma_start(wl_o[:, :], i["L0_attn_W_o"]).then_inc(z["wl_in"], 16)
            sp.dma_start(ac[:, :], c["ac"]).then_inc(z["wl_in"], 16)
            sp.dma_start(as_[:, :], c["as_"]).then_inc(z["wl_in"], 16)
            sp.wait_ge(z["wl_zero"], WZ)
            hf = RD // 2
            for n, name in (("q", "L0_attn_W_qrope"), ("k", "L0_attn_W_krope")):
                src = i[name].rearrange("p (h d) -> p h d", h=HEADS)
                sp.dma_start(wa[n][:, :, 0:RD], src).then_inc(z["wl_in"], 16)
                sp.dma_start(wa[n + "r"][:, :, 0:hf], src[:, :, hf:RD]).then_inc(z["wl_in"], 16)
                sp.dma_start(wa[n + "r"][:, :, hf:RD], src[:, :, 0:hf]).then_inc(z["wl_in"], 16)
            for n, name in (("q", "L0_attn_W_qdec"), ("kc", "L0_attn_W_kdec")):
                src = i[name].rearrange("p (h d) -> p h d", h=HEADS)
                sp.dma_start(wa[n][:, :, RD:QD], src).then_inc(z["wl_in"], 16)


        @block.gpsimd
        def _(pool):
            for n, t in enumerate(wa.values()):
                nc.gpsimd.memset(t[:, :, :], 0.0).then_inc(z["wl_zero"], 1)
                pool.wait_ge(z["wl_zero"], n + 1)
            nc.gpsimd.memset(mean_kv[:, :], 1.0 / KR).then_inc(z["wl_zero"], 1)
            pool.wait_ge(z["wl_zero"], 6)
            nc.gpsimd.memset(vall[:, :, :, :], 1.0).then_inc(z["wl_zero"], 1)
            pool.wait_ge(z["wl_zero"], 7)
            for n, t in enumerate((vp[:, :, :, :], qm[0][:, :], qm[1][:, :])):
                nc.gpsimd.memset(t, 0.0).then_inc(z["wl_zero"], 1)
                pool.wait_ge(z["wl_zero"], 8 + n)
            for n in range(G):
                pool.wait_ge(z["lat_mse"], n + 1)
                if n >= 1:
                    pool.wait_ge(z["lat_diag"], n)
                nc.gpsimd.tensor_tensor(lrs[:, :], lms[:, :], neg_half[:, 0:GT // P], ALU.pow).then_inc(z["lat_pow"], 1)
            pool.wait_ge(z["wl_in"], WL)
            pool.wait_ge(z["lat_pow"], G)
            pool.wait_ge(z["v_copied"], G)
            with pool.Fori(0, PAIRS) as pair:
                pool.wait_ge(z["ol_normed"], pair * len(rows) + 1)
                for m, n in enumerate(wa):
                    copy_on_pool(nc, ws[n][:, :, :], wa[n][:, bass.ds(pair * 2, 2), :],
                                 zeros[0:wa[n].shape[0], 0:P].rearrange("p (h d) -> p h d", h=2)).then_inc(z["wl_slots"], 1)
                    pool.wait_ge(z["wl_slots"], pair * WS + (m + 1))
                for h in range(2):
                    nc.gpsimd.tensor_tensor(vp[:, h, :, 0:VW], vall[:, :, bass.ds(pair * 2 + h, 1), :].rearrange("p t a d -> p t (a d)"),
                                            zeros[:, 0:VW].unsqueeze(1).to_broadcast([P, TILES, VW]), ALU.add).then_inc(z["wl_slots"], 1)
                for j, (w, n) in enumerate(items):
                    if w == "k":
                        pool.wait_ge(z["ra_ready"], pair * len(items) + (j + 1))
                        pool.wait_ge(z["rb_ready"], pair * len(items) + (j + 1))
                        nc.gpsimd.tensor_tensor(kT[:, n * GT:(n + 1) * GT], ra[:, j % 2, :], rb[:, j % 2, :], ALU.add).then_inc(z["rope_ready"], 1)

        @block.tensor
        def _(pe):
            pe.wait_ge(z["wl_in"], WL)
            pe.wait_ge(z["wl_zero"], WZ)
            for n in range(G):
                cols = slice(1 + n * GT, 1 + (n + 1) * GT)
                if n >= 1:
                    pe.wait_ge(z["lat_kv"], n)
                    pe.wait_ge(z["lat_q"], n)
                pe.matmul(ps[0:KR, 0, :], wl_kv[:, :], x_a[:, cols], start=True, stop=True)
                pe.matmul(ps[0:QR, 1, :], wl_q[:, :], x_a[:, cols], start=True, stop=True).then_inc(z["lat_ready"], 1)
                pe.wait_ge(z["lat_sq"], n + 1)
                if n >= 1:
                    pe.wait_ge(z["lat_mse"], n)
                    pe.wait_ge(z["lat_kv"], n)
                for m in range(GT // P):
                    mm = pe.matmul(ps[:, 2, m:m + 1], lsq[:, m * P:(m + 1) * P], mean_kv[:, 0:1], start=True, stop=True)
                mm.then_inc(z["lat_ms"], 1)
                pe.wait_ge(z["lat_diag"], n + 1)
                pe.matmul(ps[0:KR, 2, :], ones_w[:, 0:KR], ldg[:, :, :], start=True, stop=True).then_inc(z["lat_rs"], 1)
            for n in range(G):
                pe.wait_ge(z["lat_kv"], n + 1)
                if n >= 2:
                    pe.wait_ge(z["v_copied"], n - 1)
                for m in range(4):
                    t = 4 * n + m
                    mm = pe.matmul(ps[:, 4 + n % 2, m * P:(m + 1) * P], kvc[:, t * P:(t + 1) * P], wl_v[:, :], start=True, stop=True)
                mm.then_inc(z["v_mm"], 1)
            pe.wait_ge(z["v_copied"], G)
            pe.wait_ge(z["sel_ready"], 1)
            with pe.Fori(0, PAIRS) as pair:
                pe.wait_ge(z["wl_slots"], (pair + 1) * WS)
                pe.wait_ge(z["ol_normed"], pair * len(rows) + 1)
                for j, (w, n) in enumerate(items):
                    if j >= 2:
                        pe.wait_ge(z["ra_ready"], pair * len(items) + (j - 1))
                        pe.wait_ge(z["rb_ready"], pair * len(items) + (j - 1))
                    cols = slice(1 + n * GT, 1 + (n + 1) * GT)
                    a, b = ps[:, j % 2, :], ps[:, 2 + j % 2, :]
                    flat = lambda t: t[:, :, :].rearrange("p h d -> p (h d)")
                    if w == "q":
                        pe.matmul(a, flat(ws["q"]), qc[:, n * GT:(n + 1) * GT], start=True, stop=True)
                        mm = pe.matmul(b, flat(ws["qr"]), qc[:, n * GT:(n + 1) * GT], start=True, stop=True)
                    else:
                        pe.matmul(a, flat(ws["k"]), x_a[:, cols], start=True, stop=False)
                        pe.matmul(a, flat(ws["kc"]), kvc[:, n * GT:(n + 1) * GT], start=False, stop=True)
                        mm = pe.matmul(b, flat(ws["kr"]), x_a[:, cols], start=True, stop=True)
                    mm.then_inc(z["ab_ready"], 1)

                def scores(x, m):
                    h, r = rows[x]
                    last = max([p for p in range(x) if (p, m) in quad_no], default=None)
                    if last is None:
                        pe.wait_ge(z["q_roped"], (pair + 1) * 2 * G)
                        pe.wait_ge(z["rope_ready"], (pair + 1) * G)
                    else:
                        pe.wait_ge(z["row_exp"], pair * NQ + (quad_no[last, m] + 1))
                    w = min(GT, (r + 1) * P - m * GT)
                    end = m == r // 4
                    mm = pe.matmul(ps[:, m, 0:w], qm[h][:, r * P:(r + 1) * P], kT[:, m * GT:m * GT + w],
                                   start=True, stop=not end, skip_group_check=True)
                    if end:
                        mm = pe.matmul(ps[:, m, w - P:w], ident_h[:, :], causal[:, :], start=False, stop=True, skip_group_check=True)
                    mm.then_inc(z["sc_ready"], 1)

                def turn(y):
                    x, m = quads[y]
                    r = rows[x][1]
                    pe.wait_ge(z["row_exp"], pair * NQ + (y + 1))
                    if y >= 2:
                        pe.wait_ge(z["ptl_odd" if y % 2 else "ptl_even"], pair * (NQ // 2) + y // 2)
                    for t in range(4 * m, min(4 * m + 4, r + 1)):
                        mm = pe.transpose(ps[:, 4 + y % 2, (t % 4) * P:(t % 4 + 1) * P], prow[:, x % 2, t * P:(t + 1) * P], ident[:, :])
                    mm.then_inc(z["ptl_ready"], 1)

                def out(y):
                    x, m = quads[y]
                    h, r = rows[x]
                    pe.wait_ge(z["ptl_odd" if y % 2 else "ptl_even"], pair * (NQ // 2) + (y // 2 + 1))
                    if m == 0 and x >= 2:
                        pe.wait_ge(z["ol_normed"], pair * len(rows) + x)
                    for t in range(4 * m, min(4 * m + 4, r + 1)):
                        j = t % 4
                        mm = pe.matmul(ps[32 * j:32 * (j + 1), 6 + x % 2, 0:P], vp[:, h, t, :], ptl[:, y % 4, j * P:(j + 1) * P],
                                       start=(t < 4), stop=(t + 4 > r), skip_group_check=True)
                    mm.then_inc(z["pv_part"], 1)

                def strips_sum(x):
                    w = 32 * min(4, rows[x][1] + 1)
                    pe.wait_ge(z["ol_copied"], pair * len(rows) + (x + 1))
                    pe.matmul(ps[:, 6 + x % 2, 2 * P:2 * P + VW], osb[0:w, x % 2, :], sel[0:w, :], start=True, stop=True,
                              skip_group_check=True).then_inc(z["ol_summed"], 1)

                scores(0, 0)
                for y in range(NQ + 3):
                    if y < NQ:
                        before, after = scores_at(y)
                        for q in before:
                            scores(*q)
                        turn(y)
                        for q in after:
                            scores(*q)
                    if 0 <= y - 2 < NQ:
                        out(y - 2)
                    if row_ended(y - 3) is not None:
                        strips_sum(row_ended(y - 3))

            for n in range(G):
                pe.wait_ge(z["ol_normed"], PAIRS * len(rows) + 1)
                if n >= 2:
                    pe.wait_ge(z["lo_copied"], n - 1)
                for m in range(4):
                    mm = pe.transpose(ps[:, n % 2, m * P:(m + 1) * P], oall[:, 4 * n + m, :], ident[:, :])
                mm.then_inc(z["lo_tr"], 1)
                pe.wait_ge(z["lo_copied"], n + 1)
                if n >= 2:
                    pe.wait_ge(z["lo_added"], n - 1)
                pe.matmul(ps[:, 2 + n % 2, :], wl_o[:, :], lot[:, n % 2, :], start=True, stop=True).then_inc(z["lo_mm"], 1)

        @block.scalar
        def _(act):
            for n in range(G):
                act.wait_ge(z["lat_ready"], n + 1)
                if n >= 1:
                    act.wait_ge(z["lat_ms"], n)
                nc.scalar.activation(lsq[:, :], ps[0:KR, 0, :], ACT.Square).then_inc(z["lat_sq"], 1)
                nc.scalar.copy(qc[:, n * GT:(n + 1) * GT], ps[0:QR, 1, :]).then_inc(z["lat_q"], 1)
            with act.Fori(0, PAIRS) as pair:
                def exps(x, m):
                    y = quad_no[x, m]
                    act.wait_ge(z["row_neg"], pair * len(rows) + (x + 1))
                    act.wait_ge(z["sc_ready"], pair * NQ + (y + 1))
                    if (x - 2, m) in quad_no:
                        act.wait_ge(z["ptl_ready"], pair * NQ + (quad_no[x - 2, m] + 1))
                    w = min(GT, (rows[x][1] + 1) * P - m * GT)
                    nc.scalar.activation(prow[:, x % 2, m * GT:m * GT + w], ps[:, m, 0:w],
                                         ACT.Exp, bias=rng[:, x % 2:x % 2 + 1], scale=scale).then_inc(z["row_exp"], 1)

                def turned(y):
                    x, m = quads[y]
                    w = min(GT, (rows[x][1] + 1) * P - m * GT)
                    act.wait_ge(z["ptl_ready"], pair * NQ + (y + 1))
                    if y >= 4:
                        act.wait_ge(z["pv_part"], pair * NQ + (y - 3))
                    nc.scalar.copy(ptl[:, y % 4, 0:w], ps[:, 4 + y % 2, 0:w]).then_inc(z["ptl_even"], 1)

                for x in range(len(rows)):
                    exps(x, 0)
                    if (x, 1) in quad_no:
                        exps(x, 1)
                    for m in range(4):
                        if (x, m) in quad_no and quad_no[x, m] % 2 == 0:
                            turned(quad_no[x, m])
                        if (x, m + 2) in quad_no:
                            exps(x, m + 2)

        @block.vector
        def _(dve):
            for n in range(G):
                cols = slice(n * GT, (n + 1) * GT)
                dve.wait_ge(z["lat_ms"], n + 1)
                if n >= 1:
                    dve.wait_ge(z["lat_pow"], n)
                nc.vector.tensor_scalar(lms[:, :], ps[:, 2, 0:GT // P], RMS_EPS, None, ALU.add).then_inc(z["lat_mse"], 1)
                dve.wait_ge(z["lat_pow"], n + 1)
                if n >= 1:
                    dve.wait_ge(z["lat_rs"], n)
                nc.vector.tensor_tensor(ldg[:, :, :], ident[:, :].unsqueeze(1).to_broadcast([P, GT // P, P]),
                                        lrs[:, :].unsqueeze(2).to_broadcast([P, GT // P, P]), ALU.mult).then_inc(z["lat_diag"], 1)
                dve.wait_ge(z["lat_rs"], n + 1)
                dve.wait_ge(z["lat_q"], n + 1)
                nc.vector.tensor_copy(lrb[:, :], ps[0:KR, 2, :]).then_inc(z["lat_spread"], 1)
                dve.wait_ge(z["lat_spread"], n + 1)
                nc.vector.scalar_tensor_tensor(kvc[:, cols], ps[0:KR, 0, :], g_kv[:, 0:1], lrb[:, :], ALU.mult, ALU.mult).then_inc(z["lat_kv"], 1)
            for n in range(G):
                dve.wait_ge(z["v_mm"], n + 1)
                nc.vector.tensor_copy(vall[:, 4 * n:4 * n + 4, :, 0:CD],
                                      ps[:, 4 + n % 2, :].rearrange("p (t h d) -> p t h d", t=4, h=HEADS)).then_inc(z["v_copied"], 1)
            nc.vector.tensor_reduce(sel[:, :], ident[:, :].rearrange("p (j c) -> p c j", j=4)[:, 0:VW, :], X, ALU.add).then_inc(z["sel_ready"], 1)
            nc.vector.memset(lrec[:, :], 0.0).then_inc(z["ol_normed"], 1)
            with dve.Fori(0, PAIRS) as pair:
                for j, (w, n) in enumerate(items):
                    cols = slice(n * GT, (n + 1) * GT)
                    dve.wait_ge(z["ab_ready"], pair * len(items) + (j + 1))
                    if 2 <= j < G + 2:
                        dve.wait_ge(z["q_roped"], pair * 2 * G + 2 * (j - 1))
                    elif j >= G + 2:
                        dve.wait_ge(z["rope_ready"], pair * G + (j - G - 1))
                    nc.vector.tensor_tensor(ra[:, j % 2, :], ps[:, j % 2, :], ac[:, cols], ALU.mult).then_inc(z["ra_ready"], 1)
                    nc.vector.tensor_tensor(rb[:, j % 2, :], ps[:, 2 + j % 2, :], as_[:, cols], ALU.mult).then_inc(z["rb_ready"], 1)
                    if w == "q":
                        dve.wait_ge(z["ra_ready"], pair * len(items) + (j + 1))
                        dve.wait_ge(z["rb_ready"], pair * len(items) + (j + 1))
                        for h in range(2):
                            hp = slice(64 * h, 64 * h + 64)
                            nc.vector.tensor_tensor(qm[h][hp, cols], ra[hp, j % 2, :], rb[hp, j % 2, :], ALU.add).then_inc(z["q_roped"], 1)

                def part_max(x, m):
                    w = min(GT, (rows[x][1] + 1) * P - m * GT)
                    dve.wait_ge(z["sc_ready"], pair * NQ + (quad_no[x, m] + 1))
                    if m == 0 and x >= 2:
                        dve.wait_ge(z["row_top"], pair * len(rows) + (x - 1))
                    nc.vector.tensor_reduce(rpm[:, x % 2, m:m + 1], ps[:, m, 0:w], X, ALU.max).then_inc(z["row_max"], 1)

                def top(x):
                    nq = rows[x][1] // 4 + 1
                    dve.wait_ge(z["row_max"], pair * NQ + (quad_no[x, nq - 1] + 1))
                    if x >= 2:
                        dve.wait_ge(z["row_neg"], pair * len(rows) + (x - 1))
                    nc.vector.tensor_reduce(rmx[:, x % 2:x % 2 + 1], rpm[:, x % 2, 0:nq], X, ALU.max).then_inc(z["row_top"], 1)
                    dve.wait_ge(z["row_top"], pair * len(rows) + (x + 1))
                    if x >= 2:
                        y = quad_no[x - 2, rows[x - 2][1] // 4]
                        dve.wait_ge(z["row_exp"], pair * NQ + (y + 1))
                    nc.vector.tensor_scalar(rng[:, x % 2:x % 2 + 1], rmx[:, x % 2:x % 2 + 1], -scale, None, ALU.mult).then_inc(z["row_neg"], 1)

                def maxima(x, m):
                    part_max(x, m)
                    if m == rows[x][1] // 4:
                        top(x)

                def turned(y):
                    x, m = quads[y]
                    w = min(GT, (rows[x][1] + 1) * P - m * GT)
                    dve.wait_ge(z["ptl_ready"], pair * NQ + (y + 1))
                    if y >= 4:
                        dve.wait_ge(z["pv_part"], pair * NQ + (y - 3))
                    nc.vector.tensor_copy(ptl[:, y % 4, 0:w], ps[:, 4 + y % 2, 0:w]).then_inc(z["ptl_odd"], 1)

                def outputs(x):
                    w = 32 * min(4, rows[x][1] + 1)
                    dve.wait_ge(z["pv_part"], pair * NQ + (quad_no[x, rows[x][1] // 4] + 1))
                    if x >= 2:
                        dve.wait_ge(z["ol_summed"], pair * len(rows) + (x - 1))
                    nc.vector.tensor_copy(osb[0:w, x % 2, :], ps[0:w, 6 + x % 2, 0:P]).then_inc(z["ol_copied"], 1)

                def norm(x):
                    h, r = rows[x]
                    s0 = 2 * P
                    dve.wait_ge(z["ol_summed"], pair * len(rows) + (x + 1))
                    dve.wait_ge(z["ol_normed"], pair * len(rows) + max(x, 1))
                    nc.vector.reciprocal(lrec[:, x % 2:x % 2 + 1], ps[:, 6 + x % 2, s0 + CD:s0 + VW]).then_inc(z["ol_rec"], 1)
                    dve.wait_ge(z["ol_rec"], pair * len(rows) + (x + 1))
                    nc.vector.tensor_scalar(oall[:, r, bass.ds(pair * 2 * CD + h * CD, CD)], ps[:, 6 + x % 2, s0:s0 + CD],
                                            lrec[:, x % 2:x % 2 + 1], None, ALU.mult).then_inc(z["ol_normed"], 1)

                maxima(0, 0)
                for y in range(NQ + 3):
                    if y < NQ:
                        before, after = scores_at(y)
                        for q in before:
                            maxima(*q)
                        if y % 2:
                            turned(y)
                        for q in after:
                            maxima(*q)
                    if row_ended(y - 2) is not None:
                        outputs(row_ended(y - 2))
                    if row_ended(y - 3) is not None:
                        norm(row_ended(y - 3))

            for n in range(G):
                cols = slice(n * GT, (n + 1) * GT)
                dve.wait_ge(z["lo_tr"], n + 1)
                nc.vector.tensor_copy(lot[:, n % 2, :], ps[:, n % 2, :]).then_inc(z["lo_copied"], 1)
                dve.wait_ge(z["lo_mm"], n + 1)
                nc.vector.tensor_tensor(x_res[:, cols], ps[:, 2 + n % 2, :], x_res[:, cols], ALU.add).then_inc(z["lo_added"], 1)


_INS = ["L0_attn_x", "L0_attn_W_kv", "L0_attn_g_kv", "L0_attn_W_kdec", "L0_attn_W_vdec", "L0_attn_W_q", "L0_attn_W_qdec",
        "L0_attn_W_krope", "L0_attn_W_qrope", "L0_attn_W_o", "L0_ffn_Wqkv", "L0_ffn_q_scale", "L0_ffn_k_scale", "L0_ffn_Wo",
        "L0_ffn_ln_g", "L0_ffn_ln_b", "L0_ffn_W1", "L0_ffn_b1", "L0_ffn_W2", "L0_ffn_b2"]


def kernel(**inputs):
    import concourse.bacc as _bacc
    from concourse.bass_utils import run_bass_kernel_spmd as _run

    nc = _bacc.Bacc("TRN2", target_bir_lowering=False, num_devices=1)
    arrays, ins, consts = {}, {}, {}
    for name in _INS:
        a = np.ascontiguousarray(inputs[name])
        arrays[f"in_{name}"] = a
        ins[name] = nc.dram_tensor(f"in_{name}", a.shape, mybir.dt.from_np(a.dtype), kind="ExternalInput").ap()
    for name, a in tables().items():
        arrays[f"const_{name}"] = a
        consts[name] = nc.dram_tensor(f"const_{name}", a.shape, F32, kind="ExternalInput").ap()
    out = nc.dram_tensor("out_0", (1, T, P), F32, kind="ExternalOutput").ap()
    macaron_kernel(nc, ins, consts, out)
    r = _run(nc, [arrays], core_ids=[0])
    return r.results[0]["out_0"]
```

```python
from contextlib import ExitStack

import numpy as np

import concourse.bass as bass
from concourse import mybir


class NormBuffers:

    def __init__(self, M, V, src, xc, sq, ve, rs, dg):
        self.M, self.V, self.src, self.xc, self.sq, self.ve, self.rs, self.dg = M, V, src, xc, sq, ve, rs, dg


ALU = mybir.AluOpType
ACT = mybir.ActivationFunctionType
F32 = mybir.dt.float32
BF16 = mybir.dt.bfloat16
X = mybir.AxisListType.X

P = 128
T = 2048
TILES = T // P
DEPTH = 6
HEADS = 16
DH = 64
WIN = 32
HU = 4
UT = HEADS // HU
UNITS = TILES * UT
KEYS = P + WIN
INNER = 341
CH = [(0, 128), (128, 128), (256, 85)]
G = 4
GT = T // G
NEG = -1.0e30
LN_EPS = 1e-5

QR, KR, CD, RD = 64, 32, 8, 32
QD = CD + RD
RMS_EPS = 1e-6
PAIRS = HEADS // 2

LAG_R, LAG_V, LAG_T, LAG_S, LAG_P, LAG_O, LAG_Y = 1, 1, 2, 3, 4, 5, 7

WA, WF = 16 * 8, 16 * 12

SEMAPHORES = (
    "const_in consts_ready x_in wa_in wf_in"
    " xs_ready tab_ready qk_ready squared summed clamped inv_ready normed t1_ready t2_ready rotated k_rotated"
    " tr_ready tr_read s_ready k_carried maxed negated exped recip_ready weighted pt_ready pt_copied pt_read v_ready vs_ready v_read"
    " o_ready v_carried ot_read y_ready x_b_ready"
    " sh_lo sh_hi mean_ready ln_centred ln_squared var_ready vare_ready pow_ready ln_diag rstd_ready ln_scaled ln_ready"
    " up_ready gelu_ready prod_ready down_ready x_a_ready"
    " xt_ready x_res_ready mixed out_t_ready out_ready stored"
    " wl_in wl_zero wl_slots lat_ready lat_sq lat_q lat_ms lat_mse lat_pow lat_diag lat_rs lat_spread lat_kv v_mm v_copied"
    " a_ready b_ready ra_ready rb_ready rope_ready"
    " q_roped sel_ready sc_ready row_max row_top row_neg row_exp ptl_ready ptl_even ptl_odd pv_part ol_copied ol_summed"
    " ol_rec ol_normed"
    " lo_tr lo_copied lo_mm lo_added"
)


def tables():
    f = np.float32
    half = np.arange(0, DH, 2, dtype=f)
    inv = (f(1.0) / (f(10000.0) ** (half / f(DH)))).astype(f)
    t = np.arange(T, dtype=f)
    fr = (t[:, None] * inv[None, :]).astype(f)
    fr = np.concatenate([fr, fr], -1)
    base = ((half + f(0.4 * DH)) / f(1.4 * DH)).astype(f)
    base = np.concatenate([base, base])
    local = (np.arange(T) % P - P // 2) / (WIN // 2)
    grow = base[None, :].astype(np.float64) ** local[:, None]
    cos, sin = np.cos(fr), np.sin(fr)
    sgn = np.concatenate([-np.ones(DH // 2), np.ones(DH // 2)])
    wc = np.stack([cos * grow, cos / grow], 1)
    ws = np.stack([sin * sgn * grow, sin * sgn / grow], 1)
    wc = wc.reshape(TILES, P, 2, DH).transpose(1, 0, 2, 3)
    ws = ws.reshape(TILES, P, 2, DH).transpose(1, 0, 2, 3)
    carry = (base.astype(np.float64) ** (P / (WIN // 2)))
    carry = np.concatenate([carry, carry])[:, None]
    i, j = np.arange(P)[:, None], np.arange(P)[None, :]
    main = np.where((j <= i) & (j >= i - WIN), 0.0, NEG)
    js = np.arange(WIN)[None, :]
    side = np.where((i < WIN) & (js >= i), 0.0, NEG)
    wmask = np.stack([np.concatenate([main, np.full((P, WIN), NEG)], 1),
                      np.concatenate([main, side], 1)], 1)
    causal = np.where(j <= i, 0.0, NEG)
    inv2 = (1.0 / 10000.0 ** (np.arange(0, RD, 2, dtype=f) / RD)).astype(f)
    fr2 = np.outer(t, inv2).astype(f)
    e2 = np.concatenate([fr2, fr2], -1)
    ac, as_ = np.zeros((P, T)), np.zeros((P, T))
    sg2 = np.concatenate([-np.ones(RD // 2), np.ones(RD // 2)])
    for h in range(2):
        ac[64 * h:64 * h + RD] = np.cos(e2).T
        ac[64 * h + RD:64 * h + QD] = 1.0
        as_[64 * h:64 * h + RD] = (np.sin(e2) * sg2).T
    out = dict(ident=np.eye(P), wc=wc, ws=ws, carry=carry, wmask=wmask, causal=causal, ac=ac, as_=as_)
    return {k: np.ascontiguousarray(v, dtype=f) for k, v in out.items()}



def macaron_kernel(nc, i, c, out):
    with ExitStack() as ctx:
        def sb(name, shape, dt=F32):
            return ctx.enter_context(nc.sbuf_tensor(name, shape, dt))

        z = {n: ctx.enter_context(nc.semaphore(n)) for n in SEMAPHORES.split()}
        x_res = sb("x_res", [P, T])
        x_a = sb("x_a", [P, 1 + T + P])
        x_b = sb("x_b", [P, 1 + T])
        ident = sb("ident", [P, P])
        ident_h = sb("ident_h", [P, P], BF16)
        wmask = sb("wmask", [P, 2, KEYS], BF16)
        causal = sb("causal", [P, P], BF16)
        carry_f = sb("carry_f", [P, 1])
        mean_w = sb("mean_w", [P, P])
        ones_w = sb("ones_w", [P, P])
        neg_half = sb("neg_half", [P, 2 * HU])
        zeros = sb("zeros", [P, P])
        x_dram = i["L0_attn_x"].rearrange("a (n p) d -> p (a n) d", p=P)
        out_dram = out.rearrange("a (n p) d -> p (a n) d", p=P)

        load_input(nc, z, c, x_dram, x_res, x_a, x_b, ident, ident_h, wmask, causal, carry_f, mean_w, ones_w, neg_half, zeros)
        outer_norm(nc, z, "na", 0, x_res, x_a, ident, mean_w, ones_w, neg_half)
        window_stack(nc, z, i, c, 0, G, x_a, x_b, ident, ident_h, wmask, carry_f, mean_w, ones_w, neg_half, zeros)
        mix(nc, z, 0, x_res, x_a)
        n1 = G + DEPTH * G
        outer_norm(nc, z, "nb", n1, x_res, x_a, ident, mean_w, ones_w, neg_half)
        latent_attention(nc, z, i, c, x_res, x_a, x_b, ident, ident_h, causal, ones_w, neg_half, zeros)
        outer_norm(nc, z, "nc", n1 + G, x_res, x_a, ident, mean_w, ones_w, neg_half)
        window_stack(nc, z, i, c, 1, n1 + 2 * G, x_a, x_b, ident, ident_h, wmask, carry_f, mean_w, ones_w, neg_half, zeros)
        mix(nc, z, 1, x_res, x_a)
        store_output(nc, z, out_dram, x_res, ident)


def load_input(nc, z, c, x_dram, x_res, x_a, x_b, ident, ident_h, wmask, causal, carry_f, mean_w, ones_w, neg_half, zeros):
    with ExitStack() as st:
        x_tok = st.enter_context(nc.sbuf_tensor("x_tok", [P, TILES, P], F32))
        wmask_f = st.enter_context(nc.sbuf_tensor("wmask_f", [P, 2, KEYS], F32))
        causal_f = st.enter_context(nc.sbuf_tensor("causal_f", [P, P], F32))
        tp = st.enter_context(nc.psum_tensor("turned_in", [P, 2, GT], F32))
        block = st.enter_context(nc.Block())

        @block.sync
        def _(sp):
            sp.dma_start(ident[:, :], c["ident"]).then_inc(z["const_in"], 16)
            for n in range(G):
                sp.dma_start(x_tok[:, 4 * n:4 * n + 4, :], x_dram[:, 4 * n:4 * n + 4, :]).then_inc(z["x_in"], 16)
            sp.dma_start(wmask_f[:, :, :], c["wmask"]).then_inc(z["const_in"], 16)
            sp.dma_start(causal_f[:, :], c["causal"]).then_inc(z["const_in"], 16)
            sp.dma_start(carry_f[:, :], c["carry"]).then_inc(z["const_in"], 16)

        @block.gpsimd
        def _(pool):
            nc.gpsimd.memset(mean_w[:, :], 1.0 / P).then_inc(z["consts_ready"], 1)
            nc.gpsimd.memset(neg_half[:, :], -0.5).then_inc(z["x_a_ready"], 1)
            nc.gpsimd.memset(ones_w[:, :], 1.0).then_inc(z["consts_ready"], 1)
            nc.gpsimd.memset(zeros[:, :], 0.0).then_inc(z["consts_ready"], 1)
            nc.gpsimd.memset(x_a[:, :], 0.0).then_inc(z["consts_ready"], 1)
            nc.gpsimd.memset(x_b[:, 0:1], 0.0).then_inc(z["consts_ready"], 1)

        @block.tensor
        def _(pe):
            pe.wait_ge(z["const_in"], 64)
            for n in range(G):
                pe.wait_ge(z["x_in"], 16 * G)
                if n >= 2:
                    pe.wait_ge(z["x_res_ready"], n - 1)
                for m in range(4):
                    mm = pe.transpose(tp[:, n % 2, m * P:(m + 1) * P], x_tok[:, 4 * n + m, :], ident[:, :])
                mm.then_inc(z["xt_ready"], 1)

        @block.vector
        def _(dve):
            dve.wait_ge(z["const_in"], 64)
            nc.vector.tensor_copy(ident_h[:, :], ident[:, :]).then_inc(z["consts_ready"], 1)
            nc.vector.tensor_copy(wmask[:, :, :], wmask_f[:, :, :]).then_inc(z["consts_ready"], 1)
            nc.vector.tensor_copy(causal[:, :], causal_f[:, :]).then_inc(z["consts_ready"], 1)
            for n in range(G):
                dve.wait_ge(z["xt_ready"], n + 1)
                nc.vector.tensor_copy(x_res[:, n * GT:(n + 1) * GT], tp[:, n % 2, :]).then_inc(z["x_res_ready"], 1)


def norm_mean(nc, z, pe, b, mean_w, q, n):
    if n >= 1:
        pe.wait_ge(z["ln_centred"], q)
    pe.matmul(b.M, mean_w[:, :], b.src(n), start=True, stop=True).then_inc(z["mean_ready"], 1)


def norm_var(nc, z, pe, b, mean_w, q, n):
    pe.wait_ge(z["ln_squared"], q + 1)
    if n >= 1:
        pe.wait_ge(z["ln_scaled"], q)
    for m in range(GT // P):
        mm = pe.matmul(b.V[:, m:m + 1], b.sq(n)[:, m * P:(m + 1) * P], mean_w[:, 0:1], start=True, stop=True)
    mm.then_inc(z["var_ready"], 1)


def norm_spread(nc, z, pe, b, ones_w, q, n):
    pe.wait_ge(z["ln_diag"], q + 1)
    pe.matmul(b.V, ones_w[:, :], b.dg[:, :, :], start=True, stop=True).then_inc(z["rstd_ready"], 1)


def norm_centre(nc, z, dve, b, q, n):
    dve.wait_ge(z["mean_ready"], q + 1)
    if n >= 2:
        dve.wait_ge(z["ln_squared"], q - 1)
        dve.wait_ge(z["ln_scaled"], q - 1)
    nc.vector.tensor_tensor(b.xc(n), b.src(n), b.M, ALU.subtract).then_inc(z["ln_centred"], 1)


def norm_square(nc, z, act, b, q, n):
    act.wait_ge(z["ln_centred"], q + 1)
    if n >= 2:
        act.wait_ge(z["var_ready"], q - 1)
    nc.scalar.activation(b.sq(n), b.xc(n), ACT.Square).then_inc(z["ln_squared"], 1)


def norm_eps(nc, z, dve, b, q, n):
    dve.wait_ge(z["var_ready"], q + 1)
    if n >= 1:
        dve.wait_ge(z["pow_ready"], q)
    nc.vector.tensor_scalar(b.ve, b.V[:, 0:GT // P], LN_EPS, None, ALU.add).then_inc(z["vare_ready"], 1)


def norm_rstd(nc, z, pool, b, neg_half, q, n):
    if n >= 1:
        pool.wait_ge(z["ln_diag"], q)
    pool.wait_ge(z["vare_ready"], q + 1)
    nc.gpsimd.tensor_tensor(b.rs, b.ve, neg_half[:, 0:GT // P], ALU.pow).then_inc(z["pow_ready"], 1)


def norm_diagonal(nc, z, dve, b, ident, q, n):
    dve.wait_ge(z["pow_ready"], q + 1)
    if n >= 1:
        dve.wait_ge(z["rstd_ready"], q)
    nc.vector.tensor_tensor(b.dg[:, :, :], ident[:, :].unsqueeze(1).to_broadcast([P, GT // P, P]),
                            b.rs.unsqueeze(2).to_broadcast([P, GT // P, P]), ALU.mult).then_inc(z["ln_diag"], 1)


def outer_norm(nc, z, tag, q0, x_res, x_a, ident, mean_w, ones_w, neg_half):
    with ExitStack() as st:
        b4 = {n: st.enter_context(nc.sbuf_tensor(f"{tag}_{n}", [P, 2, GT], F32)) for n in ("xc", "sq")}
        small = st.enter_context(nc.sbuf_tensor(f"{tag}_small", [P, 2, GT // P], F32))
        dg = st.enter_context(nc.sbuf_tensor(f"{tag}_dg", [P, GT // P, P], F32))
        ps = st.enter_context(nc.psum_tensor(f"{tag}_ps", [P, 2, GT], F32))
        b = NormBuffers(
            M=ps[:, 0, :], V=ps[:, 1, :], src=lambda n: x_res[:, n * GT:(n + 1) * GT],
            xc=lambda n: b4["xc"][:, n % 2, :], sq=lambda n: b4["sq"][:, n % 2, :],
            ve=small[:, 0, :], rs=small[:, 1, :], dg=dg)
        block = st.enter_context(nc.Block())

        @block.tensor
        def _(pe):
            pe.wait_ge(z["consts_ready"], 8)
            for n in range(G + 1):
                if n < G:
                    norm_mean(nc, z, pe, b, mean_w, q0 + n, n)
                if n >= 1:
                    norm_var(nc, z, pe, b, mean_w, q0 + n - 1, n - 1)
                    norm_spread(nc, z, pe, b, ones_w, q0 + n - 1, n - 1)

        @block.scalar
        def _(act):
            for n in range(G):
                norm_square(nc, z, act, b, q0 + n, n)

        @block.gpsimd
        def _(pool):
            for n in range(G):
                norm_rstd(nc, z, pool, b, neg_half, q0 + n, n)

        @block.vector
        def _(dve):
            for n in range(G + 1):
                if n < G:
                    norm_centre(nc, z, dve, b, q0 + n, n)
                if n >= 1:
                    m = n - 1
                    norm_eps(nc, z, dve, b, q0 + m, m)
                    norm_diagonal(nc, z, dve, b, ident, q0 + m, m)
                    dve.wait_ge(z["rstd_ready"], q0 + m + 1)
                    nc.vector.tensor_tensor(x_a[:, 1 + m * GT:1 + (m + 1) * GT], b.xc(m), b.V, ALU.mult).then_inc(z["ln_scaled"], 1)


def window_stack(nc, z, i, c, k, q0, x_a, x_b, ident, ident_h, wmask, carry_f, mean_w, ones_w, neg_half, zeros):
    with ExitStack() as st:
        def sb(name, shape, dt=F32):
            return st.enter_context(nc.sbuf_tensor(f"{name}_{k}", shape, dt))

        w_qkv = sb("w_qkv", [P, 3, HEADS * DH])
        w_o = sb("w_o", [P, HEADS * DH // P, P])
        w_1 = sb("w_1", [P, 2 * INNER])
        w_2 = sb("w_2", [P, len(CH), P])
        vec = sb("vec", [P, 9])
        qk_sc = sb("qk_sc", [P, 2, DH])
        qk_sw = sb("qk_sw", [P, 2, DH])
        wcos = sb("wcos", [P, TILES + 1, 2, DH])
        wsin = sb("wsin", [P, TILES + 1, 2, DH])
        tab_c = sb("tab_c", [P, 2, 2, DH])
        tab_s = sb("tab_s", [P, 2, 2, DH])
        xs = sb("xs", [P, 2, P])
        QK = 2 * HU * DH
        sq = sb("sq", [P, 2, QK])
        ss = sb("ss", [P, 2, 2 * HU])
        ssm = sb("ssm", [P, 2, 2 * HU])
        inv = sb("inv", [P, 2, 2 * HU])
        qn = sb("qn", [P, 2, QK])
        t1 = sb("t1", [P, 2, QK])
        t2 = sb("t2", [P, 2, QK])
        rot = sb("rot", [P, 4, QK])
        qkt = sb("qkt", [P, 8, 4, KEYS])
        mx = sb("mx", [P, 2, HU])
        nmx = sb("nmx", [P, 2, HU])
        sums = sb("sums", [P, 2, HU])
        prob = sb("prob", [P, 2, HU, KEYS])
        pt = sb("pt", [P, 2, HU, P])
        pts = sb("pts", [P, 2, HU, WIN])
        vt = sb("vt", [P, 8, HU, DH])
        v_car = sb("v_car", [P, UT, HU, DH])
        rec = sb("rec", [P, 2, HU])
        ots = sb("ots", [P, 8, 2, P])
        f2 = {n: sb("f" + n, [P, 2, GT]) for n in ("src", "xc", "sq", "xn", "gl")}
        fsmall = sb("fsmall", [P, 2, GT // P])
        fdg = sb("fdg", [P, GT // P, P])
        fsc = sb("fsc", [P, GT])
        hm = sb("hm", [P, 4, GT])
        ps = st.enter_context(nc.psum_tensor(f"ps_{k}", [P, 8, 512], F32))
        fb = NormBuffers(
            M=ps[:, 0, :], V=ps[:, 1, :], src=lambda n: f2["src"][:, n % 2, :],
            xc=lambda n: f2["xc"][:, n % 2, :], sq=lambda n: f2["sq"][:, n % 2, :],
            ve=fsmall[:, 0, :], rs=fsmall[:, 1, :], dg=fdg)
        L0 = k * DEPTH
        side = ps[:, 6, 256:256 + HU * WIN]
        heads_qk = lambda t: t.rearrange("p (q h d) -> p q h d", q=2, h=HU)
        scores = ps[:, 2:4, 0:2 * KEYS].rearrange("p b (r j) -> p b r j", r=2)

        def slots(eng, slot):
            for s in range(8):
                slot(s, 0, "first")
            with eng.Fori(1, TILES // 2) as pair:
                for s in range(8):
                    slot(s, pair, "steady")
            for s in range(8):
                slot(s, TILES // 2, "last")

        def clock(L, s, pair, part):
            def live(lag):
                return {"first": s >= lag, "steady": True, "last": s < lag}[part]

            def had(lag, back):
                return part != "first" or s - lag - back >= 0

            def done(lag, back=0):
                return (L + L0) * UNITS + pair * 8 + (s - lag - back + 1)
            return live, had, done

        def tile_no(L, s, pair):
            return (L + L0) * (TILES + 1) + pair * 2 + (s // UT + 1)

        def tiles_out(L, s, pair):
            return (L + L0) * TILES + pair * 2 + (s - LAG_Y - (UT - 1)) // UT + 1

        block = st.enter_context(nc.Block())

        @block.sync
        def _(sp):
            sp.dma_start(wcos[:, 0:TILES], c["wc"]).then_inc(z["const_in"], 16)
            sp.dma_start(wsin[:, 0:TILES], c["ws"]).then_inc(z["const_in"], 16)
            hf = DH // 2
            def attention_weights(L):
                sp.dma_start(w_qkv[:, :, :], i["L0_ffn_Wqkv"][bass.ds(L, 1)].rearrange("a p (t n) -> p (a t) n", t=3)).then_inc(z["wa_in"], 16)
                sp.dma_start(w_o[:, :, :], i["L0_ffn_Wo"][bass.ds(L, 1)].rearrange("a (c p) n -> p (a c) n", p=P)).then_inc(z["wa_in"], 16)

            def attention_scales(L):
                for q, name in enumerate(("L0_ffn_q_scale", "L0_ffn_k_scale")):
                    row = i[name][bass.ds(L, 1)]
                    sp.dma_start(qk_sc[:, q, :], row.to_broadcast([P, DH])).then_inc(z["wa_in"], 16)
                    sp.dma_start(qk_sw[:, q, 0:hf], row[:, hf:DH].to_broadcast([P, hf])).then_inc(z["wa_in"], 16)
                    sp.dma_start(qk_sw[:, q, hf:DH], row[:, 0:hf].to_broadcast([P, hf])).then_inc(z["wa_in"], 16)

            def feed_forward_weights(L):
                sp.dma_start(w_1[:, :], i["L0_ffn_W1"][bass.ds(L, 1)].rearrange("a p n -> p (a n)")).then_inc(z["wf_in"], 16)
                whole = 2 * P
                sp.dma_start(w_2[:, 0:2, :], i["L0_ffn_W2"][bass.ds(L, 1), 0:whole].rearrange("a (c p) n -> p (a c) n", p=P)).then_inc(z["wf_in"], 16)
                sp.dma_start(w_2[0:INNER - whole, 2, :], i["L0_ffn_W2"][bass.ds(L, 1), whole:INNER].rearrange("a p n -> p (a n)")).then_inc(z["wf_in"], 16)
                with nc.allow_non_contiguous_dma(reason="vectors onto partitions"):
                    for q, name in enumerate(("L0_ffn_ln_g", "L0_ffn_ln_b", "L0_ffn_b2")):
                        sp.dma_start(vec[:, q:q + 1], i[name][bass.ds(L, 1)].rearrange("a p -> p a")).then_inc(z["wf_in"], 16)
                    for q in range(2):
                        for m, (lo, w) in enumerate(CH):
                            b1 = i["L0_ffn_b1"][bass.ds(L, 1), q * INNER + lo:q * INNER + lo + w]
                            sp.dma_start(vec[0:w, 3 + 3 * q + m:4 + 3 * q + m], b1.rearrange("a p -> p a")).then_inc(z["wf_in"], 16)

            attention_weights(0)
            attention_scales(0)
            feed_forward_weights(0)
            with sp.Fori(1, DEPTH) as L:
                sp.wait_ge(z["y_ready"], (L + L0) * TILES)
                attention_weights(L)
                sp.wait_ge(z["tab_ready"], (L + L0) * (2 * TILES + 2))
                attention_scales(L)
                sp.wait_ge(z["x_a_ready"], (L + L0) * G + 1)
                feed_forward_weights(L)

        @block.gpsimd
        def _(pool):
            nc.gpsimd.memset(qkt[:, :, :, :], 0.0).then_inc(z["consts_ready"], 1)
            nc.gpsimd.memset(v_car[:, :, :, :], 0.0).then_inc(z["consts_ready"], 1)
            nc.gpsimd.memset(wcos[:, TILES], 0.0).then_inc(z["consts_ready"], 1)
            nc.gpsimd.memset(wsin[:, TILES], 0.0).then_inc(z["consts_ready"], 1)
            pool.wait_ge(z["consts_ready"], 8 + 4 * (k + 1))
            pool.wait_ge(z["const_in"], 64 + 32 * (k + 1))
            with pool.Fori(0, DEPTH) as L:
                def scaled_tables(tile, par):
                    flat = lambda t: t[:, bass.ds(tile, 1)].rearrange("p a q d -> p (a q) d")
                    nc.gpsimd.tensor_tensor(tab_c[:, par], flat(wcos), qk_sc[:, :, :], ALU.mult).then_inc(z["tab_ready"], 1)
                    nc.gpsimd.tensor_tensor(tab_s[:, par], flat(wsin), qk_sw[:, :, :], ALU.mult).then_inc(z["tab_ready"], 1)

                pool.wait_ge(z["wa_in"], (L + L0 + 1) * WA)
                scaled_tables(0, 0)

                def slot(s, pair, part):
                    live, had, done = clock(L, s, pair, part)
                    r2, par = s % 2, s // UT
                    if live(LAG_R):
                        n = (s - LAG_R) % 8
                        pool.wait_ge(z["normed"], done(LAG_R))
                        pool.wait_ge(z["tab_ready"], 2 * tile_no(L, s - LAG_R, pair))
                        if had(LAG_R, 2):
                            pool.wait_ge(z["rotated"], done(LAG_R, 2))
                            pool.wait_ge(z["k_rotated"], done(LAG_R, 2))
                        cb = tab_c[:, n // UT].unsqueeze(2).to_broadcast([P, 2, HU, DH])
                        nc.gpsimd.tensor_tensor(heads_qk(t1[:, n % 2]), heads_qk(qn[:, n % 2]), cb, ALU.mult).then_inc(z["t1_ready"], 1)
                        pool.wait_ge(z["t1_ready"], done(LAG_R))
                        pool.wait_ge(z["t2_ready"], 2 * done(LAG_R))
                        if had(LAG_R, 4):
                            pool.wait_ge(z["tr_ready"], done(LAG_R, 4))
                        nc.gpsimd.tensor_tensor(rot[:, n % 4, QK // 2:QK], t1[:, n % 2, QK // 2:QK], t2[:, n % 2, QK // 2:QK], ALU.add).then_inc(z["k_rotated"], 1)
                    if live(0):
                        if s % UT == 1:
                            if had(0, 2):
                                pool.wait_ge(z["t2_ready"], 2 * done(0, 2))
                                pool.wait_ge(z["t1_ready"], done(0, 2))
                            scaled_tables(pair * 2 + (par + 1), (par + 1) % 2)
                        pool.wait_ge(z["clamped"], done(0))
                        if had(0, 2):
                            pool.wait_ge(z["normed"], done(0, 2))
                        nc.gpsimd.tensor_tensor(inv[:, r2], ssm[:, r2], neg_half[:, 0:2 * HU], ALU.pow).then_inc(z["inv_ready"], 1)
                    if live(LAG_S):
                        m = (s - LAG_S) % 8
                        pool.wait_ge(z["s_ready"], done(LAG_S))
                        nc.gpsimd.tensor_tensor(qkt[:, (m + UT) % 8, 2:4, P:KEYS], qkt[:, m, 2:4, P - WIN:P],
                                                carry_f[:, 0:1].unsqueeze(2).to_broadcast([P, 2, WIN]), ALU.mult).then_inc(z["k_carried"], 1)
                slots(pool, slot)

                for n in range(G):
                    norm_rstd(nc, z, pool, fb, neg_half, q0 + L * G + n, n)

        @block.tensor
        def _(pe):
            pe.wait_ge(z["consts_ready"], 8 + 4 * (k + 1))
            with pe.Fori(0, DEPTH) as L:
                pe.wait_ge(z["wa_in"], (L + L0 + 1) * WA)
                pe.wait_ge(z["x_a_ready"], (L + L0) * G + 1)

                def slot(s, pair, part):
                    live, had, done = clock(L, s, pair, part)
                    if live(0):
                        u = s % UT
                        pe.wait_ge(z["xs_ready"], 2 * tile_no(L, s, pair))
                        if had(0, 2):
                            pe.wait_ge(z["squared"], done(0, 2))
                            pe.wait_ge(z["normed"], done(0, 2))
                        pe.matmul(ps[:, s % 2, :], xs[:, s // UT, :], w_qkv[:, 0:2, u * 256:(u + 1) * 256],
                                  start=True, stop=True).then_inc(z["qk_ready"], 1)
                    if live(LAG_T):
                        pe.wait_ge(z["rotated"], done(LAG_T))
                        pe.wait_ge(z["k_rotated"], done(LAG_T))
                        if had(LAG_T, 1):
                            pe.wait_ge(z["tr_read"], done(LAG_T, 1))
                        for m in range(4):
                            mm = pe.transpose(ps[:, 4, m * P:(m + 1) * P],
                                              rot[:, (s - LAG_T) % 4, m * P:(m + 1) * P], ident[:, :])
                        mm.then_inc(z["tr_ready"], 1)
                    if live(LAG_Y) and (s - LAG_Y) % UT == UT - 1:
                        pe.wait_ge(z["ot_read"], done(LAG_Y))
                        if live(LAG_S):
                            pe.wait_ge(z["exped"], done(LAG_S, 1))
                        else:
                            pe.wait_ge(z["exped"], (L + L0 + 1) * UNITS)
                        base = (s - LAG_Y - (UT - 1)) % 8
                        for m in range(2 * UT):
                            mm = pe.matmul(ps[:, 2, 384:512], w_o[:, m, :], ots[:, base + m // 2, m % 2, :],
                                           start=(m == 0), stop=(m == 2 * UT - 1))
                        mm.then_inc(z["y_ready"], 1)
                    if live(LAG_S):
                        n = (s - LAG_S) % 8
                        pe.wait_ge(z["tr_read"], done(LAG_S))
                        if had(LAG_S, 1):
                            pe.wait_ge(z["exped"], done(LAG_S, 1))
                        if had(LAG_S, UT):
                            pe.wait_ge(z["k_carried"], done(LAG_S, UT))
                        first = part == "first" and n < UT
                        for b in range(2):
                            m = wmask[:, 0 if first else 1].unsqueeze(1).to_broadcast([P, 2, KEYS])
                            pe.matmul(scores[:, b], ident_h[:, :], m, start=True, stop=False, skip_group_check=True)
                            h0 = 64 * b
                            for r in range(2):
                                mm = pe.matmul(scores[:, b, r, :], qkt[h0:h0 + 64, n, r, 0:P], qkt[h0:h0 + 64, n, 2 + r, :],
                                               start=False, stop=True, skip_group_check=True)
                        mm.then_inc(z["s_ready"], 1)
                    if live(LAG_P):
                        n = (s - LAG_P) % 8
                        pe.wait_ge(z["weighted"], done(LAG_P))
                        if part != "last" or s <= LAG_V:
                            pe.wait_ge(z["v_read"], done(LAG_V, 1))
                        if had(LAG_P, 1):
                            pe.wait_ge(z["pt_read"], done(LAG_P, 1))
                        for h in range(HU):
                            mm = pe.transpose(ps[:, 5, h * P:(h + 1) * P], prob[:, n % 2, h, 0:P], ident[:, :])
                        mm.then_inc(z["pt_ready"], 1)
                        for h in range(HU):
                            mm = pe.transpose(side[0:WIN, h * WIN:(h + 1) * WIN], prob[0:WIN, n % 2, h, P:KEYS], ident[0:WIN, 0:WIN])
                        if not live(LAG_V):
                            mm.then_inc(z["vs_ready"], 1)
                    if live(LAG_V):
                        n = (s - LAG_V) % 8
                        if had(LAG_V, 1) and not live(LAG_P):
                            pe.wait_ge(z["v_read"], done(LAG_V, 1))
                        mm = pe.matmul(ps[:, 6, 0:256], xs[:, n // UT, :], w_qkv[:, 2, (n % UT) * 256:(n % UT + 1) * 256],
                                       start=True, stop=True)
                        mm.then_inc(z["v_ready"], 1)
                    if live(LAG_O):
                        n = (s - LAG_O) % 8
                        pe.wait_ge(z["pt_read"], done(LAG_O))
                        pe.wait_ge(z["v_read"], done(LAG_O))
                        if had(LAG_O, UT - 1):
                            pe.wait_ge(z["v_carried"], done(LAG_O, UT - 1))
                        if had(LAG_O, 1):
                            pe.wait_ge(z["ot_read"], done(LAG_O, 1))
                        def head(h):
                            return ps[64 * (h % 2):64 * (h % 2) + 64, 7, h // 2 * P:(h // 2 + 1) * P]
                        for r in range(HU // 2):
                            for h in (2 * r, 2 * r + 1):
                                pe.matmul(head(h), vt[:, n, h, :], pt[:, n % 2, h, :], start=True, stop=False, skip_group_check=True)
                            for h in (2 * r, 2 * r + 1):
                                mm = pe.matmul(head(h)[:, 0:WIN], v_car[P - WIN:P, n % UT, h, :], pts[P - WIN:P, n % 2, h, :],
                                               start=False, stop=True, skip_group_check=True, tile_position=(P - WIN, 64 * (h % 2)))
                        mm.then_inc(z["o_ready"], 1)
                slots(pe, slot)

                g = L + L0
                pe.wait_ge(z["wf_in"], (g + 1) * WF)
                pe.wait_ge(z["x_b_ready"], (g + 1) * TILES)
                q1 = q0 + L * G

                def mean(n):
                    pe.wait_ge(z["sh_lo"], g * G + (n + 1))
                    pe.wait_ge(z["sh_hi"], g * G + (n + 1))
                    norm_mean(nc, z, pe, fb, mean_w, q1 + n, n)

                def up(n, m):
                    j = 3 * n + m
                    lo, w = CH[m]
                    pe.wait_ge(z["ln_ready"], g * G + (n + 1))
                    if j >= 2:
                        pe.wait_ge(z["prod_ready"], g * 3 * G + (j - 1))
                    pe.matmul(ps[0:w, 2 + j % 2, :], w_1[:, lo:lo + w], f2["xn"][:, n % 2, :], start=True, stop=True)
                    pe.matmul(ps[0:w, 4 + j % 2, :], w_1[:, INNER + lo:INNER + lo + w], f2["xn"][:, n % 2, :],
                              start=True, stop=True).then_inc(z["up_ready"], 1)

                def down(n, m):
                    j = 3 * n + m
                    w = CH[m][1]
                    pe.wait_ge(z["prod_ready"], g * 3 * G + (j + 1))
                    if m == 0 and n >= 2:
                        pe.wait_ge(z["x_a_ready"], g * G + n)
                    pe.matmul(ps[:, 6 + n % 2, :], w_2[0:w, m, :], hm[0:w, j % 4, :],
                              start=(m == 0), stop=(m == len(CH) - 1)).then_inc(z["down_ready"], 1)

                mean(0)
                norm_var(nc, z, pe, fb, mean_w, q1, 0)
                norm_spread(nc, z, pe, fb, ones_w, q1, 0)
                for n in range(G):
                    up(n, 0)
                    up(n, 1)
                    if n + 1 < G:
                        mean(n + 1)
                    down(n, 0)
                    up(n, 2)
                    if n + 1 < G:
                        norm_var(nc, z, pe, fb, mean_w, q1 + n + 1, n + 1)
                    down(n, 1)
                    if n + 1 < G:
                        norm_spread(nc, z, pe, fb, ones_w, q1 + n + 1, n + 1)
                    down(n, 2)

        @block.scalar
        def _(act):
            with act.Fori(0, DEPTH) as L:
                def slot(s, pair, part):
                    live, had, done = clock(L, s, pair, part)
                    if live(0):
                        act.wait_ge(z["qk_ready"], done(0))
                        if had(0, 2):
                            act.wait_ge(z["summed"], done(0, 2))
                        nc.scalar.activation(sq[:, s % 2], ps[:, s % 2, :], ACT.Square).then_inc(z["squared"], 1)
                    if live(LAG_V + 1):
                        n = (s - LAG_V - 1) % 8
                        act.wait_ge(z["v_ready"], done(LAG_V + 1))
                        if had(LAG_V + 1, 6):
                            act.wait_ge(z["v_carried"], done(LAG_V + 1, 6))
                        nc.scalar.copy(vt[:, n, :, 0:DH], ps[:, 6, 0:256].rearrange("p (h d) -> p h d", h=HU)).then_inc(z["v_read"], 1)
                    if live(LAG_O + 1):
                        n = (s - LAG_O - 1) % 8
                        act.wait_ge(z["o_ready"], done(LAG_O + 1))
                        nc.scalar.copy(ots[:, n].rearrange("p a t -> p (a t)"), ps[:, 7, 0:2 * P]).then_inc(z["ot_read"], 1)
                    if live(LAG_O + 1):
                        n = (s - LAG_O - 1) % 8
                        act.wait_ge(z["o_ready"], done(LAG_O + 1))
                        act.wait_ge(z["v_read"], done(LAG_O + 1))
                        nc.scalar.copy(v_car[P - WIN:P, n % UT], vt[P - WIN:P, n]).then_inc(z["v_carried"], 1)
                    if live(LAG_T):
                        n = (s - LAG_T) % 8
                        act.wait_ge(z["tr_ready"], done(LAG_T))
                        if had(LAG_T, 6):
                            act.wait_ge(z["s_ready"], done(LAG_T, 6))
                            act.wait_ge(z["k_carried"], done(LAG_T, 6))
                        nc.scalar.copy(qkt[:, n, :, 0:P], ps[:, 4, :].rearrange("p (a t) -> p a t", t=P)).then_inc(z["tr_read"], 1)
                    if live(LAG_P):
                        n = (s - LAG_P) % 8
                        act.wait_ge(z["pt_ready"], done(LAG_P))
                        if had(LAG_P, 2):
                            act.wait_ge(z["o_ready"], done(LAG_P, 2))
                        nc.scalar.copy(pt[:, n % 2].rearrange("p a t -> p (a t)"), ps[:, 5, :]).then_inc(z["pt_copied"], 1)
                        if live(LAG_V):
                            act.wait_ge(z["v_ready"], done(LAG_V))
                        else:
                            act.wait_ge(z["vs_ready"], (L + L0) * (LAG_P - LAG_V) + (s - LAG_V + 1))
                        nc.scalar.copy(pts[P - WIN:P, n % 2].rearrange("p a t -> p (a t)"), side[0:WIN]).then_inc(z["pt_read"], 1)
                    if live(LAG_S):
                        n = (s - LAG_S) % 8
                        act.wait_ge(z["negated"], done(LAG_S))
                        if had(LAG_S, 2):
                            act.wait_ge(z["pt_ready"], done(LAG_S, 2))
                            act.wait_ge(z["pt_read"], done(LAG_S, 2))
                        for h in range(HU):
                            e = nc.scalar.activation(prob[:, n % 2, h, :], scores[:, h % 2, h // 2, :], ACT.Exp, scale=float(DH) ** 0.5,
                                                     bias=nmx[:, n % 2, h:h + 1], accum_out=sums[:, n % 2, h:h + 1])
                        e.then_inc(z["exped"], 1)
                slots(act, slot)

                g = L + L0
                q1 = q0 + L * G

                def shift(n):
                    act.wait_ge(z["x_b_ready"], g * TILES + 4 * (n + 1))
                    if n >= 2:
                        act.wait_ge(z["ln_centred"], q1 + (n - 1))
                    nc.scalar.copy(f2["src"][0:64, n % 2, :], x_b[0:64, 1 + n * GT:1 + (n + 1) * GT]).then_inc(z["sh_lo"], 1)

                def gelu(n, m):
                    j = 3 * n + m
                    w = CH[m][1]
                    act.wait_ge(z["up_ready"], g * 3 * G + (j + 1))
                    if j >= 2:
                        act.wait_ge(z["prod_ready"], g * 3 * G + (j - 1))
                    nc.scalar.activation(f2["gl"][0:w, j % 2, :], ps[0:w, 4 + j % 2, :], ACT.Gelu,
                                         bias=vec[0:w, 6 + m:7 + m]).then_inc(z["gelu_ready"], 1)

                act.wait_ge(z["wf_in"], (g + 1) * WF)
                shift(0)
                shift(1)
                norm_square(nc, z, act, fb, q1, 0)
                for n in range(G):
                    gelu(n, 0)
                    if n + 1 < G:
                        norm_square(nc, z, act, fb, q1 + n + 1, n + 1)
                    gelu(n, 1)
                    gelu(n, 2)
                    if n + 2 < G:
                        shift(n + 2)

        @block.vector
        def _(dve):
            with dve.Fori(0, DEPTH) as L:
                def slot(s, pair, part):
                    live, had, done = clock(L, s, pair, part)
                    if live(LAG_R):
                        n = (s - LAG_R) % 8
                        dve.wait_ge(z["inv_ready"], done(LAG_R))
                        if had(LAG_R, 2):
                            dve.wait_ge(z["t1_ready"], done(LAG_R, 2))
                            dve.wait_ge(z["t2_ready"], 2 * done(LAG_R, 2))
                        ib = inv[:, n % 2].unsqueeze(2).to_broadcast([P, 2 * HU, DH])
                        nc.vector.tensor_tensor(qn[:, n % 2].rearrange("p (h d) -> p h d", d=DH),
                                                ps[:, n % 2].rearrange("p (h d) -> p h d", d=DH), ib, ALU.mult).then_inc(z["normed"], 1)
                        hf = DH // 2
                        dve.wait_ge(z["normed"], done(LAG_R))
                        dve.wait_ge(z["tab_ready"], 2 * tile_no(L, s - LAG_R, pair))
                        if had(LAG_R, 2):
                            dve.wait_ge(z["rotated"], done(LAG_R, 2))
                            dve.wait_ge(z["k_rotated"], done(LAG_R, 2))
                        a, b = heads_qk(t2[:, n % 2]), heads_qk(qn[:, n % 2])
                        for lo, hi in ((0, hf), (hf, 0)):
                            sn = tab_s[:, n // UT, :, lo:lo + hf].unsqueeze(2).to_broadcast([P, 2, HU, hf])
                            nc.vector.tensor_tensor(a[:, :, :, lo:lo + hf], b[:, :, :, hi:hi + hf], sn, ALU.mult).then_inc(z["t2_ready"], 1)
                    if live(LAG_P):
                        n = (s - LAG_P) % 8
                        dve.wait_ge(z["exped"], done(LAG_P))
                        if had(LAG_P, 2):
                            dve.wait_ge(z["weighted"], done(LAG_P, 2))
                        nc.vector.reciprocal(rec[:, n % 2], sums[:, n % 2]).then_inc(z["recip_ready"], 1)
                        dve.wait_ge(z["recip_ready"], done(LAG_P))
                        nc.vector.tensor_tensor(prob[:, n % 2], prob[:, n % 2], rec[:, n % 2].unsqueeze(2).to_broadcast([P, HU, KEYS]),
                                                ALU.mult).then_inc(z["weighted"], 1)
                    if live(0):
                        dve.wait_ge(z["squared"], done(0))
                        if had(0, 2):
                            dve.wait_ge(z["clamped"], done(0, 2))
                        nc.vector.tensor_reduce(ss[:, s % 2], sq[:, s % 2].rearrange("p (h d) -> p h d", d=DH), X, ALU.add).then_inc(z["summed"], 1)
                        dve.wait_ge(z["summed"], done(0))
                        if had(0, 2):
                            dve.wait_ge(z["inv_ready"], done(0, 2))
                        nc.vector.tensor_scalar(ssm[:, s % 2], ss[:, s % 2], 1e-24, None, ALU.max).then_inc(z["clamped"], 1)
                    if live(LAG_S):
                        n = (s - LAG_S) % 8
                        dve.wait_ge(z["s_ready"], done(LAG_S))
                        if had(LAG_S, 2):
                            dve.wait_ge(z["negated"], done(LAG_S, 2))
                        m = mx[:, n % 2].rearrange("p (r b) -> p b r", b=2)
                        nc.vector.tensor_reduce(m, scores, X, ALU.max).then_inc(z["maxed"], 1)
                    if live(LAG_Y) and (s - LAG_Y) % UT == UT - 1:
                        dve.wait_ge(z["y_ready"], tiles_out(L, s, pair))
                        tile = pair * 2 + (s - LAG_Y - (UT - 1)) // UT
                        cols = bass.ds(tile * P + 1, P)
                        nc.vector.tensor_tensor(x_b[:, cols], ps[:, 2, 384:512], x_a[:, cols], ALU.add).then_inc(z["x_b_ready"], 1)
                    if live(LAG_S):
                        dve.wait_ge(z["maxed"], done(LAG_S))
                        if had(LAG_S, 2):
                            dve.wait_ge(z["exped"], done(LAG_S, 2))
                        nc.vector.tensor_scalar(nmx[:, n % 2], mx[:, n % 2], -float(DH) ** 0.5, None, ALU.mult).then_inc(z["negated"], 1)
                    if live(LAG_R):
                        n = (s - LAG_R) % 8
                        dve.wait_ge(z["t1_ready"], done(LAG_R))
                        dve.wait_ge(z["t2_ready"], 2 * done(LAG_R))
                        if had(LAG_R, 4):
                            dve.wait_ge(z["tr_ready"], done(LAG_R, 4))
                        nc.vector.tensor_tensor(rot[:, n % 4, 0:QK // 2], t1[:, n % 2, 0:QK // 2], t2[:, n % 2, 0:QK // 2], ALU.add).then_inc(z["rotated"], 1)
                    if live(0) and s % UT == 1:
                        if had(0, 2):
                            dve.wait_ge(z["v_ready"], done(0, 2))
                        shifted(pair * 2 + (s // UT + 1), (s // UT + 1) % 2)
                def shifted(tile, par):
                    nc.vector.tensor_copy(xs[0:64, par, :], x_a[0:64, bass.ds(tile * P + 1, P)]).then_inc(z["xs_ready"], 1)
                    nc.vector.tensor_copy(xs[64:P, par, :], x_a[64:P, bass.ds(tile * P, P)]).then_inc(z["xs_ready"], 1)
                dve.wait_ge(z["x_a_ready"], (L + L0) * G + 1)
                dve.wait_ge(z["ln_scaled"], q0 + L * G)
                shifted(0, 0)
                slots(dve, slot)

                g = L + L0
                q1 = q0 + L * G

                def affine(n):
                    dve.wait_ge(z["rstd_ready"], q1 + (n + 1))
                    if n >= 1:
                        dve.wait_ge(z["ln_ready"], g * G + n)
                    nc.vector.scalar_tensor_tensor(fsc[:, :], fb.xc(n), vec[:, 0:1], fb.V, ALU.mult, ALU.mult).then_inc(z["ln_scaled"], 1)
                    dve.wait_ge(z["ln_scaled"], q1 + (n + 1))
                    if n >= 2:
                        dve.wait_ge(z["up_ready"], g * 3 * G + 3 * (n - 1))
                    nc.vector.tensor_scalar(f2["xn"][:, n % 2, :], fsc[:, :], vec[:, 1:2], None, ALU.add).then_inc(z["ln_ready"], 1)

                def prod(n, m):
                    j = 3 * n + m
                    w = CH[m][1]
                    dve.wait_ge(z["gelu_ready"], g * 3 * G + (j + 1))
                    if j >= 4:
                        dve.wait_ge(z["down_ready"], g * 3 * G + (j - 3))
                    nc.vector.scalar_tensor_tensor(hm[0:w, j % 4, :], ps[0:w, 2 + j % 2, :], vec[0:w, 3 + m:4 + m],
                                                   f2["gl"][0:w, j % 2, :], ALU.add, ALU.mult).then_inc(z["prod_ready"], 1)

                def shift(n):
                    dve.wait_ge(z["x_b_ready"], g * TILES + 4 * (n + 1))
                    if n >= 2:
                        dve.wait_ge(z["ln_centred"], q1 + (n - 1))
                    nc.vector.tensor_copy(f2["src"][64:P, n % 2, :], x_b[64:P, n * GT:(n + 1) * GT]).then_inc(z["sh_hi"], 1)

                dve.wait_ge(z["wf_in"], (g + 1) * WF)
                shift(0)
                shift(1)
                norm_centre(nc, z, dve, fb, q1, 0)
                norm_eps(nc, z, dve, fb, q1, 0)
                norm_diagonal(nc, z, dve, fb, ident, q1, 0)
                affine(0)
                for n in range(G):
                    prod(n, 0)
                    if n + 1 < G:
                        norm_centre(nc, z, dve, fb, q1 + n + 1, n + 1)
                    prod(n, 1)
                    if n + 1 < G:
                        norm_eps(nc, z, dve, fb, q1 + n + 1, n + 1)
                    prod(n, 2)
                    if n + 1 < G:
                        norm_diagonal(nc, z, dve, fb, ident, q1 + n + 1, n + 1)
                        affine(n + 1)
                    if n + 2 < G:
                        shift(n + 2)
                    dve.wait_ge(z["down_ready"], g * 3 * G + 3 * (n + 1))
                    cols = slice(1 + n * GT, 1 + (n + 1) * GT)
                    nc.vector.scalar_tensor_tensor(x_a[:, cols], ps[:, 6 + n % 2, :], vec[:, 2:3], x_b[:, cols],
                                                   ALU.add, ALU.add).then_inc(z["x_a_ready"], 1)


def copy_on_pool(nc, dst, src, zeros):
    return nc.gpsimd.tensor_tensor(dst, src, zeros, ALU.add)


def mix(nc, z, k, x_res, x_a):
    with nc.Block() as block:
        @block.vector
        def _(dve):
            nc.vector.scalar_tensor_tensor(x_res[:, :], x_a[:, 1:1 + T], 0.5, x_res[:, :], ALU.mult, ALU.add).then_inc(z["mixed"], 1)


def store_output(nc, z, out_dram, x_res, ident):
    with ExitStack() as st:
        o_tok = st.enter_context(nc.sbuf_tensor("o_tok", [P, TILES, P], F32))
        tp = st.enter_context(nc.psum_tensor("turned_out", [P, 2, GT], F32))
        block = st.enter_context(nc.Block())

        @block.tensor
        def _(pe):
            for n in range(G):
                if n >= 2:
                    pe.wait_ge(z["out_ready"], n - 1)
                for m in range(4):
                    t = 4 * n + m
                    mm = pe.transpose(tp[:, n % 2, m * P:(m + 1) * P], x_res[:, t * P:(t + 1) * P], ident[:, :])
                mm.then_inc(z["out_t_ready"], 1)

        @block.vector
        def _(dve):
            for n in range(G):
                dve.wait_ge(z["out_t_ready"], n + 1)
                nc.vector.tensor_copy(o_tok[:, 4 * n:4 * n + 4, :].rearrange("p a d -> p (a d)"), tp[:, n % 2, :]).then_inc(z["out_ready"], 1)

        @block.sync
        def _(sp):
            for n in range(G):
                sp.wait_ge(z["out_ready"], n + 1)
                sp.dma_start(out_dram[:, 4 * n:4 * n + 4, :], o_tok[:, 4 * n:4 * n + 4, :]).then_inc(z["stored"], 16)
            sp.wait_ge(z["stored"], 16 * G)


def latent_attention(nc, z, i, c, x_res, x_a, x_b, ident, ident_h, causal, ones_w, neg_half, zeros):
    VW = CD + 1
    with ExitStack() as st:
        def sb(name, shape, dt=F32):
            return st.enter_context(nc.sbuf_tensor(name, shape, dt))

        wl_kv = sb("wl_kv", [P, KR])
        wl_q = sb("wl_q", [P, QR])
        g_kv = sb("g_kv", [KR, 1])
        wl_v = sb("wl_v", [KR, P])
        wl_o = sb("wl_o", [P, P])
        wa = {"q": sb("wa_q", [QR, HEADS + 2, QD]), "qr": sb("wa_qr", [QR, HEADS + 2, QD]), "k": sb("wa_k", [P, HEADS + 2, QD]),
              "kr": sb("wa_kr", [P, HEADS + 2, QD]), "kc": sb("wa_kc", [KR, HEADS + 2, QD])}
        ws = {n: sb("ws_" + n, [t.shape[0], 2, 64]) for n, t in wa.items()}
        mean_kv = sb("mean_kv", [KR, KR])
        kvc = sb("kvc", [KR, T])
        qc = sb("qc", [QR, T])
        lms = sb("lms", [P, GT // P])
        lrs = sb("lrs", [P, GT // P])
        ac = sb("ac", [P, T])
        as_ = sb("as_", [P, T])
        qm = sb("qm", [P, 2, 2, T])
        kT = sb("kT", [P, 2, T])
        ra = sb("ra", [P, 2, GT])
        rb = sb("rb", [P, 2, GT])
        vall = sb("vall", [P, TILES, HEADS + 2, VW])
        vp = sb("vp", [P, 2, 2, TILES, 32])
        sel = sb("sel", [P, VW])
        RX = 8
        prow = sb("prow", [P, RX, GT])
        ptl = sb("ptl", [P, 4, GT])
        rpm = sb("rpm", [P, RX, 4])
        rmx = sb("rmx", [P, RX])
        rng = sb("rng", [P, RX])
        osb = sb("osb", [P, 2, P])
        lrec = sb("lrec", [P, 2, TILES])
        lsq = prow[0:KR, 0, :]
        lrb = prow[0:KR, 1, :]
        ldg = prow[:, 2, :].rearrange("p (m w) -> p m w", w=P)
        oall = x_b[:, 1:1 + T].rearrange("p (t d) -> p t d", d=P)
        lot = ptl[:, 0:2, :]
        ps = st.enter_context(nc.psum_tensor("ps_l", [P, 8, 512], F32))
        scale = 1.0 / float(np.sqrt(np.float32(QD)))

        WL = 16 * (7 + 8)
        WS = len(wa) + 2
        WZ = 2 * len(wa) + 4
        AHEAD = 4

        block = st.enter_context(nc.Block())
        rows = [(h, r) for h in range(2) for r in range(TILES)]
        items = [(w, n) for w in ("q", "k") for n in range(G)]
        quads = [(x, m) for x, (h, r) in enumerate(rows) for m in range(r // 4 + 1)]
        NQ = len(quads)
        quad_no = {q: y for y, q in enumerate(quads)}

        def row_ended(y):
            return quads[y][0] if 0 <= y < NQ and quads[y][1] == rows[quads[y][0]][1] // 4 else None

        def width(y):
            x, m = quads[y]
            return min(GT, (rows[x][1] + 1) * P - m * GT)

        def last_quad(x):
            return quad_no[x, rows[x][1] // 4]

        def rope_at(y):
            j, k = divmod(y, NQ // len(items))
            return (j, "a") if k == 2 else (j, "b") if k == 6 else None

        @block.sync
        def _(sp):
            sp.dma_start(wl_kv[:, :], i["L0_attn_W_kv"]).then_inc(z["wl_in"], 16)
            sp.dma_start(wl_q[:, :], i["L0_attn_W_q"]).then_inc(z["wl_in"], 16)
            with nc.allow_non_contiguous_dma(reason="a vector onto partitions"):
                sp.dma_start(g_kv[:, :], i["L0_attn_g_kv"].rearrange("(p a) -> p a", a=1)).then_inc(z["wl_in"], 16)
            sp.dma_start(wl_v[:, :], i["L0_attn_W_vdec"]).then_inc(z["wl_in"], 16)
            sp.dma_start(wl_o[:, :], i["L0_attn_W_o"]).then_inc(z["wl_in"], 16)
            sp.dma_start(ac[:, :], c["ac"]).then_inc(z["wl_in"], 16)
            sp.dma_start(as_[:, :], c["as_"]).then_inc(z["wl_in"], 16)
            sp.wait_ge(z["wl_zero"], len(wa))
            hf = RD // 2
            for n, name in (("q", "L0_attn_W_qrope"), ("k", "L0_attn_W_krope")):
                src = i[name].rearrange("p (h d) -> p h d", h=HEADS)
                sp.dma_start(wa[n][:, 0:HEADS, 0:RD], src).then_inc(z["wl_in"], 16)
                sp.dma_start(wa[n + "r"][:, 0:HEADS, 0:hf], src[:, :, hf:RD]).then_inc(z["wl_in"], 16)
                sp.dma_start(wa[n + "r"][:, 0:HEADS, hf:RD], src[:, :, 0:hf]).then_inc(z["wl_in"], 16)
            for n, name in (("q", "L0_attn_W_qdec"), ("kc", "L0_attn_W_kdec")):
                src = i[name].rearrange("p (h d) -> p h d", h=HEADS)
                sp.dma_start(wa[n][:, 0:HEADS, RD:QD], src).then_inc(z["wl_in"], 16)


        @block.gpsimd
        def _(pool):
            fills = [(t[:, :, :], 0.0) for t in wa.values()] + [(mean_kv[:, :], 1.0 / KR)] + [(t[:, :, :], 0.0) for t in ws.values()]
            fills += [(vall[:, :, :, :], 1.0)]
            for n, (t, value) in enumerate(fills):
                nc.gpsimd.memset(t, value).then_inc(z["wl_zero"], 1)
                pool.wait_ge(z["wl_zero"], n + 1)
            for n in range(G):
                pool.wait_ge(z["lat_mse"], n + 1)
                if n >= 1:
                    pool.wait_ge(z["lat_diag"], n)
                nc.gpsimd.tensor_tensor(lrs[:, :], lms[:, :], neg_half[:, 0:GT // P], ALU.pow).then_inc(z["lat_pow"], 1)
            nc.gpsimd.memset(qm[:, :, :, :], 0.0).then_inc(z["wl_zero"], 1)
            nc.gpsimd.memset(vp[:, :, :, :, :], 0.0).then_inc(z["wl_zero"], 1)
            pool.wait_ge(z["wl_zero"], WZ)
            pool.wait_ge(z["wl_in"], WL)
            pool.wait_ge(z["lat_pow"], G)
            pool.wait_ge(z["v_copied"], G)

            def pair_slots(pair, b):
                for m, n in enumerate(wa):
                    copy_on_pool(nc, ws[n][:, :, 0:QD], wa[n][:, bass.ds(pair * 2, 2), :],
                                 zeros[0:wa[n].shape[0], 0:2 * QD].rearrange("p (h d) -> p h d", h=2)).then_inc(z["wl_slots"], 1)
                    pool.wait_ge(z["wl_slots"], pair * WS + (m + 1))
                for h in range(2):
                    nc.gpsimd.tensor_tensor(vp[:, b, h, :, 0:VW], vall[:, :, bass.ds(pair * 2 + h, 1), :].rearrange("p t a d -> p t (a d)"),
                                            zeros[:, 0:VW].unsqueeze(1).to_broadcast([P, TILES, VW]), ALU.add).then_inc(z["wl_slots"], 1)

            def keys(pair, b):
                for n in range(G):
                    pool.wait_ge(z["ra_ready"], pair * len(items) + (G + n + 1))
                    pool.wait_ge(z["rb_ready"], pair * len(items) + (G + n + 1))
                    nc.gpsimd.tensor_tensor(kT[:, b, n * GT:(n + 1) * GT], ra[:, n % 2, :], rb[:, n % 2, :], ALU.add).then_inc(z["rope_ready"], 1)

            pair_slots(0, 0)
            keys(0, 0)
            with pool.Fori(0, PAIRS // 2) as two:
                for b in range(2):
                    pool.wait_ge(z["ol_normed"], two * 2 + (b + 1))
                    pair_slots(two * 2 + (b + 1), 1 - b)
                    keys(two * 2 + (b + 1), 1 - b)

        @block.tensor
        def _(pe):
            pe.wait_ge(z["wl_in"], WL)
            pe.wait_ge(z["wl_zero"], WZ - 2)
            for n in range(G):
                cols = slice(1 + n * GT, 1 + (n + 1) * GT)
                if n >= 1:
                    pe.wait_ge(z["lat_kv"], n)
                    pe.wait_ge(z["lat_q"], n)
                pe.matmul(ps[0:KR, 0, :], wl_kv[:, :], x_a[:, cols], start=True, stop=True)
                pe.matmul(ps[0:QR, 1, :], wl_q[:, :], x_a[:, cols], start=True, stop=True).then_inc(z["lat_ready"], 1)
                pe.wait_ge(z["lat_sq"], n + 1)
                if n >= 1:
                    pe.wait_ge(z["lat_mse"], n)
                    pe.wait_ge(z["lat_kv"], n)
                for m in range(GT // P):
                    mm = pe.matmul(ps[:, 2, m:m + 1], lsq[:, m * P:(m + 1) * P], mean_kv[:, 0:1], start=True, stop=True)
                mm.then_inc(z["lat_ms"], 1)
                pe.wait_ge(z["lat_diag"], n + 1)
                pe.matmul(ps[0:KR, 2, :], ones_w[:, 0:KR], ldg, start=True, stop=True).then_inc(z["lat_rs"], 1)
            for n in range(G):
                pe.wait_ge(z["lat_kv"], n + 1)
                if n >= 2:
                    pe.wait_ge(z["v_copied"], n - 1)
                for m in range(4):
                    t = 4 * n + m
                    mm = pe.matmul(ps[:, 4 + n % 2, m * P:(m + 1) * P], kvc[:, t * P:(t + 1) * P], wl_v[:, :], start=True, stop=True)
                mm.then_inc(z["v_mm"], 1)
            pe.wait_ge(z["v_copied"], G)
            pe.wait_ge(z["sel_ready"], 1)

            def rope(pair, j, half):
                w, n = items[j]
                first = isinstance(pair, int)
                cols = slice(1 + n * GT, 1 + (n + 1) * GT)
                flat = lambda t: t[:, :, :].rearrange("p h d -> p (h d)")
                if half == "a":
                    if j == 0:
                        pe.wait_ge(z["wl_slots"], (pair + 1) * WS)
                    if j >= 1 or not first:
                        pe.wait_ge(z["rb_ready"], pair * len(items) + j)
                    if w == "q":
                        mm = pe.matmul(ps[:, 7, :], flat(ws["q"]), qc[:, n * GT:(n + 1) * GT], start=True, stop=True)
                    else:
                        pe.matmul(ps[:, 7, :], flat(ws["k"]), x_a[:, cols], start=True, stop=False)
                        mm = pe.matmul(ps[:, 7, :], flat(ws["kc"]), kvc[:, n * GT:(n + 1) * GT], start=False, stop=True)
                    mm.then_inc(z["a_ready"], 1)
                else:
                    pe.wait_ge(z["ra_ready"], pair * len(items) + (j + 1))
                    if w == "q":
                        mm = pe.matmul(ps[:, 7, :], flat(ws["qr"]), qc[:, n * GT:(n + 1) * GT], start=True, stop=True)
                    else:
                        mm = pe.matmul(ps[:, 7, :], flat(ws["kr"]), x_a[:, cols], start=True, stop=True)
                    mm.then_inc(z["b_ready"], 1)

            def scores(pair, b, y):
                x, m = quads[y]
                h, r = rows[x]
                if y == 0:
                    pe.wait_ge(z["q_roped"], (pair + 1) * 2 * G)
                    pe.wait_ge(z["rope_ready"], (pair + 1) * G)
                if y >= AHEAD:
                    pe.wait_ge(z["row_exp"], pair * NQ + (y - AHEAD + 1))
                w = width(y)
                end = m == r // 4
                mm = pe.matmul(ps[:, y % 4, 0:w], qm[:, b, h, r * P:(r + 1) * P], kT[:, b, m * GT:m * GT + w],
                               start=True, stop=not end, skip_group_check=True)
                if end:
                    mm = pe.matmul(ps[:, y % 4, w - P:w], ident_h[:, :], causal[:, :], start=False, stop=True, skip_group_check=True)
                mm.then_inc(z["sc_ready"], 1)

            def turn(pair, y):
                pe.wait_ge(z["row_exp"], pair * NQ + (y + 1))
                if y >= 2:
                    pe.wait_ge(z["ptl_odd" if y % 2 else "ptl_even"], pair * (NQ // 2) + y // 2)
                for t in range(width(y) // P):
                    mm = pe.transpose(ps[:, 4 + y % 2, t * P:(t + 1) * P], prow[:, y % RX, t * P:(t + 1) * P], ident[:, :])
                mm.then_inc(z["ptl_ready"], 1)

            def strips_sum(pair, x):
                w = 32 * min(4, rows[x][1] + 1)
                pe.wait_ge(z["ol_copied"], pair * len(rows) + (x + 1))
                pe.matmul(ps[:, 6, P + x * VW:P + (x + 1) * VW], osb[0:w, x % 2, :], sel[0:w, :], start=True, stop=True,
                          skip_group_check=True).then_inc(z["ol_summed"], 1)

            def out(pair, b, y):
                x, m = quads[y]
                h, r = rows[x]
                pe.wait_ge(z["ptl_odd" if y % 2 else "ptl_even"], pair * (NQ // 2) + (y // 2 + 1))
                if y == 0:
                    pe.wait_ge(z["ol_normed"], pair + 1)
                elif m == 0:
                    strips_sum(pair, x - 1)
                for t in range(4 * m, min(4 * m + 4, r + 1)):
                    j = t % 4
                    mm = pe.matmul(ps[32 * j:32 * (j + 1), 6, 0:P], vp[:, b, h, t, :], ptl[:, y % 4, j * P:(j + 1) * P],
                                   start=(t < 4), stop=(t + 4 > r), skip_group_check=True)
                mm.then_inc(z["pv_part"], 1)

            for j in range(len(items)):
                rope(0, j, "a")
                rope(0, j, "b")
            with pe.Fori(0, PAIRS // 2) as two:
                for b in range(2):
                    pair = two * 2 + b
                    for y in range(AHEAD):
                        scores(pair, b, y)
                    for y in range(NQ + 2):
                        if y + AHEAD < NQ:
                            scores(pair, b, y + AHEAD)
                        if y < NQ:
                            turn(pair, y)
                        if y >= 2:
                            out(pair, b, y - 2)
                        if y < NQ and rope_at(y) is not None:
                            rope(two * 2 + (b + 1), *rope_at(y))
                    strips_sum(pair, len(rows) - 1)

            for n in range(G):
                pe.wait_ge(z["ol_normed"], PAIRS + 1)
                if n >= 2:
                    pe.wait_ge(z["lo_copied"], n - 1)
                for m in range(4):
                    mm = pe.transpose(ps[:, n % 2, m * P:(m + 1) * P], oall[:, 4 * n + m, :], ident[:, :])
                mm.then_inc(z["lo_tr"], 1)
                pe.wait_ge(z["lo_copied"], n + 1)
                if n >= 2:
                    pe.wait_ge(z["lo_added"], n - 1)
                pe.matmul(ps[:, 2 + n % 2, :], wl_o[:, :], lot[:, n % 2, :], start=True, stop=True).then_inc(z["lo_mm"], 1)

        @block.scalar
        def _(act):
            for n in range(G):
                act.wait_ge(z["lat_ready"], n + 1)
                if n >= 1:
                    act.wait_ge(z["lat_ms"], n)
                nc.scalar.activation(lsq, ps[0:KR, 0, :], ACT.Square).then_inc(z["lat_sq"], 1)
                nc.scalar.copy(qc[:, n * GT:(n + 1) * GT], ps[0:QR, 1, :]).then_inc(z["lat_q"], 1)

            def exps(pair, y):
                x, m = quads[y]
                act.wait_ge(z["row_neg"], pair * len(rows) + (x + 1))
                if y >= RX:
                    act.wait_ge(z["ptl_ready"], pair * NQ + (y - RX + 1))
                nc.scalar.activation(prow[:, y % RX, 0:width(y)], ps[:, y % 4, 0:width(y)],
                                     ACT.Exp, bias=rng[:, x % RX:x % RX + 1], scale=scale).then_inc(z["row_exp"], 1)

            def turned(pair, y):
                act.wait_ge(z["ptl_ready"], pair * NQ + (y + 1))
                if y >= 4:
                    act.wait_ge(z["pv_part"], pair * NQ + (y - 3))
                nc.scalar.copy(ptl[:, y % 4, 0:width(y)], ps[:, 4 + y % 2, 0:width(y)]).then_inc(z["ptl_even"], 1)

            with act.Fori(0, PAIRS // 2) as two:
                for b in range(2):
                    pair = two * 2 + b
                    exps(pair, 0)
                    for y in range(NQ):
                        early = y + 1 < NQ and last_quad(quads[y + 1][0]) < y + AHEAD
                        if early:
                            exps(pair, y + 1)
                        if y % 2 == 0:
                            turned(pair, y)
                        if y + 1 < NQ and not early:
                            exps(pair, y + 1)

        @block.vector
        def _(dve):
            for n in range(G):
                cols = slice(n * GT, (n + 1) * GT)
                dve.wait_ge(z["lat_ms"], n + 1)
                if n >= 1:
                    dve.wait_ge(z["lat_pow"], n)
                nc.vector.tensor_scalar(lms[:, :], ps[:, 2, 0:GT // P], RMS_EPS, None, ALU.add).then_inc(z["lat_mse"], 1)
                dve.wait_ge(z["lat_pow"], n + 1)
                if n >= 1:
                    dve.wait_ge(z["lat_rs"], n)
                nc.vector.tensor_tensor(ldg, ident[:, :].unsqueeze(1).to_broadcast([P, GT // P, P]),
                                        lrs[:, :].unsqueeze(2).to_broadcast([P, GT // P, P]), ALU.mult).then_inc(z["lat_diag"], 1)
                dve.wait_ge(z["lat_rs"], n + 1)
                dve.wait_ge(z["lat_q"], n + 1)
                nc.vector.tensor_copy(lrb, ps[0:KR, 2, :]).then_inc(z["lat_spread"], 1)
                dve.wait_ge(z["lat_spread"], n + 1)
                nc.vector.scalar_tensor_tensor(kvc[:, cols], ps[0:KR, 0, :], g_kv[:, 0:1], lrb, ALU.mult, ALU.mult).then_inc(z["lat_kv"], 1)
            for n in range(G):
                dve.wait_ge(z["v_mm"], n + 1)
                nc.vector.tensor_copy(vall[:, 4 * n:4 * n + 4, 0:HEADS, 0:CD],
                                      ps[:, 4 + n % 2, :].rearrange("p (t h d) -> p t h d", t=4, h=HEADS)).then_inc(z["v_copied"], 1)
            nc.vector.tensor_reduce(sel[:, :], ident[:, :].rearrange("p (j c) -> p c j", j=4)[:, 0:VW, :], X, ALU.add).then_inc(z["sel_ready"], 1)
            nc.vector.memset(lrec[:, :, :], 0.0).then_inc(z["ol_normed"], 1)
            dve.wait_ge(z["wl_zero"], WZ)

            def rope(pair, b, j, half):
                w, n = items[j]
                cols = slice(n * GT, (n + 1) * GT)
                if half == "a":
                    if j >= G + 2:
                        dve.wait_ge(z["rope_ready"], pair * G + (j - G - 1))
                    elif j >= 2:
                        dve.wait_ge(z["q_roped"], pair * 2 * G + 2 * (j - 1))
                    elif not isinstance(pair, int):
                        dve.wait_ge(z["rope_ready"], pair * G + (j - 1))
                    dve.wait_ge(z["a_ready"], pair * len(items) + (j + 1))
                    nc.vector.tensor_tensor(ra[:, j % 2, :], ps[:, 7, :], ac[:, cols], ALU.mult).then_inc(z["ra_ready"], 1)
                else:
                    dve.wait_ge(z["b_ready"], pair * len(items) + (j + 1))
                    nc.vector.tensor_tensor(rb[:, j % 2, :], ps[:, 7, :], as_[:, cols], ALU.mult).then_inc(z["rb_ready"], 1)
                    if w == "q":
                        dve.wait_ge(z["ra_ready"], pair * len(items) + (j + 1))
                        dve.wait_ge(z["rb_ready"], pair * len(items) + (j + 1))
                        for h in range(2):
                            hp = slice(64 * h, 64 * h + 64)
                            nc.vector.tensor_tensor(qm[hp, b, h, cols], ra[hp, j % 2, :], rb[hp, j % 2, :], ALU.add).then_inc(z["q_roped"], 1)

            def maxima(pair, y):
                x, m = quads[y]
                dve.wait_ge(z["sc_ready"], pair * NQ + (y + 1))
                if m == 0 and x >= RX:
                    dve.wait_ge(z["row_top"], pair * len(rows) + (x - RX + 1))
                nc.vector.tensor_reduce(rpm[:, x % RX, m:m + 1], ps[:, y % 4, 0:width(y)], X, ALU.max).then_inc(z["row_max"], 1)
                if row_ended(y) is None:
                    return
                dve.wait_ge(z["row_max"], pair * NQ + (y + 1))
                if x >= RX:
                    dve.wait_ge(z["row_neg"], pair * len(rows) + (x - RX + 1))
                nc.vector.tensor_reduce(rmx[:, x % RX:x % RX + 1], rpm[:, x % RX, 0:m + 1], X, ALU.max).then_inc(z["row_top"], 1)
                dve.wait_ge(z["row_top"], pair * len(rows) + (x + 1))
                if x >= RX:
                    dve.wait_ge(z["row_exp"], pair * NQ + (last_quad(x - RX) + 1))
                nc.vector.tensor_scalar(rng[:, x % RX:x % RX + 1], rmx[:, x % RX:x % RX + 1], -scale, None, ALU.mult).then_inc(z["row_neg"], 1)

            def turned(pair, y):
                dve.wait_ge(z["ptl_ready"], pair * NQ + (y + 1))
                if y >= 4:
                    dve.wait_ge(z["pv_part"], pair * NQ + (y - 3))
                nc.vector.tensor_copy(ptl[:, y % 4, 0:width(y)], ps[:, 4 + y % 2, 0:width(y)]).then_inc(z["ptl_odd"], 1)

            def outputs(pair, x):
                w = 32 * min(4, rows[x][1] + 1)
                dve.wait_ge(z["pv_part"], pair * NQ + (last_quad(x) + 1))
                if x >= 2:
                    dve.wait_ge(z["ol_summed"], pair * len(rows) + (x - 1))
                nc.vector.tensor_copy(osb[0:w, x % 2, :], ps[0:w, 6, 0:P]).then_inc(z["ol_copied"], 1)

            def norm(pair):
                both = ps[:, 6, P:P + len(rows) * VW].rearrange("p (h t d) -> p h t d", h=2, d=VW)
                dve.wait_ge(z["ol_summed"], (pair + 1) * len(rows))
                dve.wait_ge(z["ol_normed"], pair + 1)
                nc.vector.reciprocal(lrec[:, :, :], both[:, :, :, CD:VW].rearrange("p h t a -> p h (t a)")).then_inc(z["ol_rec"], 1)
                dve.wait_ge(z["ol_rec"], pair + 1)
                nc.vector.tensor_tensor(oall[:, :, bass.ds(pair * 2 * CD, 2 * CD)].rearrange("p t (h d) -> p h t d", h=2), both[:, :, :, 0:CD],
                                        lrec[:, :, :].unsqueeze(3).to_broadcast([P, 2, TILES, CD]), ALU.mult).then_inc(z["ol_normed"], 1)

            for j in range(len(items)):
                rope(0, 0, j, "a")
                rope(0, 0, j, "b")
            with dve.Fori(0, PAIRS // 2) as two:
                for b in range(2):
                    pair = two * 2 + b
                    for y in range(AHEAD):
                        maxima(pair, y)
                    for y in range(NQ + 2):
                        if y + AHEAD < NQ:
                            maxima(pair, y + AHEAD)
                        if y < NQ and y % 2:
                            turned(pair, y)
                        if row_ended(y - 2) is not None:
                            outputs(pair, row_ended(y - 2))
                        if y < NQ and rope_at(y) is not None:
                            rope(two * 2 + (b + 1), 1 - b, *rope_at(y))
                    norm(pair)

            for n in range(G):
                cols = slice(n * GT, (n + 1) * GT)
                dve.wait_ge(z["lo_tr"], n + 1)
                nc.vector.tensor_copy(lot[:, n % 2, :], ps[:, n % 2, :]).then_inc(z["lo_copied"], 1)
                dve.wait_ge(z["lo_mm"], n + 1)
                nc.vector.tensor_tensor(x_res[:, cols], ps[:, 2 + n % 2, :], x_res[:, cols], ALU.add).then_inc(z["lo_added"], 1)


_INS = ["L0_attn_x", "L0_attn_W_kv", "L0_attn_g_kv", "L0_attn_W_kdec", "L0_attn_W_vdec", "L0_attn_W_q", "L0_attn_W_qdec",
        "L0_attn_W_krope", "L0_attn_W_qrope", "L0_attn_W_o", "L0_ffn_Wqkv", "L0_ffn_q_scale", "L0_ffn_k_scale", "L0_ffn_Wo",
        "L0_ffn_ln_g", "L0_ffn_ln_b", "L0_ffn_W1", "L0_ffn_b1", "L0_ffn_W2", "L0_ffn_b2"]


def kernel(**inputs):
    import concourse.bacc as _bacc
    from concourse.bass_utils import run_bass_kernel_spmd as _run

    nc = _bacc.Bacc("TRN2", target_bir_lowering=False, num_devices=1)
    arrays, ins, consts = {}, {}, {}
    for name in _INS:
        a = np.ascontiguousarray(inputs[name])
        arrays[f"in_{name}"] = a
        ins[name] = nc.dram_tensor(f"in_{name}", a.shape, mybir.dt.from_np(a.dtype), kind="ExternalInput").ap()
    for name, a in tables().items():
        arrays[f"const_{name}"] = a
        consts[name] = nc.dram_tensor(f"const_{name}", a.shape, F32, kind="ExternalInput").ap()
    out = nc.dram_tensor("out_0", (1, T, P), F32, kind="ExternalOutput").ap()
    macaron_kernel(nc, ins, consts, out)
    r = _run(nc, [arrays], core_ids=[0])
    return r.results[0]["out_0"]
```
